# Optimizing a Trainium2 kernel written in Bass

```python
import numpy as np
import jax
import jax.numpy as jnp

def _softmax(x, axis=-1):
    return jax.nn.softmax(x, axis=axis)

def _gelu(x):
    return jax.nn.gelu(x, approximate=True)

def _silu(x):
    return jax.nn.silu(x)

def _sigmoid(x):
    return jax.nn.sigmoid(x)

def _layernorm(x, axis=-1, eps=1e-05):
    m = jnp.mean(x, axis=axis, keepdims=True)
    v = jnp.var(x, axis=axis, keepdims=True)
    return (x - m) / jnp.sqrt(v + eps)

def _scatter_add(tgt, idx, src, axis=0):
    return tgt.at[idx].add(src)

def _segment_sum(src, seg, n):
    return jax.ops.segment_sum(src, seg, n)
kernel_name = 'mk_early_fusion_d2_tok_img768_r4_b79d78'

def setup_inputs(seed: int=0):
    np.random.seed(seed)
    _w = jnp.asarray

    def _rec_inputs():
        import jax
        import jax.numpy as jnp
        _rk = jax.random.key(seed)
        x = 7.57192e-06 + 1.00007 * jax.random.normal(jax.random.fold_in(_rk, 1), (32, 3, 96, 96), jnp.float32)
        txt = 0.000375391 + 0.999744 * jax.random.normal(jax.random.fold_in(_rk, 2), (32, 77, 192), jnp.float32)
        return (x, txt)
    x, txt = _rec_inputs()

    def _L0_tok_setup():
        import jax, jax.numpy as jnp
        import numpy as np
        PATCH = 16
        HALF = PATCH // 2
        DIM = 192
        CH = 3
        PATCH_DIM = PATCH * PATCH * 5 * CH
        LN_EPS = 1e-05

        def _shift2d(x, t, l):
            H, W = (x.shape[-2], x.shape[-1])
            at, al = (abs(t), abs(l))
            xp = jnp.pad(x, ((0, 0), (0, 0), (at, at), (al, al)))
            return xp[:, :, at - t:at - t + H, al - l:al - l + W]
        key = jax.random.key(seed)
        k1, k2 = jax.random.split(key, 2)
        x = jax.random.normal(k1, (64, CH, 224, 224), dtype=jnp.float32)
        ln_gamma = jnp.ones((PATCH_DIM,), dtype=jnp.float32)
        ln_beta = jnp.zeros((PATCH_DIM,), dtype=jnp.float32)
        W = jax.random.normal(k2, (DIM, PATCH_DIM), dtype=jnp.float32) * np.float32(1.0 / np.sqrt(PATCH_DIM))
        b = jnp.zeros((DIM,), dtype=jnp.float32)
        return {'x': x, 'ln_gamma': ln_gamma, 'ln_beta': ln_beta, 'W': W, 'b': b}
    _L0_tok_all = _L0_tok_setup()
    _L0_tok_in = {k: v for k, v in _L0_tok_all.items() if k in ('ln_gamma', 'ln_beta', 'W', 'b')}
    del _L0_tok_all

    def _L0_attn_setup():
        import jax, jax.numpy as jnp
        import numpy as np
        B, N, C, H = (8, 1024, 192, 8)
        key = jax.random.key(seed)
        k1, k2, k3 = jax.random.split(key, 3)
        x = jax.random.normal(k1, (B, N, C), dtype=jnp.float32)
        W_qkv = jax.random.normal(k2, (C, 3 * C), dtype=jnp.float32) * 0.02
        W_proj = jax.random.normal(k3, (C, C), dtype=jnp.float32) * 0.02
        b_proj = jnp.zeros((C,), dtype=jnp.float32)
        temp = jnp.ones((H, 1, 1), dtype=jnp.float32)
        return {'x': x, 'W_qkv': W_qkv, 'W_proj': W_proj, 'b_proj': b_proj, 'temp': temp}
    _L0_attn_all = _L0_attn_setup()
    _L0_attn_in = {k: v for k, v in _L0_attn_all.items() if k in ('W_qkv', 'W_proj', 'b_proj', 'temp')}
    del _L0_attn_all

    def _L0_ffn_setup():
        import jax, jax.numpy as jnp
        import numpy as np
        B, S, D = (2, 256, 192)
        NF, NR, R, DS, K = (128, 128, 128, 64, 4)

        @jax.checkpoint
        def feature_fn(x, neurons, weights):
            all_h = jnp.einsum('bsd,ndr->bsnr', x, neurons)
            return jnp.einsum('bsnr,bsn->bsr', all_h, weights)

        @jax.checkpoint
        def restore_fn(h, neurons, weights):
            all_out = jnp.einsum('bsr,nrd->bsnd', h, neurons)
            return jnp.einsum('bsnd,bsn->bsd', all_out, weights)

        def topk_sparsify(weights, k):
            topk_vals, topk_idx = jax.lax.top_k(weights, k)
            N = weights.shape[-1]
            one_hot_mask = jax.nn.one_hot(topk_idx, N, dtype=weights.dtype)
            sparse = (one_hot_mask * topk_vals[..., jnp.newaxis]).sum(axis=-2)
            sparse = sparse / (sparse.sum(axis=-1, keepdims=True) + 1e-08)
            return (sparse, topk_idx)
        key = jax.random.key(seed)
        ks = jax.random.split(key, 8)
        x = jax.random.normal(ks[0], (B, S, D), jnp.float32)
        f_know = jax.random.normal(ks[1], (NF, D, R), jnp.float32) * 0.02
        r_know = jax.random.normal(ks[2], (NR, R, D), jnp.float32) * 0.02
        W_fk = jax.random.normal(ks[3], (D, DS), jnp.float32) * 0.02
        b_fk = jnp.zeros((DS,), jnp.float32)
        W_rk = jax.random.normal(ks[4], (D, DS), jnp.float32) * 0.02
        b_rk = jnp.zeros((DS,), jnp.float32)
        emb_fk = jax.random.normal(ks[5], (NF, DS), jnp.float32) * 0.02
        emb_rk = jax.random.normal(ks[6], (NR, DS), jnp.float32) * 0.02
        return {'x': x, 'f_know': f_know, 'r_know': r_know, 'W_fk': W_fk, 'b_fk': b_fk, 'W_rk': W_rk, 'b_rk': b_rk, 'emb_fk': emb_fk, 'emb_rk': emb_rk}
    _L0_ffn_all = _L0_ffn_setup()
    _L0_ffn_in = {k: v for k, v in _L0_ffn_all.items() if k in ('f_know', 'r_know', 'W_fk', 'b_fk', 'W_rk', 'b_rk', 'emb_fk', 'emb_rk')}
    del _L0_ffn_all

    def _L1_attn_setup():
        import jax, jax.numpy as jnp
        import numpy as np
        D_IN = 192
        D_OUT = 192
        NUM_HEADS = 12
        HEAD_DIM = D_OUT // NUM_HEADS
        key = jax.random.key(seed)
        ks = jax.random.split(key, 6)
        s = 0.02
        x = jax.random.normal(ks[0], (2, 1024, D_IN), dtype=jnp.float32)
        w_query = jax.random.normal(ks[1], (D_IN, D_OUT), dtype=jnp.float32) * s
        w_key = jax.random.normal(ks[2], (D_IN, D_OUT), dtype=jnp.float32) * s
        w_value = jax.random.normal(ks[3], (D_IN, D_OUT), dtype=jnp.float32) * s
        w_out = jax.random.normal(ks[4], (D_OUT, D_OUT), dtype=jnp.float32) * s
        b_out = jnp.zeros((D_OUT,), dtype=jnp.float32)
        return {'x': x, 'w_query': w_query, 'w_key': w_key, 'w_value': w_value, 'w_out': w_out, 'b_out': b_out}
    _L1_attn_all = _L1_attn_setup()
    _L1_attn_in = {k: v for k, v in _L1_attn_all.items() if k in ('w_query', 'w_key', 'w_value', 'w_out', 'b_out')}
    del _L1_attn_all

    def _L1_ffn_setup():
        import jax, jax.numpy as jnp
        import numpy as np
        B, SEQ, D = (2, 256, 192)
        E, H = (8, 768)
        CAPACITY = 2
        key = jax.random.key(seed)
        ks = jax.random.split(key, 6)
        x = jax.random.normal(ks[0], (B, SEQ, D), dtype=jnp.float32)
        gate_weight = jax.random.normal(ks[1], (E, D), dtype=jnp.float32) * 0.006
        w1 = jax.random.normal(ks[2], (E, D, H), dtype=jnp.float32) * (1.0 / np.sqrt(D))
        b1 = jnp.zeros((E, H), dtype=jnp.float32)
        w2 = jax.random.normal(ks[3], (E, H, D), dtype=jnp.float32) * (1.0 / np.sqrt(H))
        b2 = jnp.zeros((E, D), dtype=jnp.float32)
        return {'x': x, 'gate_weight': gate_weight, 'w1': w1, 'b1': b1, 'w2': w2, 'b2': b2}
    _L1_ffn_all = _L1_ffn_setup()
    _L1_ffn_in = {k: v for k, v in _L1_ffn_all.items() if k in ('gate_weight', 'w1', 'b1', 'w2', 'b2')}
    del _L1_ffn_all
    return {'x': x, 'txt': txt, 'L0_tok_ln_gamma': _L0_tok_in['ln_gamma'], 'L0_tok_ln_beta': _L0_tok_in['ln_beta'], 'L0_tok_W': _L0_tok_in['W'], 'L0_tok_b': _L0_tok_in['b'], 'L0_attn_W_qkv': _L0_attn_in['W_qkv'], 'L0_attn_W_proj': _L0_attn_in['W_proj'], 'L0_attn_b_proj': _L0_attn_in['b_proj'], 'L0_attn_temp': _L0_attn_in['temp'], 'L0_ffn_f_know': _L0_ffn_in['f_know'], 'L0_ffn_r_know': _L0_ffn_in['r_know'], 'L0_ffn_W_fk': _L0_ffn_in['W_fk'], 'L0_ffn_b_fk': _L0_ffn_in['b_fk'], 'L0_ffn_W_rk': _L0_ffn_in['W_rk'], 'L0_ffn_b_rk': _L0_ffn_in['b_rk'], 'L0_ffn_emb_fk': _L0_ffn_in['emb_fk'], 'L0_ffn_emb_rk': _L0_ffn_in['emb_rk'], 'L1_attn_w_query': _L1_attn_in['w_query'], 'L1_attn_w_key': _L1_attn_in['w_key'], 'L1_attn_w_value': _L1_attn_in['w_value'], 'L1_attn_w_out': _L1_attn_in['w_out'], 'L1_attn_b_out': _L1_attn_in['b_out'], 'L1_ffn_gate_weight': _L1_ffn_in['gate_weight'], 'L1_ffn_w1': _L1_ffn_in['w1'], 'L1_ffn_b1': _L1_ffn_in['b1'], 'L1_ffn_w2': _L1_ffn_in['w2'], 'L1_ffn_b2': _L1_ffn_in['b2']}

def reference(x, txt, L0_tok_ln_gamma, L0_tok_ln_beta, L0_tok_W, L0_tok_b, L0_attn_W_qkv, L0_attn_W_proj, L0_attn_b_proj, L0_attn_temp, L0_ffn_f_know, L0_ffn_r_know, L0_ffn_W_fk, L0_ffn_b_fk, L0_ffn_W_rk, L0_ffn_b_rk, L0_ffn_emb_fk, L0_ffn_emb_rk, L1_attn_w_query, L1_attn_w_key, L1_attn_w_value, L1_attn_w_out, L1_attn_b_out, L1_ffn_gate_weight, L1_ffn_w1, L1_ffn_b1, L1_ffn_w2, L1_ffn_b2):
    import jax
    import jax.numpy as jnp

    def _L0_tok_ref(x, ln_gamma, ln_beta, W, b):
        import jax, jax.numpy as jnp
        import numpy as np
        PATCH = 16
        HALF = PATCH // 2
        DIM = 192
        CH = 3
        PATCH_DIM = PATCH * PATCH * 5 * CH
        LN_EPS = 1e-05

        def _shift2d(x, t, l):
            H, W = (x.shape[-2], x.shape[-1])
            at, al = (abs(t), abs(l))
            xp = jnp.pad(x, ((0, 0), (0, 0), (at, at), (al, al)))
            return xp[:, :, at - t:at - t + H, al - l:al - l + W]
        p = PATCH
        shifts = ((1, -1, 1, -1), (-1, 1, -1, 1), (-1, 1, 1, -1), (1, -1, -1, 1))
        parts = [x] + [_shift2d(x, HALF * s[2], HALF * s[0]) for s in shifts]
        xc = jnp.concatenate(parts, axis=1)
        B, C5, H, Wd = xc.shape
        h, w = (H // p, Wd // p)
        patches = xc.reshape(B, C5, h, p, w, p)
        patches = patches.transpose(0, 2, 4, 3, 5, 1).reshape(B, h * w, p * p * C5)
        mu = patches.mean(axis=-1, keepdims=True)
        var = patches.var(axis=-1, keepdims=True)
        xn = (patches - mu) * jax.lax.rsqrt(var + LN_EPS) * ln_gamma + ln_beta
        return jnp.einsum('bnp,dp->bnd', xn, W) + b

    def _L0_attn_ref(x, W_qkv, W_proj, b_proj, temp):
        import jax, jax.numpy as jnp
        import numpy as np
        B, N, C, H = (8, 1024, 192, 8)
        b, n, c = x.shape
        h = temp.shape[0]
        d = c // h
        qkv = (x @ W_qkv).reshape(b, n, h, d, 3)
        q, k, v = (qkv[..., 0], qkv[..., 1], qkv[..., 2])
        q = q / jnp.linalg.norm(q, axis=1, keepdims=True)
        k = k / jnp.linalg.norm(k, axis=1, keepdims=True)
        attn = jnp.einsum('bnhd,bnhe->bhde', q, k) * temp
        attn = jax.nn.softmax(attn, axis=-1)
        y = jnp.einsum('bhde,bnhe->bnhd', attn, v).reshape(b, n, c)
        return y @ W_proj + b_proj

    def _L0_ffn_ref(x, f_know, r_know, W_fk, b_fk, W_rk, b_rk, emb_fk, emb_rk):
        import jax, jax.numpy as jnp
        import numpy as np
        B, S, D = (2, 256, 192)
        NF, NR, R, DS, K = (128, 128, 128, 64, 4)

        @jax.checkpoint
        def feature_fn(x, neurons, weights):
            all_h = jnp.einsum('bsd,ndr->bsnr', x, neurons)
            return jnp.einsum('bsnr,bsn->bsr', all_h, weights)

        @jax.checkpoint
        def restore_fn(h, neurons, weights):
            all_out = jnp.einsum('bsr,nrd->bsnd', h, neurons)
            return jnp.einsum('bsnd,bsn->bsd', all_out, weights)

        def topk_sparsify(weights, k):
            topk_vals, topk_idx = jax.lax.top_k(weights, k)
            N = weights.shape[-1]
            one_hot_mask = jax.nn.one_hot(topk_idx, N, dtype=weights.dtype)
            sparse = (one_hot_mask * topk_vals[..., jnp.newaxis]).sum(axis=-2)
            sparse = sparse / (sparse.sum(axis=-1, keepdims=True) + 1e-08)
            return (sparse, topk_idx)
        emb_fk_n = emb_fk / (jnp.linalg.norm(emb_fk, axis=-1, keepdims=True) + 1e-08)
        emb_rk_n = emb_rk / (jnp.linalg.norm(emb_rk, axis=-1, keepdims=True) + 1e-08)
        logits_fk = jnp.einsum('bsd,nd->bsn', x @ W_fk + b_fk, emb_fk_n)
        logits_rk = jnp.einsum('bsd,nd->bsn', x @ W_rk + b_rk, emb_rk_n)
        w_fk, _ = topk_sparsify(jax.nn.softmax(logits_fk, axis=-1), K)
        w_rk, _ = topk_sparsify(jax.nn.softmax(logits_rk, axis=-1), K)
        h = feature_fn(x, f_know, w_fk)
        out = restore_fn(h, r_know, w_rk)
        return out

    def _L1_attn_ref(x, w_query, w_key, w_value, w_out, b_out):
        import jax, jax.numpy as jnp
        import numpy as np
        D_IN = 192
        D_OUT = 192
        NUM_HEADS = 12
        HEAD_DIM = D_OUT // NUM_HEADS
        b, n, _ = x.shape
        q = (x @ w_query).reshape(b, n, NUM_HEADS, HEAD_DIM)
        k = (x @ w_key).reshape(b, n, NUM_HEADS, HEAD_DIM)
        v = (x @ w_value).reshape(b, n, NUM_HEADS, HEAD_DIM)
        scores = jnp.einsum('bqhd,bkhd->bhqk', q, k)
        causal = jnp.triu(jnp.ones((n, n), dtype=bool), k=1)
        scores = jnp.where(causal, -jnp.inf, scores)
        scale = 1.0 / jnp.sqrt(jnp.asarray(HEAD_DIM, dtype=scores.dtype))
        weights = jax.nn.softmax(scores * scale, axis=-1)
        ctx = jnp.einsum('bhqk,bkhd->bqhd', weights, v).reshape(b, n, D_OUT)
        return ctx @ w_out + b_out

    def _L1_ffn_ref(x, gate_weight, w1, b1, w2, b2):
        import jax, jax.numpy as jnp
        import numpy as np
        B, SEQ, D = (2, 256, 192)
        E, H = (8, 768)
        CAPACITY = 2
        Bb, s, d = x.shape
        xf = x.reshape(-1, d)
        S = xf.shape[0]
        k = S * CAPACITY
        logits = xf @ gate_weight.T
        scores = jax.nn.softmax(logits, axis=-1).T
        vals, idx = jax.lax.top_k(scores.reshape(-1), k)
        gate = jnp.zeros((E * S,), dtype=x.dtype).at[idx].add(vals).reshape(E, S)
        h = jax.nn.gelu(jnp.einsum('sd,edh->esh', xf, w1) + b1[:, None, :], approximate=True)
        out = jnp.einsum('esh,ehd->esd', h, w2) + b2[:, None, :]
        y = jnp.einsum('es,esd->sd', gate, out)
        return y.reshape(Bb, s, d)
    h = _L0_tok_ref(x, L0_tok_ln_gamma, L0_tok_ln_beta, L0_tok_W, L0_tok_b)
    h = jnp.concatenate([h, txt], axis=1)
    h = h + _L0_attn_ref(_layernorm(h, axis=-1), L0_attn_W_qkv, L0_attn_W_proj, L0_attn_b_proj, L0_attn_temp)
    h = h + _L0_ffn_ref(_layernorm(h, axis=-1), L0_ffn_f_know, L0_ffn_r_know, L0_ffn_W_fk, L0_ffn_b_fk, L0_ffn_W_rk, L0_ffn_b_rk, L0_ffn_emb_fk, L0_ffn_emb_rk)
    h = h + _L1_attn_ref(_layernorm(h, axis=-1), L1_attn_w_query, L1_attn_w_key, L1_attn_w_value, L1_attn_w_out, L1_attn_b_out)
    h = h + _L1_ffn_ref(_layernorm(h, axis=-1), L1_ffn_gate_weight, L1_ffn_w1, L1_ffn_b1, L1_ffn_w2, L1_ffn_b2)
    return h

_drawn_inputs = setup_inputs


def setup_inputs(seed=0):
    import zlib

    import numpy as np

    out = dict(_drawn_inputs(seed))
    spreads = {'L0_tok_ln_gamma': (1.0, 0.2),
     'L0_tok_ln_beta': (0.0, 0.1),
     'L0_tok_b': (0.0, 0.1),
     'L0_attn_b_proj': (0.0, 0.1),
     'L0_attn_temp': (1.0, 0.6),
     'L0_ffn_b_fk': (0.0, 0.448),
     'L0_ffn_b_rk': (0.0, 0.441),
     'L1_attn_b_out': (0.0, 0.1),
     'L1_ffn_b1': (0.0, 0.625),
     'L1_ffn_b2': (0.0, 0.425)}
    factors = {'L0_attn_W_qkv': 2.705,
     'L0_attn_W_proj': 2.808,
     'L0_ffn_f_know': 2.825,
     'L0_ffn_r_know': 2.825,
     'L0_ffn_W_fk': 2.877,
     'L0_ffn_W_rk': 2.823,
     'L0_ffn_emb_fk': 2.874,
     'L0_ffn_emb_rk': 2.874,
     'L1_attn_w_query': 8.0,
     'L1_attn_w_key': 8.0}
    for name, (base, spread) in spreads.items():
        noise = np.random.default_rng([zlib.crc32(name.encode()), seed]).standard_normal(out[name].shape)
        drawn = base * np.exp(spread * noise) if base else spread * noise
        out[name] = jnp.asarray(drawn.astype(out[name].dtype))
    for name, factor in factors.items():
        out[name] = (out[name] * factor).astype(out[name].dtype)
    return out
```

```python
from contextlib import ExitStack, contextmanager
import numpy as np
import concourse.bass as bass
from concourse import mybir

F32 = mybir.dt.float32
BF16 = mybir.dt.bfloat16
I32 = mybir.dt.int32
U32 = mybir.dt.uint32
ALU = mybir.AluOpType
ACT = mybir.ActivationFunctionType
AX = mybir.AxisListType

P = 128
NB = 32
TI, TT = 36, 77
T = TI + TT
D = 192
DH = D // 2
LN_EPS = 1e-5
NEG = -1e30

BLK = 7
NCH = 6
NK = 4 * NCH
PATCH_DIM = 3840
GRP = 3
GM = GRP * TI
NGRP = 11

NE, TOPK = 128, 4
R = 128
NBLK0 = (NB * T * TOPK + NE * (P - 1)) // P

NX, HID = 8, 768
HC = HID // P
K1 = 2 * NB * T
NBLK1 = (K1 + NX * (P - 1)) // P
FAR = 1 << 20

C_ID, C_ONE, C_TRS, C_TRI, C_IOTA, C_CAUS, C_BLKM, C_MULT, C_EPS, C_VALID, C_FAR, C_SENT, C_NHALF, C_VM1, C_DUMMY, C_ROW1, C_END = np.cumsum(
    [0, P, P, P, P, 256, 3 * P, DH, NK, 1, 1, 1, 4, 1, 1, 1, 1]).tolist()


@contextmanager
def semaphores(nc):
    taken = []

    def take(name):
        taken.append(nc.alloc_semaphore(name))
        return taken[-1]

    yield take
    nc.clear_and_free_semaphores(taken)
    nc.all_engine_barrier()


class Link:

    def __init__(self, eng, sem):
        self.eng, self.sem, self.base, self.n = eng, sem, 0, 0

    def done(self, ins):
        self.n += 1
        ins.then_inc(self.sem, 1)
        self.eng.wait_ge(self.sem, self.base + self.n)

    def loop(self, it, per):
        self.start, self.per, self.n, self.base = self.base + self.n, per, 0, self.base + self.n + it * per

    def end(self, turns):
        assert self.n == self.per, (self.n, self.per)
        self.base, self.n = self.start + turns * self.per, 0


def program(nc, x_blocks, txt, w_shift, w_base, g_shift, g_base, b_shift, b_base, tok_b,
            wqk, wv, wp, bp, temp, emb, wcat, bcat, f_know, r_know, wq1, wk1, wv1, wo1, bo1, gate_w, w1, b2, w2, bits, consts, out):
    with ExitStack() as top:
        resid = top.enter_context(nc.sbuf_tensor("resid", [P, NB * D], F32))
        cst = top.enter_context(nc.sbuf_tensor("cst", [P, C_END], F32))
        mean = top.enter_context(nc.sbuf_tensor("mean", [P, NB], F32))
        rstd = top.enter_context(nc.sbuf_tensor("rstd", [P, NB], F32))
        tok_rows = nc.dram_tensor("tok_rows", (NGRP * GRP * TI, D), F32, kind="Internal").ap()
        cstb = top.enter_context(nc.sbuf_tensor("cstb", [P, 4, P], BF16))
        slot_mem = nc.dram_tensor("slot_mem", (NBLK0 * P * D,), F32, kind="Internal").ap()
        embed_patches(nc, x_blocks, txt, w_shift, w_base, g_shift, g_base, b_shift, b_base, tok_b, consts,
                      cst, cstb, resid, tok_rows, slot_mem)
        layer_norm_stats(nc, "ln0", resid, cst, mean, rstd)
        channel_attention(nc, wqk, wv, wp, bp, temp, cst, resid, mean, rstd)
        layer_norm_stats(nc, "ln1", resid, cst, mean, rstd)
        sparse_ffn(nc, emb, wcat, bcat, f_know, r_know, cst, cstb, resid, mean, rstd, slot_mem)
        layer_norm_stats(nc, "ln2", resid, cst, mean, rstd)
        causal_attention(nc, wq1, wk1, wv1, wo1, bo1, cst, cstb, resid, mean, rstd)
        layer_norm_stats(nc, "ln3", resid, cst, mean, rstd)
        expert_ffn(nc, gate_w, w1, b2, w2, bits, cst, cstb, resid, mean, rstd, out)


def sparse_ffn(nc, emb, wcat, bcat, f_know, r_know, cst, cstb, resid, mean, rstd, slot_mem):
    with ExitStack() as ctx:
        def sb(name, shape, dt=F32):
            return ctx.enter_context(nc.sbuf_tensor("sf_" + name, shape, dt))

        embt = sb("embt", [P, 2 * NE])
        chosen = sb("chosen", [P, 2 * NB, NE], BF16)
        weight, index = sb("weight", [P, 2 * NB, 4]), sb("index", [P, 2 * NB, 4])
        slot = sb("slot", [P, NB, 8], I32)
        seg_start = sb("seg_start", [P, 2, P], BF16)
        block_expert = sb("block_expert", [1, 2, 256], I32)
        n = NBLK0 * P
        wide_rows = slot_mem.rearrange("(s d) -> s d", d=D)
        narrow_rows = slot_mem[0:n * R].rearrange("(s d) -> s d", d=R)
        feature_rows = nc.dram_tensor("feature_rows", (n, R), F32, kind="Internal").ap()
        restore_rows = nc.dram_tensor("restore_rows", (n, D), F32, kind="Internal").ap()
        route_tokens(nc, emb, wcat, bcat, cst, resid, mean, rstd, embt, chosen, weight, index)
        block_tables(nc, cst, cstb, chosen, seg_start, block_expert)
        place_tokens(nc, cst, cstb, resid, mean, rstd, chosen, index, seg_start, slot, wide_rows)
        blocks_product(nc, "feature", cst, block_expert, 0, wide_rows, f_know, feature_rows, D, R)
        combine_rows(nc, "mid", cst, slot, weight, 0, feature_rows, R, resid, narrow_rows)
        blocks_product(nc, "restore", cst, block_expert, 1, narrow_rows, r_know, restore_rows, R, D)
        combine_rows(nc, "end", cst, slot, weight, 1, restore_rows, D, resid, None)


def embed_patches(nc, x_blocks, txt, w_shift, w_base, g_shift, g_base, b_shift, b_base, tok_b, consts,
                  cst, cstb, resid, tok_rows, slot_mem):
    with ExitStack() as ctx:
        take = ctx.enter_context(semaphores(nc))
        def sb(name, shape, dt=F32):
            return ctx.enter_context(nc.sbuf_tensor(name, shape, dt))

        def sem(name):
            return take(name)

        ws = sb("ws", [P, NK, D])
        wb = sb("wb", [P, NK, D])
        weff = sb("weff", [P, NK, D + 1])
        gain = sb("gain", [P, 4, NK])
        bias = sb("bias", [1, D])
        xg = sb("xg", [P, 2, NCH * GRP, BLK * BLK])
        xw = sb("xw", [P, 2, NK, GRP * TI])
        xsq = sb("xsq", [P, 2, NK, GRP * TI])
        colsum = sb("colsum", [P, D])
        shift = sb("shift", [P, D])
        ZN = 2 * D * 8
        zrow = sb("zrow", [P, ZN])
        st = sb("st", [P, 2, 8])
        tok = sb("tok", [P, 2, D])
        rows = sb("rows", [P, 2, D])
        y_ps = ctx.enter_context(nc.psum_tensor("y_ps", [P, 2, 512], F32))
        q_ps = ctx.enter_context(nc.psum_tensor("q_ps", [P, 2, 512], F32))
        c_ps = ctx.enter_context(nc.psum_tensor("c_ps", [P, 2, 512], F32))
        w_in, cst_in, txt_in, zeroed = sem("w_in"), sem("cst_in"), sem("txt_in"), sem("zeroed")
        x_in = [sem("x_in0"), sem("x_in1")]
        weff_ready, sums_ready, sums_out, products_done = (
            sem("weff_ready"), sem("sums_ready"), sem("sums_out"), sem("products_done"))
        windows_ready, squared, var_ready, rstd_ready = sem("windows_ready"), sem("squared"), sem("var_ready"), sem("rstd_ready")
        tok_ready, tok_in, chain = sem("tok_ready"), sem("tok_in"), sem("chain")
        slots_clear = sem("slots_clear")
        rows_stored = [sem("rows_stored0"), sem("rows_stored1")]
        eps_added, y_used = sem("eps_added"), sem("y_used")
        block = ctx.enter_context(nc.Block())

        @block.sync
        def _(sp):
            sp.dma_start(cst[:], consts).then_inc(cst_in, 16)
            for n, g in enumerate((g_shift, g_base, b_shift, b_base)):
                sp.dma_start(gain[:, n, :], g).then_inc(w_in, 16)
            sp.dma_start(bias[:], tok_b).then_inc(w_in, 16)
            sp.dma_start(ws[:], w_shift).then_inc(w_in, 16)
            sp.dma_start(wb[:], w_base).then_inc(w_in, 16)
            for u in range(2):
                sp.dma_start(xg[:, u], x_blocks[u]).then_inc(x_in[u], 16)

            def more(it, u):
                sp.wait_ge(windows_ready, 2 * it + u + 1)
                sp.wait_ge(squared, 2 * it + u + 1)
                sp.dma_start(xg[:, u], x_blocks[bass.ds(2 * it + u + 2, 1)]).then_inc(x_in[u], 16)

            with sp.Fori(0, NGRP // 2 - 1) as it:
                for u in range(2):
                    more(it, u)
            more(NGRP // 2 - 1, 0)
            sp.wait_ge(rows_stored[0], 16 * (NGRP // 2 + 2))
            sp.wait_ge(rows_stored[1], 16 * (NGRP // 2 + 1))
            sp.wait_ge(zeroed, 1)
            sp.dma_start(resid[0:TI, :].rearrange("t (b d) -> t b d", b=NB),
                         tok_rows[0:NB * TI].rearrange("(b t) d -> t b d", t=TI)).then_inc(tok_in, 16)
            sp.wait_ge(tok_in, 16)
            sp.wait_ge(txt_in, 16)

        @block.gpsimd
        def _(pool):
            pool.memset(resid[:], 0.0).then_inc(zeroed, 1)
            pool.memset(zrow[:], 0.0).then_inc(zeroed, 1)
            pool.wait_ge(zeroed, 2)
            pool.dma_start(slot_mem.rearrange("(p a n) -> p a n", p=P, n=ZN),
                           zrow[:].unsqueeze(1).to_broadcast([P, NBLK0 * D // ZN, ZN])).then_inc(slots_clear, 16)
            pool.dma_start(resid[TI:T, :].rearrange("t (b d) -> t b d", b=NB),
                           txt.rearrange("b t d -> t b d")).then_inc(txt_in, 16)
            pool.wait_ge(cst_in, 16)

            def inverse_deviation(it, u):
                s = st[0:GM, u]
                pool.wait_ge(var_ready, 2 * it + u + 1)
                pool.tensor_tensor(s[:, 3:4], s[:, 2:3], cst[0:GM, C_EPS:C_EPS + 1], ALU.add).then_inc(eps_added, 1)
                pool.wait_ge(eps_added, 2 * it + u + 1)
                pool.tensor_tensor(s[:, 4:5], s[:, 3:4], cst[0:GM, C_NHALF:C_NHALF + 1], ALU.pow).then_inc(rstd_ready, 1)

            with pool.Fori(0, NGRP // 2) as it:
                for u in range(2):
                    inverse_deviation(it, u)
            inverse_deviation(NGRP // 2, 0)
            pool.wait_ge(slots_clear, 16)

        def window(u, q):
            a, b = q // 2, q % 2
            return xg[:, u].rearrange("p g (i j) -> p g i j", i=BLK)[:, :, a:a + 6, b:b + 6]

        def windows(x, u, q):
            return x[:, u, q * NCH:(q + 1) * NCH].rearrange("p c (s i j) -> p (c s) i j", s=GRP, i=6)

        @block.vector
        def _(dve):
            link = Link(dve, chain)

            def lay_windows(it, u):
                dve.wait_ge(x_in[u], 16 * it + 16)
                for q in range(4):
                    ins = dve.tensor_copy(windows(xw, u, q), window(u, q))
                ins.then_inc(windows_ready, 1)

            for u in range(2):
                lay_windows(0, u)
            dve.wait_ge(w_in, 7 * 16)

            def wide(n):
                return gain[:, n, :].unsqueeze(2).to_broadcast([P, NK, D])

            dve.tensor_tensor(weff[:, :, 0:D], ws[:], wide(0), ALU.mult).then_inc(chain, 1)
            dve.wait_ge(sums_ready, 1)
            dve.wait_ge(cst_in, 16)
            dve.tensor_tensor(wb[:], wb[:], wide(1), ALU.mult).then_inc(chain, 1)
            dve.wait_ge(chain, 2)
            dve.tensor_tensor(weff[:, :, 0:D], weff[:, :, 0:D], wb[:], ALU.add).then_inc(weff_ready, 1)
            dve.tensor_copy(weff[:, :, D], cst[:, C_MULT:C_MULT + NK]).then_inc(weff_ready, 1)
            link.base = 2
            dve.tensor_copy(shift[:], c_ps[:, 0, 0:D]).then_inc(sums_out, 1)
            dve.wait_ge(sums_ready, 2)
            dve.tensor_copy(colsum[:], c_ps[:, 1, 0:D]).then_inc(sums_out, 1)
            dve.wait_ge(sums_out, 2)

            for n, c in enumerate((C_ID, C_ONE, C_TRI, C_TRS)):
                dve.tensor_copy(cstb[:, n], cst[:, c:c + P])
            dve.memset(st[:, 0], 0.0).then_inc(y_used, 2)
            for u in range(2):
                dve.memset(rows[:, u], 0.0).then_inc(rows_stored[u], 16)

            def normalise(it, u):
                s = st[0:GM, u]
                dve.wait_ge(products_done, 2 * it + u + 1)
                link.done(dve.tensor_scalar(s[:, 0:1], y_ps[0:GM, u, D:D + 1], -1.0 / PATCH_DIM, None, ALU.mult))
                link.done(dve.tensor_tensor(s[:, 1:2], s[:, 0:1], s[:, 0:1], ALU.mult))
                dve.scalar_tensor_tensor(s[:, 2:3], q_ps[0:GM, u, 0:1], 1.0 / PATCH_DIM, s[:, 1:2],
                                         ALU.mult, ALU.subtract).then_inc(var_ready, 1)
                dve.scalar_tensor_tensor(tok[0:GM, u], colsum[0:GM], s[:, 0:1], y_ps[0:GM, u, 0:D],
                                         ALU.mult, ALU.add).then_inc(y_used, 1)
                dve.wait_ge(y_used, 2 * it + u + 3)
                dve.wait_ge(rstd_ready, 2 * it + u + 1)
                dve.wait_ge(rows_stored[u], 16 * it + 16)
                dve.scalar_tensor_tensor(rows[0:GM, u], tok[0:GM, u], s[:, 4:5], shift[0:GM], ALU.mult, ALU.add)\
                   .then_inc(tok_ready, 1)

            with dve.Fori(0, NGRP // 2 - 1) as it:
                link.loop(it, 4)
                for u in range(2):
                    normalise(it, u)
                    lay_windows(it + 1, u)
            link.end(NGRP // 2 - 1)
            last = NGRP // 2 - 1
            normalise(last, 0)
            lay_windows(last + 1, 0)
            normalise(last, 1)
            normalise(last + 1, 0)

        @block.scalar
        def _(act):
            def square(it, u):
                act.wait_ge(x_in[u], 16 * it + 16)
                for q in range(4):
                    ins = act.activation(windows(xsq, u, q), window(u, q), ACT.Square)
                ins.then_inc(squared, 1)

            def finish(it, u):
                g1 = 2 * it + u + 1
                act.wait_ge(tok_ready, g1)
                n = GRP * TI
                act.dma_start(tok_rows[bass.ds((2 * it + u) * n, n), :], rows[0:n, u, :])\
                   .then_inc(rows_stored[u], 16)

            for u in range(2):
                square(0, u)
            with act.Fori(0, NGRP // 2 - 1) as it:
                for u in range(2):
                    act.wait_ge(products_done, 2 * it + u + 1)
                    square(it + 1, u)
                    finish(it, u)
            it = NGRP // 2 - 1
            act.wait_ge(products_done, 2 * it + 1)
            square(it + 1, 0)
            finish(it, 0)
            finish(it, 1)
            finish(it + 1, 0)

        @block.tensor
        def _(pe):
            ones = cst[:, C_ONE:C_ONE + P]
            pe.wait_ge(w_in, 7 * 16)
            pe.wait_ge(cst_in, 16)
            pe.matmul(c_ps[:, 0, 0:D], ones[0:1, :], bias[:], start=True, stop=False)
            for part, w in ((2, ws), (3, wb)):
                for k in range(NK):
                    mm = pe.matmul(c_ps[:, 0, 0:D], gain[:, part, k:k + 1].to_broadcast([P, P]), w[:, k, :],
                                   start=False, stop=part == 3 and k == NK - 1)
            mm.then_inc(sums_ready, 1)
            pe.wait_ge(weff_ready, 2)
            for k in range(NK):
                mm = pe.matmul(c_ps[:, 1, 0:D], ones, weff[:, k, 0:D], start=k == 0, stop=k == NK - 1)
            mm.then_inc(sums_ready, 1)

            def group(it, u):
                m = GRP * TI
                pe.wait_ge(windows_ready, 2 * it + u + 1)
                for k in range(NK):
                    pe.matmul(y_ps[0:m, u, 0:D + 1], xw[:, u, k, :], weff[:, k, :], start=k == 0, stop=k == NK - 1)
                pe.wait_ge(squared, 2 * it + u + 1)
                for k in range(NK):
                    mm = pe.matmul(q_ps[0:m, u, 0:1], xsq[:, u, k, :], weff[:, k, D:D + 1],
                                   start=k == 0, stop=k == NK - 1)
                mm.then_inc(products_done, 1)

            with pe.Fori(0, NGRP // 2) as it:
                for u in range(2):
                    pe.wait_ge(y_used, 2 * it + u + 1)
                    group(it, u)
            pe.wait_ge(y_used, NGRP)
            group(NGRP // 2, 0)


def layer_norm_stats(nc, name, resid, cst, mean, rstd):
    with ExitStack() as ctx:
        take = ctx.enter_context(semaphores(nc))
        six = ctx.enter_context(nc.sbuf_tensor(name + "_six", [P, NB, 6], F32))
        ve = ctx.enter_context(nc.sbuf_tensor(name + "_ve", [P, NB], F32))
        six_ready = take(name + "_six_ready")
        var = ctx.enter_context(nc.sbuf_tensor(name + "_var", [P, NB], F32))
        tmp = ctx.enter_context(nc.sbuf_tensor(name + "_tmp", [P, 4, NB], F32))
        var_ready = take(name + "_var_ready")
        chain = take(name + "_chain")
        ve_ready = take(name + "_ve_ready")
        block = ctx.enter_context(nc.Block())

        @block.vector
        def _(dve):
            with dve.Fori(0, NB) as b:
                dve.bn_stats(six[:, bass.ds(b, 1), :], resid[:, bass.ds(b * D, D)]).then_inc(six_ready, 1)
            dve.wait_ge(six_ready, NB)
            link = Link(dve, chain)
            dve.tensor_tensor(tmp[:, 0], six[:, :, 1], six[:, :, 4], ALU.add).then_inc(chain, 1)
            dve.tensor_tensor(tmp[:, 1], six[:, :, 1], six[:, :, 4], ALU.subtract).then_inc(chain, 1)
            dve.tensor_tensor(tmp[:, 2], six[:, :, 2], six[:, :, 5], ALU.add).then_inc(chain, 1)
            dve.wait_ge(chain, 3)
            link.base = 3
            dve.tensor_scalar(mean[:], tmp[:, 0], 0.5, None, ALU.mult).then_inc(var_ready, 1)
            link.done(dve.scalar_tensor_tensor(tmp[:, 3], tmp[:, 1], 0.25, tmp[:, 1], ALU.mult, ALU.mult))
            dve.scalar_tensor_tensor(var[:], tmp[:, 2], 1.0 / D, tmp[:, 3], ALU.mult, ALU.add).then_inc(var_ready, 1)
            dve.wait_ge(var_ready, 2)

        @block.gpsimd
        def _(pool):
            pool.wait_ge(var_ready, 2)
            pool.tensor_scalar(ve[:], var[:], LN_EPS, None, ALU.add).then_inc(ve_ready, 1)
            pool.wait_ge(ve_ready, 1)
            pool.tensor_tensor(rstd[:], ve[:], cst[:, C_NHALF:C_NHALF + 1].to_broadcast([P, NB]), ALU.pow)\
                .then_inc(ve_ready, 1)
            pool.wait_ge(ve_ready, 2)


def channel_attention(nc, wqk_d, wv_d, wp_d, bp_d, temp_d, cst, resid, mean, rstd):
    U = 4
    with ExitStack() as ctx:
        take = ctx.enter_context(semaphores(nc))
        def sb(name, shape, dt=F32):
            return ctx.enter_context(nc.sbuf_tensor("ca_" + name, shape, dt))

        def sem(name):
            return take("ca_" + name)

        wqk, wv, wp = sb("wqk", [DH, 2, 2 * D]), sb("wv", [DH, 2, D]), sb("wp", [DH, 2, D])
        bp, temp = sb("bp", [1, D]), sb("temp", [DH, 2])
        hn = sb("hn", [P, U, D])
        hnt = sb("hnt", [DH, U, 2, P])
        qk = sb("qk", [P, U, 2 * D])
        sq = sb("sq", [P, U, 2 * D])
        vt = sb("vt", [DH, U, 2, P])
        ss = sb("ss", [DH, U, D + 2])
        rn = sb("rn", [DH, U, D + 2])
        rqt = sb("rqt", [DH, U, 2])
        sc = sb("sc", [DH, U, 2, DH])
        pr = sb("pr", [DH, U, 2, DH])
        nmx, sm, rs = sb("nmx", [DH, U, 2]), sb("sm", [DH, U, 2]), sb("rs", [DH, U, 2])
        mix = sb("mix", [DH, U, 2, D])
        pa = ctx.enter_context(nc.psum_tensor("ca_pa", [P, U, 512], F32))
        pb = ctx.enter_context(nc.psum_tensor("ca_pb", [P, U, 512], F32))
        w_in, hn_ready, hnt_ps, hnt_ready = sem("w_in"), sem("hn_ready"), sem("hnt_ps"), sem("hnt_ready")
        qk_ps, qk_ready, sq_ready, vt_ps = sem("qk_ps"), sem("qk_ready"), sem("sq_ready"), sem("vt_ps")
        vt_ready, gram_ps, ss_ready = sem("vt_ready"), sem("gram_ps"), sem("ss_ready")
        max_ready, exp_ready, attn_ready = sem("max_ready"), sem("exp_ready"), sem("attn_ready")
        mix_ps, mix_ready, out_ps, chain = sem("mix_ps"), sem("mix_ready"), sem("out_ps"), sem("chain")
        block = ctx.enter_context(nc.Block())

        @block.sync
        def _(sp):
            for dst, src in ((wqk, wqk_d), (wv, wv_d), (wp, wp_d), (bp, bp_d), (temp, temp_d)):
                sp.dma_start(dst[:], src).then_inc(w_in, 16)
            sp.wait_ge(w_in, 5 * 16)

        @block.tensor
        def _(pe):
            ident = cst[:, C_ID:C_ID + P]
            ones = cst[:, C_ONE:C_ONE + P]
            pe.wait_ge(w_in, 5 * 16)
            with pe.Fori(0, NB // U) as it:
                for u in range(U):
                    pe.wait_ge(hn_ready, it * U + u + 1)
                    for c in range(2):
                        mm = pe.transpose(pa[0:DH, u, c * P:(c + 1) * P], hn[:, u, c * DH:(c + 1) * DH], ident)
                    mm.then_inc(hnt_ps, 1)
                for u in range(U):
                    pe.wait_ge(hnt_ready, it * U + u + 1)
                    for c in range(2):
                        mm = pe.matmul(pb[:, u, 0:2 * D], hnt[:, u, c], wqk[:, c], start=c == 0, stop=c == 1)
                    mm.then_inc(qk_ps, 1)
                for u in range(U):
                    for g in range(2):
                        for c in range(2):
                            mm = pe.matmul(pa[0:DH, u, g * P:(g + 1) * P], wv[:, c, g * DH:(g + 1) * DH],
                                           hnt[:, u, c], start=c == 0, stop=c == 1)
                    mm.then_inc(vt_ps, 1)
                for u in range(U):
                    pe.wait_ge(qk_ready, it * U + u + 1)
                    for g in range(2):
                        pe.matmul(pb[0:DH, u, g * DH:(g + 1) * DH], qk[:, u, g * DH:(g + 1) * DH],
                                  qk[:, u, D + g * DH:D + (g + 1) * DH], start=True, stop=True)
                    pe.wait_ge(sq_ready, it * U + u + 1)
                    pe.matmul(pb[0:DH, u, D:2 * D], ones[:, 0:DH], sq[:, u, D:2 * D], start=True, stop=True)
                    for g in range(2):
                        mm = pe.matmul(pb[0:DH, u, 2 * D + g:2 * D + g + 1], sq[:, u, g * DH:(g + 1) * DH],
                                       ones[:, 0:1], start=True, stop=True)
                    mm.then_inc(gram_ps, 1)
                for u in range(U):
                    pe.wait_ge(vt_ready, it * U + u + 1)
                    pe.wait_ge(attn_ready, it * U + u + 1)
                    for g in range(2):
                        mm = pe.matmul(pa[0:DH, u, g * D:(g + 1) * D], pr[:, u, g], wp[:, g], start=True, stop=True)
                    mm.then_inc(mix_ps, 1)
                for u in range(U):
                    pe.wait_ge(mix_ready, it * U + u + 1)
                    for g in range(2):
                        pe.matmul(pb[0:T, u, 0:D], vt[:, u, g, 0:T], mix[:, u, g], start=g == 0, stop=False)
                    pe.matmul(pb[0:T, u, 0:D], ones[0:1, 0:T], bp[:], start=False, stop=True).then_inc(out_ps, 1)

        @block.scalar
        def _(act):
            with act.Fori(0, NB // U) as it:
                for u in range(U):
                    act.wait_ge(hnt_ps, it * U + u + 1)
                    act.copy(hnt[:, u], pa[0:DH, u, 0:2 * P].rearrange("p (c t) -> p c t", c=2)).then_inc(hnt_ready, 1)
                for u in range(U):
                    act.wait_ge(qk_ps, it * U + u + 1)
                    act.copy(qk[:, u], pb[:, u, 0:2 * D]).then_inc(qk_ready, 1)
                for u in range(U):
                    act.wait_ge(vt_ps, it * U + u + 1)
                    act.copy(vt[:, u], pa[0:DH, u, 0:2 * P].rearrange("p (c t) -> p c t", c=2)).then_inc(vt_ready, 1)
                for u in range(U):
                    act.wait_ge(gram_ps, it * U + u + 1)
                    act.activation(ss[:, u], pb[0:DH, u, D:2 * D + 2], ACT.Sqrt).then_inc(ss_ready, 1)
                for u in range(U):
                    act.wait_ge(max_ready, it * U + u + 1)
                    for g in range(2):
                        ins = act.activation(pr[:, u, g], sc[:, u, g], ACT.Exp, bias=nmx[:, u, g:g + 1],
                                             accum_out=sm[:, u, g:g + 1])
                        ins.then_inc(exp_ready, 1)
                for u in range(U):
                    act.wait_ge(mix_ps, it * U + u + 1)
                    act.copy(mix[:, u], pa[0:DH, u, 0:2 * D].rearrange("p (g d) -> p g d", g=2)).then_inc(mix_ready, 1)

        @block.gpsimd
        def _(pool):
            with pool.Fori(0, NB // U) as it:
                for u in range(U):
                    pool.wait_ge(qk_ready, it * U + u + 1)
                    pool.tensor_tensor(sq[:, u], qk[:, u], qk[:, u], ALU.mult).then_inc(sq_ready, 1)

        @block.vector
        def _(dve):
            link = Link(dve, chain)
            dve.wait_ge(w_in, 5 * 16)
            with dve.Fori(0, NB // U) as it:
                link.loop(it, U * 8)
                for u in range(U):
                    b = it * U + u
                    dve.tensor_scalar(hn[:, u], resid[:, bass.ds(b * D, D)], mean[:, bass.ds(b, 1)],
                                      rstd[:, bass.ds(b, 1)], ALU.subtract, ALU.mult).then_inc(hn_ready, 1)
                for u in range(U):
                    dve.wait_ge(ss_ready, it * U + u + 1)
                    link.done(dve.reciprocal(rn[:, u], ss[:, u]))
                    dve.tensor_tensor(rqt[:, u], rn[:, u, D:D + 2], temp[:], ALU.mult).then_inc(chain, 1)
                    link.n += 1
                    link.done(dve.tensor_tensor(sc[:, u].rearrange("p g d -> p (g d)"), pb[0:DH, u, 0:D], rn[:, u, 0:D],
                                                ALU.mult))
                    for g in range(2):
                        ins = dve.scalar_tensor_tensor(sc[:, u, g], sc[:, u, g], rqt[:, u, g:g + 1],
                                                       cst[0:DH, C_BLKM:C_BLKM + DH], ALU.mult, ALU.add)
                        if g == 0:
                            ins.then_inc(chain, 1)
                            link.n += 1
                    link.done(ins)
                    link.done(dve.tensor_reduce(rs[:, u], sc[:, u], AX.X, ALU.max))
                    dve.tensor_scalar(nmx[:, u], rs[:, u], -1.0, None, ALU.mult).then_inc(max_ready, 1)
                for u in range(U):
                    dve.wait_ge(max_ready, it * U + u + 1)
                    dve.wait_ge(exp_ready, 2 * (it * U + u) + 2)
                    link.done(dve.reciprocal(rs[:, u], sm[:, u]))
                    dve.tensor_tensor(pr[:, u], pr[:, u], rs[:, u].unsqueeze(2).to_broadcast([DH, 2, DH]), ALU.mult)\
                       .then_inc(attn_ready, 1)
                for u in range(U):
                    b = it * U + u
                    dve.wait_ge(out_ps, it * U + u + 1)
                    h = resid[0:T, bass.ds(b * D, D)]
                    link.done(dve.tensor_tensor(h, h, pb[0:T, u, 0:D], ALU.add))


def route_tokens(nc, emb_d, wcat_d, bcat_d, cst, resid, mean, rstd, embt, chosen, weight, index):
    U = 4
    with ExitStack() as ctx:
        take = ctx.enter_context(semaphores(nc))
        def sb(name, shape, dt=F32):
            return ctx.enter_context(nc.sbuf_tensor("rt_" + name, shape, dt))

        def sem(name):
            return take("rt_" + name)

        emb = sb("emb", [NE, 2, 64])
        junk, ess = sb("junk", [NE, 64]), sb("ess", [NE, 2])
        wcat, bcat = sb("wcat", [DH, 2, P]), sb("bcat", [P, 1])
        hn = sb("hn", [P, U, D])
        hnt = sb("hnt", [DH, U, 2, P])
        zt = sb("zt", [P, U, P])
        e = sb("e", [P, U * 2, NE + 4])
        zap = sb("zap", [P, U * 2, NE + 4])
        top8, taken = sb("top8", [P, U * 2, 8]), sb("taken", [P, U * 2, 8])
        ix = sb("ix", [P, U * 2, 8], U32)
        mx, nmx, z = sb("mx", [P, U, 2]), sb("nmx", [P, U, 2]), sb("z", [P, U * 2])
        zc = sb("zc", [P, U * 2])
        s4, den, rden = sb("s4", [P, U * 2]), sb("den", [P, U * 2]), sb("rden", [P, U * 2])
        pa = ctx.enter_context(nc.psum_tensor("rt_pa", [P, U, 512], F32))
        pb = ctx.enter_context(nc.psum_tensor("rt_pb", [P, U, 512], F32))
        w_in, setup, chain = sem("w_in"), sem("setup"), sem("chain")
        emb_sq, emb_norm, emb_unit, emb_ps, embt_ready = (
            sem("emb_sq"), sem("emb_norm"), sem("emb_unit"), sem("emb_ps"), sem("embt_ready"))
        hn_ready, hnt_ps, hnt_ready, z_ps, z_ready = (
            sem("hn_ready"), sem("hnt_ps"), sem("hnt_ready"), sem("z_ps"), sem("z_ready"))
        logit_ps, max_ready, exp_ready = sem("logit_ps"), sem("max_ready"), sem("exp_ready")
        block = ctx.enter_context(nc.Block())

        @block.sync
        def _(sp):
            for dst, src in ((emb, emb_d), (wcat, wcat_d), (bcat, bcat_d)):
                sp.dma_start(dst[:], src).then_inc(w_in, 16)
            sp.wait_ge(w_in, 3 * 16)

        @block.scalar
        def _(act):
            act.wait_ge(w_in, 3 * 16)
            for r in range(2):
                if r:
                    act.wait_ge(emb_sq, r)
                act.activation(junk[:], emb[:, r], ACT.Square, accum_out=ess[:, r:r + 1]).then_inc(emb_sq, 1)
            act.wait_ge(emb_sq, 2)
            act.activation(den[:, 0:2], ess[:], ACT.Sqrt).then_inc(emb_norm, 1)
            with act.Fori(0, NB // U) as it:
                for u in range(U):
                    act.wait_ge(hnt_ps, it * U + u + 1)
                    act.copy(hnt[:, u], pa[0:DH, u, 0:2 * P].rearrange("p (c t) -> p c t", c=2)).then_inc(hnt_ready, 1)
                for u in range(U):
                    act.wait_ge(z_ps, it * U + u + 1)
                    act.activation(zt[:, u], pb[:, u, 0:P], ACT.Identity, bias=bcat[:]).then_inc(z_ready, 1)
                for u in range(U):
                    act.wait_ge(max_ready, it * U + u + 1)
                    for r in range(2):
                        ins = act.activation(e[:, 2 * u + r, 0:NE], pa[:, u, r * NE:(r + 1) * NE], ACT.Exp,
                                             bias=nmx[:, u, r:r + 1], accum_out=z[:, 2 * u + r:2 * u + r + 1])
                    ins.then_inc(exp_ready, 1)

        @block.tensor
        def _(pe):
            ident = cst[:, C_ID:C_ID + P]
            pe.wait_ge(emb_unit, 1)
            pe.transpose(pa[:, 0, 0:P], emb[:].rearrange("n r d -> n (r d)"), ident).then_inc(emb_ps, 1)
            pe.wait_ge(embt_ready, 4)
            with pe.Fori(0, NB // U) as it:
                for u in range(U):
                    pe.wait_ge(hn_ready, it * U + u + 1)
                    for c in range(2):
                        mm = pe.transpose(pa[0:DH, u, c * P:(c + 1) * P], hn[:, u, c * DH:(c + 1) * DH], ident)
                    mm.then_inc(hnt_ps, 1)
                for u in range(U):
                    pe.wait_ge(hnt_ready, it * U + u + 1)
                    for c in range(2):
                        mm = pe.matmul(pb[:, u, 0:P], wcat[:, c], hnt[:, u, c], start=c == 0, stop=c == 1)
                    mm.then_inc(z_ps, 1)
                for u in range(U):
                    pe.wait_ge(z_ready, it * U + u + 1)
                    pe.matmul(pa[:, u, 0:2 * NE], zt[:, u], embt[:], start=True, stop=True).then_inc(logit_ps, 1)

        @block.vector
        def _(dve):
            link = Link(dve, chain)
            dve.memset(embt[0:64, NE:2 * NE], 0.0).then_inc(embt_ready, 1)
            dve.memset(embt[64:P, 0:NE], 0.0).then_inc(embt_ready, 1)
            dve.wait_ge(emb_norm, 1)
            link.done(dve.tensor_scalar(s4[:, 0:2], den[:, 0:2], 1e-8, None, ALU.add))
            link.done(dve.reciprocal(rden[:, 0:2], s4[:, 0:2]))
            dve.tensor_tensor(emb[:], emb[:], rden[:, 0:2].unsqueeze(2).to_broadcast([NE, 2, 64]), ALU.mult)\
               .then_inc(emb_unit, 1)
            dve.wait_ge(emb_ps, 1)
            dve.tensor_copy(embt[0:64, 0:NE], pa[0:64, 0, 0:NE]).then_inc(embt_ready, 1)
            dve.tensor_copy(embt[64:P, NE:2 * NE], pa[64:P, 0, 0:NE]).then_inc(embt_ready, 1)
            for buf, at in ((e, NE), (taken, 4)):
                link.done(dve.tensor_copy(buf[:, :, at:at + 4],
                                          cst[:, C_SENT:C_SENT + 4].unsqueeze(1).to_broadcast([P, 2 * U, 4])))
            with dve.Fori(0, NB // U) as it:
                link.loop(it, U + 1 + 4 + 1)
                for u in range(U):
                    b = it * U + u
                    dve.tensor_scalar(hn[:, u], resid[:, bass.ds(b * D, D)], mean[:, bass.ds(b, 1)],
                                      rstd[:, bass.ds(b, 1)], ALU.subtract, ALU.mult).then_inc(hn_ready, 1)
                for u in range(U):
                    dve.wait_ge(logit_ps, it * U + u + 1)
                    link.done(dve.tensor_reduce(mx[:, u], pa[:, u, 0:2 * NE].rearrange("p (r n) -> p r n", r=2),
                                                AX.X, ALU.max))
                    dve.tensor_scalar(nmx[:, u], mx[:, u], -1.0, None, ALU.mult).then_inc(max_ready, 1)
                for u in range(U):
                    dve.wait_ge(exp_ready, it * U + u + 1)
                    dve.tensor_copy(zc[:, 2 * u:2 * u + 2], z[:, 2 * u:2 * u + 2])
                    for r in range(2):
                        ins = dve.max(top8[:, 2 * u + r], e[:, 2 * u + r, 0:NE])
                link.done(ins)
                link.done(dve.tensor_copy(taken[:, :, 0:4], top8[:, :, 0:4]))
                dve.tensor_reduce(s4[:], top8[:, :, 0:4], AX.X, ALU.add)
                for k in range(2 * U):
                    dve.max_index(ix[:, k], top8[:, k], e[:, k, 0:NE])
                    ins = dve.match_replace(zap[:, k], taken[:, k], e[:, k], -9.0)
                link.done(ins)
                link.done(dve.scalar_tensor_tensor(den[:], zc[:], 1e-8, s4[:], ALU.mult, ALU.add))
                for k in range(2 * U):
                    dve.tensor_scalar(chosen[:, bass.ds((it * U + k // 2) * 2 + k % 2, 1), :],
                                      zap[:, k:k + 1, 0:NE], -5.0, cst[:, C_VALID:C_VALID + 1], ALU.is_lt, ALU.mult)
                link.done(dve.reciprocal(rden[:], den[:]))
                dve.tensor_copy(index[:, bass.ds(it * 2 * U, 2 * U), :], ix[:, :, 0:4])
                link.done(dve.tensor_tensor(weight[:, bass.ds(it * 2 * U, 2 * U), :], top8[:, :, 0:4],
                                            rden[:].unsqueeze(2).to_broadcast([P, 2 * U, 4]), ALU.mult))


def block_tables(nc, cst, cstb, chosen, seg_start, block_expert):
    with ExitStack() as ctx:
        take = ctx.enter_context(semaphores(nc))
        def sb(name, shape, dt=F32):
            return ctx.enter_context(nc.sbuf_tensor("bt_" + name, shape, dt))

        def sem(name):
            return take("bt_" + name)

        total = sb("total", [P, 2 * NE], BF16)
        more, blocks_i = sb("more", [P, 2], I32), sb("blocks_i", [P, 2], I32)
        blocks, blocks_b = sb("blocks", [P, 2]), sb("blocks_b", [P, 2], BF16)
        incl, before = sb("incl", [P, 2]), sb("before", [P, 2, 256], BF16)
        row = sb("row", [1, 2, 256])
        ps = ctx.enter_context(nc.psum_tensor("bt_ps", [P, 3, 512], F32))
        total_ready, count_ps, blocks_ready = sem("total_ready"), sem("count_ps"), sem("blocks_ready")
        incl_ps, before_ready, row_ps, chain = sem("incl_ps"), sem("before_ready"), sem("row_ps"), sem("chain")
        block = ctx.enter_context(nc.Block())

        @block.vector
        def _(dve):
            link = Link(dve, chain)
            link.done(dve.tensor_copy(total[:], chosen[:, 0:2].rearrange("p r n -> p (r n)")))
            with dve.Fori(1, NB) as b:
                link.loop(b - 1, 1)
                link.done(dve.tensor_tensor(total[:].rearrange("p (r n) -> p r n", r=2),
                                            total[:].rearrange("p (r n) -> p r n", r=2),
                                            chosen[:, bass.ds(2 * b, 2), :], ALU.add))
            link.end(NB - 1)
            dve.memset(row[:], 0.0).then_inc(total_ready, 1)
            dve.wait_ge(count_ps, 1)
            link.done(dve.tensor_scalar(more[:], ps[:, 0, 0:2], P - 1.0, None, ALU.add))
            link.done(dve.tensor_scalar(blocks_i[:], more[:], 7, None, ALU.arith_shift_right))
            link.done(dve.tensor_copy(blocks[:], blocks_i[:]))
            dve.tensor_copy(blocks_b[:], blocks[:]).then_inc(blocks_ready, 1)
            for r in range(2):
                dve.tensor_scalar(seg_start[:, r], cst[:, C_ONE:C_ONE + P], blocks[:, r:r + 1], float(P),
                                  ALU.mult, ALU.mult)
            dve.wait_ge(incl_ps, 1)
            link.done(dve.tensor_copy(incl[:], ps[:, 1, 0:2]))
            for r in range(2):
                dve.tensor_scalar(before[:, r], cst[:, C_IOTA:C_IOTA + 256], incl[:, r:r + 1], None, ALU.is_ge)\
                   .then_inc(before_ready, 1)
            dve.wait_ge(row_ps, 1)
            link.done(dve.tensor_scalar(block_expert[:], ps[0:1, 2, 0:512].rearrange("p (r t) -> p r t", r=2),
                                        NE - 1.0, None, ALU.min))

        @block.tensor
        def _(pe):
            ones = cstb[:, 1]
            pe.wait_ge(total_ready, 1)
            for r in range(2):
                mm = pe.matmul(ps[:, 0, r:r + 1], total[:, r * NE:(r + 1) * NE], ones[:, 0:1], start=True, stop=True)
            mm.then_inc(count_ps, 1)
            pe.wait_ge(blocks_ready, 1)
            pe.matmul(ps[:, 1, 0:2], cstb[:, 2], blocks_b[:], start=True, stop=True).then_inc(incl_ps, 1)
            pe.wait_ge(before_ready, 2)
            pe.matmul(ps[0:1, 2, 0:512], ones[:, 0:1], before[:].rearrange("p r t -> p (r t)"), start=True, stop=True)\
              .then_inc(row_ps, 1)


def place_tokens(nc, cst, cstb, resid, mean, rstd, chosen, index, seg_start, slot, slot_rows):
    U = 4
    with ExitStack() as ctx:
        take = ctx.enter_context(semaphores(nc))
        def sb(name, shape, dt=F32):
            return ctx.enter_context(nc.sbuf_tensor("pl_" + name, shape, dt))

        def sem(name):
            return take("pl_" + name)

        earlier = sb("earlier", [P, U + 1, 2, NE], BF16)
        junk = sb("junk", [P, 8, NE], BF16)
        slot_f = sb("slot_f", [P, U, 8])
        slot_i = sb("slot_i", [P, U, 8], I32)
        hn = sb("hn", [P, U, D])
        rank = ctx.enter_context(nc.psum_tensor("pl_rank", [P, U, 512], F32))
        chain, summed, rank_ps, slot_ready = sem("chain"), sem("summed"), sem("rank_ps"), sem("slot_ready")
        scattered = [sem(f"scattered{u}") for u in range(U)]
        block = ctx.enter_context(nc.Block())

        @block.tensor
        def _(pe):
            with pe.Fori(0, NB // U) as it:
                for u in range(U):
                    b2 = 2 * (it * U + u)
                    pe.wait_ge(summed, it * U + u + 1)
                    pe.matmul(rank[:, u, 0:2 * NE], cstb[:, 3], chosen[:, bass.ds(b2, 2), :], start=True, stop=False)
                    pe.matmul(rank[:, u, 0:2 * NE], cstb[:, 1], earlier[:, u], start=False, stop=False)
                    for r in range(2):
                        mm = pe.matmul(rank[:, u, r * NE:(r + 1) * NE], seg_start[:, r], cstb[:, 3],
                                       start=False, stop=r == 1)
                    mm.then_inc(rank_ps, 1)

        @block.vector
        def _(dve):
            link = Link(dve, chain)
            link.done(dve.memset(earlier[:, U], 0.0))

            def turn(it, first):
                for u in range(U):
                    if u == 0:
                        ins = dve.tensor_copy(earlier[:, 0], earlier[:, U])
                    else:
                        ins = dve.tensor_tensor(earlier[:, u], earlier[:, u - 1],
                                                chosen[:, bass.ds(2 * (it * U + u - 1), 2), :], ALU.add)
                    ins.then_inc(summed, 1)
                    dve.wait_ge(summed, it * U + u + 1)
                for u in range(U):
                    b = it * U + u
                    if u == 0:
                        link.done(dve.tensor_tensor(earlier[:, U], earlier[:, U - 1],
                                                    chosen[:, bass.ds(2 * (it * U + U - 1), 2), :], ALU.add))
                    if not first:
                        dve.wait_ge(scattered[u], 64 * it)
                    dve.tensor_scalar(hn[:, u], resid[:, bass.ds(b * D, D)], mean[:, bass.ds(b, 1)],
                                      rstd[:, bass.ds(b, 1)], ALU.subtract, ALU.mult).then_inc(slot_ready, 1)
                    dve.wait_ge(rank_ps, b + 1)
                    for k in range(8):
                        r, j = k // 4, k % 4
                        ins = dve.scalar_tensor_tensor(junk[:, k], cst[:, C_IOTA:C_IOTA + NE],
                                                       index[:, bass.ds(2 * b + r, 1), j], rank[:, u, r * NE:(r + 1) * NE],
                                                       ALU.is_equal, ALU.mult, accum_out=slot_f[:, u, k:k + 1])
                    link.done(ins)
                    ins = dve.tensor_scalar(slot_i[:, u], slot_f[:, u], cst[:, C_FAR:C_FAR + 1], None, ALU.add)
                    ins.then_inc(slot_ready, 1)
                    dve.wait_ge(slot_ready, 2 * b + 2)
                    link.done(dve.tensor_copy(slot[:, bass.ds(b, 1), :], slot_i[:, u:u + 1]))

            turn(0, True)
            with dve.Fori(1, NB // U) as it:
                link.loop(it - 1, 1 + 2 * U)
                turn(it, False)

        @block.gpsimd
        def _(pool):
            last_slot = pool.to_reg(NBLK0 * P - 1)
            for it in range(NB // U):
                for u in range(U):
                    pool.wait_ge(slot_ready, 2 * (it * U + u) + 2)
                    for j in range(4):
                        pool.indirect_dma_start(slot_rows, bass.IndirectOffsetOnAxis(slot_i[:, u, j:j + 1], 0),
                                                hn[:, u], None, bounds_check=last_slot, oob_is_err=False)\
                            .then_inc(scattered[u], 16)
            for u in range(U):
                pool.wait_ge(scattered[u], 64 * (NB // U))


def blocks_product(nc, name, cst, block_expert, part, rows_in, weights, rows_out, k, n):
    W = 8
    kc = -(-k // P)
    kp = k // kc
    turns = NBLK0 // W
    with ExitStack() as ctx:
        take = ctx.enter_context(semaphores(nc))
        def sb(nm, shape, dt=F32):
            return ctx.enter_context(nc.sbuf_tensor(f"{name}_{nm}", shape, dt))

        def sem(nm):
            return take(f"{name}_{nm}")

        x = sb("x", [P, W, k])
        w = sb("w", [kp, W, kc, n])
        xt = sb("xt", [kp, W, kc, P])
        y = sb("y", [P, W, n])
        start = sb("start", [1, 1])
        t_ps = ctx.enter_context(nc.psum_tensor(name + "_t_ps", [P, 4, 512], F32))
        y_ps = ctx.enter_context(nc.psum_tensor(name + "_y_ps", [P, 4, 512], F32))
        x_t, xt_ready, product, y_ready = sem("x_t"), sem("xt_ready"), sem("product"), sem("y_ready")
        loaded = [sem(f"loaded{u}") for u in range(W)]
        stored = [sem(f"stored{u}") for u in range(W)]
        block = ctx.enter_context(nc.Block())

        @block.sync
        def _(sp):
            def load(t, u):
                e = sp.value_load(block_expert[0:1, part, bass.ds(t, 1)], min_val=0, max_val=NE - 1)
                sp.dma_start(x[:, u], rows_in[bass.ds(t * P, P), :]).then_inc(loaded[u], 16)
                sp.dma_start(w[:, u], weights[bass.ds(e, 1)].rearrange("a (c p) n -> p (a c) n", p=kp))\
                  .then_inc(loaded[u], 16)

            for u in range(W):
                load(u, u)
            with sp.Fori(0, turns - 1) as it:
                for u in range(W):
                    sp.wait_ge(product, it * W + u + 1)
                    load(it * W + W + u, u)

        @block.tensor
        def _(pe):
            ident = cst[:, C_ID:C_ID + P]

            def turn(it, u):
                pe.wait_ge(loaded[u], 32 * it + 32)
                pe.wait_ge(y_ready, it * W + u + 1)
                for c in range(kc):
                    mm = pe.transpose(t_ps[0:kp, u % 4, c * P:(c + 1) * P], x[:, u, c * kp:(c + 1) * kp], ident)
                mm.then_inc(x_t, 1)

            def multiply(it, u):
                pe.wait_ge(xt_ready, it * W + u + 1)
                for c in range(kc):
                    mm = pe.matmul(y_ps[:, u % 4, 0:n], xt[:, u, c], w[:, u, c], start=c == 0, stop=c == kc - 1)
                mm.then_inc(product, 1)

            with pe.Fori(0, turns) as it:
                turn(it, 0)
                for u in range(W):
                    if u + 1 < W:
                        turn(it, u + 1)
                    multiply(it, u)

        @block.scalar
        def _(act):
            def send(it, u):
                act.wait_ge(y_ready, 4 + it * W + u + 1)
                act.dma_start(rows_out[bass.ds((it * W + u) * P, P), :], y[:, u]).then_inc(stored[u], 16)

            with act.Fori(0, turns) as it:
                for u in range(W):
                    act.wait_ge(x_t, it * W + u + 1)
                    act.copy(xt[:, u], t_ps[0:kp, u % 4, 0:kc * P].rearrange("p (c t) -> p c t", c=kc))\
                       .then_inc(xt_ready, 1)
                    if u >= 2:
                        send(it, u - 2)
                send(it, W - 2)
                send(it, W - 1)
            for u in range(W):
                act.wait_ge(stored[u], 16 * (turns + 1))

        @block.vector
        def _(dve):
            for u in range(W):
                dve.memset(y[:, u], 0.0).then_inc(stored[u], 16)
            dve.memset(start[:], 0.0).then_inc(y_ready, 4)
            with dve.Fori(0, turns) as it:
                for u in range(W):
                    dve.wait_ge(product, it * W + u + 1)
                    dve.wait_ge(stored[u], 16 * it + 16)
                    dve.tensor_copy(y[:, u], y_ps[:, u % 4, 0:n]).then_inc(y_ready, 1)


def combine_rows(nc, name, cst, slot, weight, part, rows, n, resid, next_rows):
    U = 4
    with ExitStack() as ctx:
        take = ctx.enter_context(semaphores(nc))
        def sb(nm, shape, dt=F32):
            return ctx.enter_context(nc.sbuf_tensor(f"{name}_{nm}", shape, dt))

        def sem(nm):
            return take(f"{name}_{nm}")

        g = sb("g", [P, U, 4, n])
        acc = sb("acc", [P, U, n])
        idx = sb("idx", [P, U, 8], I32)
        gathered = [sem(f"gathered{u}") for u in range(U)]
        scattered = [sem(f"scattered{u}") for u in range(U)]
        idx_ready, cleared, summed, chain = sem("idx_ready"), sem("cleared"), sem("summed"), sem("chain")
        block = ctx.enter_context(nc.Block())

        @block.gpsimd
        def _(pool):
            last_slot = pool.to_reg(NBLK0 * P - 1)

            def gather(it, u):
                pool.wait_ge(idx_ready, it * U + u + 1)
                for j in range(4):
                    pool.indirect_dma_start(g[:, u, j], None, rows,
                                            bass.IndirectOffsetOnAxis(idx[:, u, 4 * part + j:4 * part + j + 1], 0),
                                            bounds_check=last_slot, oob_is_err=False).then_inc(gathered[u], 16)

            def scatter(it, u):
                pool.wait_ge(summed, it * U + u + 1)
                for j in range(4):
                    pool.indirect_dma_start(next_rows, bass.IndirectOffsetOnAxis(idx[:, u, 4 + j:5 + j], 0),
                                            acc[:, u], None, bounds_check=last_slot, oob_is_err=False)\
                        .then_inc(scattered[u], 16)

            pool.wait_ge(cleared, 1)
            for it in range(NB // U):
                for u in range(U):
                    gather(it, u)
                    if next_rows is not None and u:
                        scatter(it, u - 1)
                if next_rows is not None:
                    scatter(it, U - 1)
            if next_rows is not None:
                for u in range(U):
                    pool.wait_ge(scattered[u], 64 * (NB // U))

        @block.vector
        def _(dve):
            link = Link(dve, chain)
            link.done(dve.memset(g[:], 0.0))
            link.done(dve.memset(acc[:], 0.0))
            dve.memset(idx[:], 0).then_inc(cleared, 1)
            dve.wait_ge(cleared, 1)

            def turn(it, first):
                for u in range(U):
                    if next_rows is not None and not first:
                        dve.wait_ge(scattered[u], 64 * it)
                    dve.tensor_copy(idx[:, u:u + 1], slot[:, bass.ds(it * U + u, 1), :]).then_inc(idx_ready, 1)
                for u in range(U):
                    b = it * U + u
                    wt = weight[0:T, bass.ds(2 * b + part, 1), :]
                    dve.wait_ge(gathered[u], 64 * it + 64)
                    link.done(dve.tensor_scalar(acc[0:T, u], g[0:T, u, 0], wt[:, :, 0], None, ALU.mult))
                    for j in range(1, 4):
                        ins = dve.scalar_tensor_tensor(acc[0:T, u], g[0:T, u, j], wt[:, :, j], acc[0:T, u],
                                                       ALU.mult, ALU.add)
                        if j < 3:
                            link.done(ins)
                    ins.then_inc(summed, 1)
                    if next_rows is None:
                        dve.wait_ge(summed, b + 1)
                        h = resid[0:T, bass.ds(b * D, D)]
                        link.done(dve.tensor_tensor(h, h, acc[0:T, u], ALU.add))

            turn(0, True)
            with dve.Fori(1, NB // U) as it:
                link.loop(it - 1, (4 if next_rows is None else 3) * U)
                turn(it, False)


def causal_attention(nc, wq_d, wk_d, wv_d, wo_d, bo_d, cst, cstb, resid, mean, rstd):
    U = 2
    NH, HD, HG = 12, 16, 3
    with ExitStack() as ctx:
        take = ctx.enter_context(semaphores(nc))
        def sb(name, shape, dt=F32):
            return ctx.enter_context(nc.sbuf_tensor("at_" + name, shape, dt))

        def sem(name):
            return take("at_" + name)

        wq, wk = sb("wq", [DH, 2, HG * P]), sb("wk", [DH, 2, HG * P])
        wv, wo, bo = sb("wv", [DH, 2, D]), sb("wo", [DH, 2, D]), sb("bo", [1, D])
        caus = sb("caus", [P, HG * P], BF16)
        hn, hnt = sb("hn", [P, U, D]), sb("hnt", [DH, U, 2, P])
        qt, kt = sb("qt", [P, U, HG * P]), sb("kt", [P, U, HG * P])
        v1 = sb("v1", [P, U, NH, HD + 1])
        mx, p, pt = sb("mx", [P, U, 4, HG]), sb("p", [P, U, 4, HG, P]), sb("pt", [P, U, HG, 4 * P])
        rec, av = sb("rec", [P, U, NH]), sb("av", [P, U, D])
        avt = sb("avt", [DH, U, 2, P])
        ps = ctx.enter_context(nc.psum_tensor("at_ps", [P, 4 * U, 512], F32))
        w_in, hn_ready, hnt_ps, hnt_ready = sem("w_in"), sem("hn_ready"), sem("hnt_ps"), sem("hnt_ready")
        qkv_ps, q_ready, kv_ready, score_ps = sem("qkv_ps"), sem("q_ready"), sem("kv_ready"), sem("score_ps")
        shifted, exp_ready, pt_ps = sem("shifted"), sem("exp_ready"), sem("pt_ps")
        pt_act, pt_dve, av_ps, av_ready = sem("pt_act"), sem("pt_dve"), sem("av_ps"), sem("av_ready")
        avt_ps, avt_ready, out_ps, chain = sem("avt_ps"), sem("avt_ready"), sem("out_ps"), sem("chain")
        ones_ready = sem("ones_ready")
        block = ctx.enter_context(nc.Block())

        @block.sync
        def _(sp):
            for dst, src in ((wq, wq_d), (wk, wk_d), (wv, wv_d), (wo, wo_d), (bo, bo_d)):
                sp.dma_start(dst[:], src).then_inc(w_in, 16)
            sp.wait_ge(w_in, 5 * 16)

        @block.tensor
        def _(pe):
            ident = cst[:, C_ID:C_ID + P]
            pe.wait_ge(w_in, 5 * 16)
            pe.wait_ge(ones_ready, 2)
            with pe.Fori(0, NB // U) as it:
                for u in range(U):
                    pe.wait_ge(hn_ready, it * U + u + 1)
                    for c in range(2):
                        mm = pe.transpose(ps[0:DH, 4 * u, c * P:(c + 1) * P], hn[:, u, c * DH:(c + 1) * DH], ident)
                    mm.then_inc(hnt_ps, 1)
                for u in range(U):
                    pe.wait_ge(hnt_ready, it * U + u + 1)
                    for n, w in ((1, wq), (2, wk)):
                        for g in range(HG):
                            for c in range(2):
                                pe.matmul(ps[:, 4 * u + n, g * P:(g + 1) * P], w[:, c, g * P:(g + 1) * P],
                                          hnt[:, u, c], start=c == 0, stop=c == 1)
                    for c in range(2):
                        mm = pe.matmul(ps[:, 4 * u + 3, 0:D], hnt[:, u, c], wv[:, c], start=c == 0, stop=c == 1)
                    mm.then_inc(qkv_ps, 1)
                for u in range(U):
                    pe.wait_ge(q_ready, it * U + u + 1)
                    pe.wait_ge(kv_ready, 2 * (it * U + u) + 2)
                    for j in range(4):
                        pe.matmul(ps[:, 4 * u + j, 0:HG * P], cstb[:, 0], caus[:], start=True, stop=False)
                    for g in range(HG):
                        for j in range(4):
                            mm = pe.matmul(ps[:, 4 * u + j, g * P:(g + 1) * P],
                                           qt[32 * j:32 * j + 32, u, g * P:(g + 1) * P],
                                           kt[32 * j:32 * j + 32, u, g * P:(g + 1) * P], start=False, stop=g == HG - 1)
                    mm.then_inc(score_ps, 1)
                for u in range(U):
                    pe.wait_ge(exp_ready, it * U + u + 1)
                    for g in range(HG):
                        for j in range(4):
                            mm = pe.transpose(ps[:, 4 * u + g, j * P:(j + 1) * P], p[:, u, j, g], ident)
                        mm.then_inc(pt_ps, 1)
                for u in range(U):
                    pe.wait_ge(pt_act, 2 * (it * U + u) + 2)
                    pe.wait_ge(pt_dve, it * U + u + 1)
                    for h in range(NH):
                        mm = pe.matmul(ps[:, 4 * u + 3, h * (HD + 1):(h + 1) * (HD + 1)],
                                       pt[:, u, h // 4, (h % 4) * P:(h % 4 + 1) * P], v1[:, u, h], start=True, stop=True)
                    mm.then_inc(av_ps, 1)
                for u in range(U):
                    pe.wait_ge(av_ready, it * U + u + 1)
                    for c in range(2):
                        mm = pe.transpose(ps[0:DH, 4 * u, c * P:(c + 1) * P], av[:, u, c * DH:(c + 1) * DH], ident)
                    mm.then_inc(avt_ps, 1)
                for u in range(U):
                    pe.wait_ge(avt_ready, it * U + u + 1)
                    for c in range(2):
                        pe.matmul(ps[0:T, 4 * u + 1, 0:D], avt[:, u, c, 0:T], wo[:, c], start=c == 0, stop=False)
                    pe.matmul(ps[0:T, 4 * u + 1, 0:D], cst[0:1, C_ONE:C_ONE + T], bo[:], start=False, stop=True)\
                      .then_inc(out_ps, 1)

        @block.scalar
        def _(act):
            with act.Fori(0, NB // U) as it:
                for u in range(U):
                    act.wait_ge(hnt_ps, it * U + u + 1)
                    act.copy(hnt[:, u], ps[0:DH, 4 * u, 0:2 * P].rearrange("p (c t) -> p c t", c=2)).then_inc(hnt_ready, 1)
                for u in range(U):
                    act.wait_ge(qkv_ps, it * U + u + 1)
                    act.copy(qt[:, u], ps[:, 4 * u + 1, 0:HG * P]).then_inc(q_ready, 1)
                for u in range(U):
                    for j in range(4):
                        act.wait_ge(shifted, 4 * (it * U + u) + j + 1)
                        ins = act.activation(p[:, u, j], p[:, u, j], ACT.Exp, scale=HD ** -0.5)
                    ins.then_inc(exp_ready, 1)
                for u in range(U):
                    for g in (0, 2):
                        act.wait_ge(pt_ps, 3 * (it * U + u) + g + 1)
                        act.copy(pt[:, u, g], ps[:, 4 * u + g]).then_inc(pt_act, 1)
                for u in range(U):
                    act.wait_ge(avt_ps, it * U + u + 1)
                    act.copy(avt[:, u], ps[0:DH, 4 * u, 0:2 * P].rearrange("p (c t) -> p c t", c=2)).then_inc(avt_ready, 1)

        @block.vector
        def _(dve):
            link = Link(dve, chain)
            dve.memset(v1[:], 1.0).then_inc(ones_ready, 1)
            dve.tensor_copy(caus[:], cst[:, C_CAUS:C_CAUS + HG * P]).then_inc(ones_ready, 1)
            dve.wait_ge(ones_ready, 2)
            with dve.Fori(0, NB // U) as it:
                link.loop(it, 3 * U)
                for u in range(U):
                    b = it * U + u
                    dve.tensor_scalar(hn[:, u], resid[:, bass.ds(b * D, D)], mean[:, bass.ds(b, 1)],
                                      rstd[:, bass.ds(b, 1)], ALU.subtract, ALU.mult).then_inc(hn_ready, 1)
                for u in range(U):
                    dve.wait_ge(qkv_ps, it * U + u + 1)
                    dve.tensor_copy(kt[:, u], ps[:, 4 * u + 2, 0:HG * P]).then_inc(kv_ready, 1)
                    dve.tensor_copy(v1[:, u, :, 0:HD], ps[:, 4 * u + 3, 0:D].rearrange("p (h d) -> p h d", h=NH))\
                       .then_inc(kv_ready, 1)
                for u in range(U):
                    dve.wait_ge(score_ps, it * U + u + 1)
                    for j in range(4):
                        s = ps[:, 4 * u + j, 0:HG * P].rearrange("p (g k) -> p g k", g=HG)
                        ins = dve.tensor_reduce(mx[:, u, j], s, AX.X, ALU.max)
                    link.done(ins)
                    for j in range(4):
                        s = ps[:, 4 * u + j, 0:HG * P].rearrange("p (g k) -> p g k", g=HG)
                        dve.tensor_tensor(p[:, u, j], s, mx[:, u, j].unsqueeze(2).to_broadcast([P, HG, P]),
                                          ALU.subtract).then_inc(shifted, 1)
                for u in range(U):
                    dve.wait_ge(pt_ps, 3 * (it * U + u) + 2)
                    dve.tensor_copy(pt[:, u, 1], ps[:, 4 * u + 1]).then_inc(pt_dve, 1)
                for u in range(U):
                    dve.wait_ge(av_ps, it * U + u + 1)
                    o = ps[:, 4 * u + 3, 0:NH * (HD + 1)].rearrange("p (h d) -> p h d", h=NH)
                    link.done(dve.reciprocal(rec[:, u], o[:, :, HD]))
                    dve.tensor_tensor(av[:, u].rearrange("p (h d) -> p h d", h=NH), o[:, :, 0:HD],
                                      rec[:, u].unsqueeze(2).to_broadcast([P, NH, HD]), ALU.mult).then_inc(av_ready, 1)
                for u in range(U):
                    b = it * U + u
                    dve.wait_ge(out_ps, it * U + u + 1)
                    h = resid[0:T, bass.ds(b * D, D)]
                    link.done(dve.tensor_tensor(h, h, ps[0:T, 4 * u + 1, 0:D], ALU.add))


def expert_ffn(nc, gate_d, w1_d, b2_d, w2_d, bits_d, cst, cstb, resid, mean, rstd, out):
    with ExitStack() as ctx:
        def sb(name, shape, dt=F32):
            return ctx.enter_context(nc.sbuf_tensor("mo_" + name, shape, dt))

        take = ctx.enter_context(semaphores(nc))
        rows_x = nc.dram_tensor("rows_x", (NB * T + P, D + NX), F32, kind="Internal").ap()
        rows_y = nc.dram_tensor("rows_y", (NB * T + P, D), F32, kind="Internal").ap()
        w1 = sb("w1", [DH + 1, NX * 2 * HID])
        w2 = sb("w2", [P, NX * HC * D])
        b2 = sb("b2", [P, NX * D])
        score = sb("score", [P, NX, NB])
        row_of = sb("row_of", [P, NBLK1], I32)
        block_expert = sb("block_expert", [1, NBLK1], I32)
        weights_in = take("weights_in")
        gate_scores(nc, gate_d, ((w1, w1_d), (w2, w2_d), (b2, b2_d)), weights_in, cst, resid, mean, rstd, score,
                    rows_x, rows_y)
        pick_pairs(nc, bits_d, cst, cstb, score, row_of, block_expert)
        run_experts(nc, cst, w1, w2, b2, weights_in, row_of, block_expert, rows_x, rows_y, out)


def gate_scores(nc, gate_d, weights, weights_in, cst, resid, mean, rstd, score, rows_x, rows_y):
    U = 4
    with ExitStack() as ctx:
        take = ctx.enter_context(semaphores(nc))

        def sb(name, shape, dt=F32):
            return ctx.enter_context(nc.sbuf_tensor("ga_" + name, shape, dt))

        gate = sb("gate", [DH, 2, NX])
        hn, hnt = sb("hn", [P, U, D]), sb("hnt", [DH, U, 2, P])
        logit = sb("logit", [P, NX, NB])
        mx, z, rz = sb("mx", [P, NB]), sb("z", [P, NB]), sb("rz", [P, NB])
        by_token = sb("by_token", [P, NB, NX])
        zeros = sb("zeros", [P, D + NX])
        pa = ctx.enter_context(nc.psum_tensor("ga_pa", [P, U, 512], F32))
        pb = ctx.enter_context(nc.psum_tensor("ga_pb", [P, U, 512], F32))
        w_in, hn_ready, hnt_ps, hnt_ready = take("ga_w_in"), take("ga_hn_ready"), take("ga_hnt_ps"), take("ga_hnt_ready")
        logit_ps, chain, shifted, exp_ready = take("ga_logit_ps"), take("ga_chain"), take("ga_shifted"), take("ga_exp")
        score_ready, cleared, tables = take("ga_score_ready"), take("ga_cleared"), take("ga_tables")
        hn_stored = [take(f"ga_hn_stored{u}") for u in range(U)]
        block = ctx.enter_context(nc.Block())

        @block.sync
        def _(sp):
            sp.dma_start(gate[:], gate_d).then_inc(w_in, 16)
            sp.dma_start(rows_y[0:NB * T].rearrange("(b t) d -> t b d", t=T),
                         resid[0:T, :].rearrange("t (b d) -> t b d", b=NB)).then_inc(tables, 16)
            sp.wait_ge(cleared, 1)
            sp.dma_start(rows_y[NB * T:NB * T + P], zeros[:, 0:D]).then_inc(tables, 16)
            sp.dma_start(rows_x[NB * T:NB * T + P], zeros[:]).then_inc(tables, 16)
            with sp.Fori(0, NB // U) as it:
                for u in range(U):
                    sp.wait_ge(hn_ready, it * U + u + 1)
                    sp.dma_start(rows_x[bass.ds((it * U + u) * T, T), 0:D], hn[0:T, u]).then_inc(hn_stored[u], 16)
            sp.wait_ge(score_ready, 1)
            sp.dma_start(rows_x[0:NB * T, D:D + NX].rearrange("(b t) e -> t b e", t=T), by_token[0:T])\
              .then_inc(tables, 16)
            for dst, src in weights:
                sp.dma_start(dst[:], src).then_inc(weights_in, 16)
            sp.wait_ge(tables, 4 * 16)
            for u in range(U):
                sp.wait_ge(hn_stored[u], 16 * (NB // U + 1))

        @block.tensor
        def _(pe):
            ident = cst[:, C_ID:C_ID + P]
            pe.wait_ge(w_in, 16)
            with pe.Fori(0, NB // U) as it:
                for u in range(U):
                    pe.wait_ge(hn_ready, it * U + u + 1)
                    for c in range(2):
                        mm = pe.transpose(pa[0:DH, u, c * P:(c + 1) * P], hn[:, u, c * DH:(c + 1) * DH], ident)
                    mm.then_inc(hnt_ps, 1)
                for u in range(U):
                    pe.wait_ge(hnt_ready, it * U + u + 1)
                    for c in range(2):
                        mm = pe.matmul(pb[:, u, 0:NX], hnt[:, u, c], gate[:, c], start=c == 0, stop=c == 1)
                    mm.then_inc(logit_ps, 1)

        @block.scalar
        def _(act):
            with act.Fori(0, NB // U) as it:
                for u in range(U):
                    act.wait_ge(hnt_ps, it * U + u + 1)
                    act.copy(hnt[:, u], pa[0:DH, u, 0:2 * P].rearrange("p (c t) -> p c t", c=2)).then_inc(hnt_ready, 1)
            act.wait_ge(shifted, 1)
            act.activation(logit[:], logit[:], ACT.Exp).then_inc(exp_ready, 1)

        @block.vector
        def _(dve):
            link = Link(dve, chain)
            dve.memset(zeros[:], 0.0).then_inc(cleared, 1)
            for u in range(U):
                dve.memset(hn[:, u], 0.0).then_inc(hn_stored[u], 16)
            with dve.Fori(0, NB // U) as it:
                link.loop(it, U)
                for u in range(U):
                    b = it * U + u
                    dve.wait_ge(hn_stored[u], 16 * it + 16)
                    dve.tensor_scalar(hn[:, u], resid[:, bass.ds(b * D, D)], mean[:, bass.ds(b, 1)],
                                      rstd[:, bass.ds(b, 1)], ALU.subtract, ALU.mult).then_inc(hn_ready, 1)
                for u in range(U):
                    b = it * U + u
                    dve.wait_ge(logit_ps, it * U + u + 1)
                    link.done(dve.tensor_copy(logit[:, :, bass.ds(b, 1)], pb[:, u, 0:NX].unsqueeze(2)))
            link.end(NB // U)
            by_e = "p e b -> p b e"
            link.done(dve.tensor_reduce(mx[:], logit[:].rearrange(by_e), AX.X, ALU.max))
            dve.tensor_tensor(logit[:], logit[:], mx[:].unsqueeze(1).to_broadcast([P, NX, NB]), ALU.subtract)\
               .then_inc(shifted, 1)
            dve.wait_ge(exp_ready, 1)
            link.done(dve.tensor_reduce(z[:], logit[:].rearrange(by_e), AX.X, ALU.add))
            link.done(dve.reciprocal(rz[:], z[:]))
            link.done(dve.tensor_tensor(score[:], logit[:], rz[:].unsqueeze(1).to_broadcast([P, NX, NB]), ALU.mult))
            dve.tensor_copy(by_token[:], score[:].rearrange(by_e)).then_inc(score_ready, 1)
            dve.wait_ge(score_ready, 1)
            link.done(dve.tensor_scalar(score[:], score[:], cst[:, C_VALID:C_VALID + 1], cst[:, C_VM1:C_VM1 + 1],
                                        ALU.mult, ALU.add))


def pick_pairs(nc, bits_d, cst, cstb, score, row_of, block_expert):
    NC = NX * NB
    BITS = 30
    W = 8
    with ExitStack() as ctx:
        take = ctx.enter_context(semaphores(nc))

        def sb(name, shape, dt=F32):
            return ctx.enter_context(nc.sbuf_tensor("pk_" + name, shape, dt))

        bits = sb("bits", [P, BITS], I32)
        found, cand = sb("found", [P, 1], I32), sb("cand", [P, 1], I32)
        hits, cnt, enough = sb("hits", [P, NC]), sb("cnt", [P, 1]), sb("enough", [P, 1])
        above, tie = sb("above", [P, NC]), sb("tie", [P, NC])
        mask_b = sb("mask_b", [P, 2, NC], BF16)
        ones = sb("ones", [P, NC])
        incl, rank, left, kept = sb("incl", [P, NC]), sb("rank", [P, NC]), sb("left", [P, 1]), sb("kept", [P, NC])
        cntx, inclx, startx = sb("cntx", [P, NX]), sb("inclx", [P, NX]), sb("startx", [P, NX])
        ceil_i, blk_i, blk = sb("ceil_i", [P, NX], I32), sb("blk_i", [P, NX], I32), sb("blk", [P, NX])
        iblk, shift = sb("iblk", [P, NX]), sb("shift", [P, NX])
        slot, slot_i, q_i, p_i = sb("slot", [P, NC]), sb("slot_i", [P, NC], I32), sb("q_i", [P, NC], I32), sb("p_i", [P, NC], I32)
        qf, pf = sb("qf", [P, NC]), sb("pf", [P, NC])
        row1 = sb("row1", [P, NC])
        past, nblk = sb("past", [1, NBLK1, NX]), sb("nblk", [1, NBLK1])
        hot_p, hot_q = sb("hot_p", [P, W, P]), sb("hot_q", [P, W, NBLK1])
        listed, empty = sb("listed", [P, NBLK1]), sb("empty", [P, NBLK1])
        ps = ctx.enter_context(nc.psum_tensor("pk_ps", [P, 4, 512], F32))
        bits_in, chain, counted, total_ps = take("pk_bits_in"), take("pk_chain"), take("pk_counted"), take("pk_total_ps")
        mask_ready, prefix_ps, hot_ready, used = take("pk_mask_ready"), take("pk_prefix_ps"), take("pk_hot"), take("pk_used")
        listed_ps = take("pk_listed_ps")
        block = ctx.enter_context(nc.Block())
        dummy = cst[:, C_DUMMY:C_DUMMY + 1]

        @block.sync
        def _(sp):
            sp.dma_start(bits[:], bits_d).then_inc(bits_in, 16)
            sp.wait_ge(bits_in, 16)

        @block.tensor
        def _(pe):
            with pe.Fori(0, BITS) as i:
                pe.wait_ge(counted, i + 1)
                pe.matmul(ps[:, 0, 0:1], cst[:, C_ONE:C_ONE + P], cnt[:], start=True, stop=True).then_inc(total_ps, 1)
            pe.wait_ge(counted, BITS + 1)
            pe.matmul(ps[:, 0, 0:1], cst[:, C_ONE:C_ONE + P], cnt[:], start=True, stop=True).then_inc(total_ps, 1)
            for n in range(2):
                pe.wait_ge(mask_ready, n + 1)
                pe.matmul(ps[:, 1, 0:NC], cstb[:, 1], mask_b[:, n], start=True, stop=True)
                pe.matmul(ps[:, 2, 0:NC], cstb[:, 3], mask_b[:, n], start=True, stop=True).then_inc(prefix_ps, 1)

            def column(it, w, first, last):
                pe.wait_ge(hot_ready, 2 * (it * W + w) + 2)
                pe.matmul(ps[:, 3, 0:NBLK1], hot_p[:, w], hot_q[:, w], start=first, stop=last).then_inc(used, 1)

            for w in range(W):
                column(0, w, w == 0, False)
            with pe.Fori(1, NC // W - 1) as it:
                for w in range(W):
                    column(it, w, False, False)
            for w in range(W):
                column(NC // W - 1, w, False, w == W - 1)

        @block.vector
        def _(dve):
            link = Link(dve, chain)
            s = score[:].rearrange("p e b -> p (e b)")
            by_e = "p (e b) -> p e b"
            dve.memset(ones[:], 1.0)
            link.done(dve.memset(found[:], 0))
            dve.wait_ge(bits_in, 16)
            with dve.Fori(0, BITS) as i:
                link.loop(i, 3)
                link.done(dve.tensor_tensor(cand[:], found[:], bits[:, bass.ds(i, 1)], ALU.bitwise_or))
                dve.tensor_scalar(hits[:], s, cand[:].bitcast(F32), None, ALU.is_ge, ALU.add, accum_out=cnt[:])\
                   .then_inc(counted, 1)
                dve.wait_ge(total_ps, i + 1)
                link.done(dve.tensor_scalar(enough[:], ps[:, 0, 0:1], float(K1), None, ALU.is_ge))
                link.done(dve.scalar_tensor_tensor(found[:].bitcast(F32), cand[:].bitcast(F32), enough[:],
                                                   found[:].bitcast(F32), ALU.mult, ALU.max))
            link.end(BITS)
            kth = found[:].bitcast(F32)
            dve.tensor_scalar(above[:], s, kth, None, ALU.is_gt, ALU.add, accum_out=cnt[:]).then_inc(counted, 1)
            link.done(dve.tensor_scalar(tie[:], s, kth, None, ALU.is_equal))
            dve.tensor_copy(mask_b[:, 0], tie[:]).then_inc(mask_ready, 1)
            dve.wait_ge(total_ps, BITS + 1)
            link.done(dve.tensor_scalar(left[:], ps[:, 0, 0:1], -1.0, float(K1), ALU.mult, ALU.add))

            def prefix(n):
                dve.wait_ge(prefix_ps, n + 1)
                link.done(dve.tensor_tensor_scan(incl[:], ones[:], ps[:, 1, 0:NC], 0.0, ALU.mult, ALU.add))
                link.done(dve.tensor_tensor(rank[:], incl[:], ps[:, 1, 0:NC], ALU.subtract))
                link.done(dve.tensor_tensor(rank[:], rank[:], ps[:, 2, 0:NC], ALU.add))

            prefix(0)
            link.done(dve.scalar_tensor_tensor(kept[:], rank[:], left[:], tie[:], ALU.is_lt, ALU.mult))
            link.done(dve.tensor_tensor(kept[:], kept[:], above[:], ALU.add))
            dve.tensor_copy(mask_b[:, 1], kept[:]).then_inc(mask_ready, 1)
            prefix(1)
            link.done(dve.tensor_reduce(cntx[:], ps[:, 1, 0:NC].rearrange(by_e, e=NX), AX.X, ALU.add))
            link.done(dve.tensor_tensor_scan(inclx[:], ones[:, 0:NX], cntx[:], 0.0, ALU.mult, ALU.add))
            link.done(dve.tensor_tensor(startx[:], inclx[:], cntx[:], ALU.subtract))
            link.done(dve.tensor_scalar(ceil_i[:], cntx[:], P - 1.0, None, ALU.add))
            link.done(dve.tensor_scalar(blk_i[:], ceil_i[:], 7, None, ALU.arith_shift_right))
            link.done(dve.tensor_copy(blk[:], blk_i[:]))
            link.done(dve.tensor_tensor_scan(iblk[:], ones[:, 0:NX], blk[:], 0.0, ALU.mult, ALU.add))
            link.done(dve.tensor_tensor(shift[:], iblk[:], blk[:], ALU.subtract))
            link.done(dve.scalar_tensor_tensor(shift[:], shift[:], float(P), startx[:], ALU.mult, ALU.subtract))
            link.done(dve.tensor_tensor(slot[:].rearrange(by_e, e=NX), rank[:].rearrange(by_e, e=NX),
                                        shift[:].unsqueeze(2).to_broadcast([P, NX, NB]), ALU.add))
            link.done(dve.scalar_tensor_tensor(slot[:], slot[:], 1.0, kept[:], ALU.add, ALU.mult))
            link.done(dve.tensor_scalar(slot_i[:], slot[:], -1.0, None, ALU.add))
            link.done(dve.tensor_scalar(q_i[:], slot_i[:], 7, None, ALU.arith_shift_right))
            link.done(dve.tensor_scalar(p_i[:], slot_i[:], P - 1, None, ALU.bitwise_and))
            link.done(dve.tensor_copy(qf[:], q_i[:]))
            link.done(dve.tensor_copy(pf[:], p_i[:]))
            link.done(dve.tensor_scalar(row1[:].rearrange(by_e, e=NX),
                                        cst[:, C_IOTA:C_IOTA + NB].unsqueeze(1).to_broadcast([P, NX, NB]),
                                        float(T), cst[:, C_ROW1:C_ROW1 + 1], ALU.mult, ALU.add))
            link.done(dve.tensor_tensor(past[:], cst[0:1, C_IOTA:C_IOTA + NBLK1].unsqueeze(2).to_broadcast([1, NBLK1, NX]),
                                        iblk[0:1, :].unsqueeze(1).to_broadcast([1, NBLK1, NX]), ALU.is_ge))
            link.done(dve.tensor_reduce(nblk[:], past[:], AX.X, ALU.add))
            link.done(dve.tensor_scalar(block_expert[:], nblk[:], NX - 1.0, None, ALU.min))

            def column(it, w, first):
                k = it * W + w
                if not first:
                    dve.wait_ge(used, k - W + 1)
                dve.tensor_scalar(hot_p[:, w], cst[:, C_IOTA:C_IOTA + P], pf[:, bass.ds(k, 1)], None, ALU.is_equal)\
                   .then_inc(hot_ready, 1)
                dve.tensor_scalar(hot_q[:, w], cst[:, C_IOTA:C_IOTA + NBLK1], qf[:, bass.ds(k, 1)],
                                  row1[:, bass.ds(k, 1)], ALU.is_equal, ALU.mult).then_inc(hot_ready, 1)

            for w in range(W):
                column(0, w, True)
            with dve.Fori(1, NC // W) as it:
                for w in range(W):
                    column(it, w, False)
            dve.wait_ge(used, NC)
            link.done(dve.tensor_scalar(empty[:], ps[:, 3, 0:NBLK1], 0.0, dummy, ALU.is_equal, ALU.mult))
            link.done(dve.scalar_tensor_tensor(row_of[:], ps[:, 3, 0:NBLK1], -1.0, empty[:], ALU.add, ALU.add))


def run_experts(nc, cst, w1, w2, b2, weights_in, row_of, block_expert, rows_x, rows_y, out):
    W = 4
    TURNS = NBLK1 // W
    HH = HID // 2
    with ExitStack() as ctx:
        take = ctx.enter_context(semaphores(nc))

        def sb(name, shape, dt=F32):
            return ctx.enter_context(nc.sbuf_tensor("ex_" + name, shape, dt))

        x = sb("x", [P, W, D + NX])
        xt = sb("xt", [DH + 1, 2, 2, P])
        h = sb("h", [P, 2, HID])
        ht = sb("ht", [P, 2, HID])
        yb = sb("yb", [P, W, D])
        y = sb("y", [P, W, D])
        xt_ps = ctx.enter_context(nc.psum_tensor("ex_xt_ps", [P, 1, 512], F32))
        h_ps = ctx.enter_context(nc.psum_tensor("ex_h_ps", [P, 4, 512], F32))
        ht_ps = ctx.enter_context(nc.psum_tensor("ex_ht_ps", [P, 2, 512], F32))
        y_ps = ctx.enter_context(nc.psum_tensor("ex_y_ps", [P, 1, 512], F32))
        x_t, xt_ready, h_done, gelu_ready = take("ex_x_t"), take("ex_xt_ready"), take("ex_h_done"), take("ex_gelu")
        h_t, ht_act, ht_dve, y_done = take("ex_h_t"), take("ex_ht_act"), take("ex_ht_dve"), take("ex_y_done")
        y_read, y_ready, ones_ready, stored = take("ex_y_read"), take("ex_y_ready"), take("ex_ones"), take("ex_stored")
        gathered = [take(f"ex_gathered{u}") for u in range(W)]
        added = [take(f"ex_added{u}") for u in range(W)]
        block = ctx.enter_context(nc.Block())

        @block.gpsimd
        def _(pool):
            last = pool.to_reg(NB * T + P - 1)

            def gather(t):
                if t >= W:
                    pool.wait_ge(y_ready, t - W + 1)
                pool.indirect_dma_start(x[:, t % W], None, rows_x, bass.IndirectOffsetOnAxis(row_of[:, t:t + 1], 0),
                                        bounds_check=last, oob_is_err=True).then_inc(gathered[t % W], 16)

            for t in range(W - 1):
                gather(t)
            for t in range(NBLK1):
                if t + W - 1 < NBLK1:
                    gather(t + W - 1)
                pool.wait_ge(y_ready, t + 1)
                if t:
                    pool.wait_ge(added[(t - 1) % W], 16 * ((t - 1) // W + 1))
                pool.indirect_dma_start(rows_y, bass.IndirectOffsetOnAxis(row_of[:, t:t + 1], 0), y[:, t % W], None,
                                        bounds_check=last, oob_is_err=True, compute_op=ALU.add)\
                    .then_inc(added[t % W], 16)
            for u in range(W):
                pool.wait_ge(added[u], 16 * TURNS)
            pool.dma_start(out.rearrange("b t d -> (b t) d"), rows_y[0:NB * T]).then_inc(stored, 16)
            pool.wait_ge(stored, 16)

        @block.tensor
        def _(pe):
            ident = cst[:, C_ID:C_ID + P]
            pe.wait_ge(weights_in, 3 * 16)
            pe.wait_ge(ones_ready, 1)

            def expert(t):
                return pe.value_load(block_expert[0:1, bass.ds(t, 1)], min_val=0, max_val=NX - 1)

            def hidden(it, u):
                t = it * W + u
                e = expert(t)
                pe.wait_ge(gathered[u], 16 * it + 16)
                for c in range(2):
                    mm = pe.transpose(xt_ps[0:DH, 0, c * P:(c + 1) * P], x[:, u, c * DH:(c + 1) * DH], ident)
                mm.then_inc(x_t, 1)
                pe.wait_ge(xt_ready, t + 1)
                for n in range(2):
                    for c in range(2):
                        k = DH + c
                        mm = pe.matmul(h_ps[:, 2 * (u % 2) + n, 0:HH], xt[0:k, u % 2, c],
                                       w1[0:k, bass.ds(e * (2 * HID) + c * HID + n * HH, HH)],
                                       start=c == 0, stop=c == 1)
                    mm.then_inc(h_done, 1)

            def output(it, u):
                t = it * W + u
                e = expert(t)
                for n in range(2):
                    pe.wait_ge(gelu_ready, 2 * t + n + 1)
                    for k in range(3):
                        mm = pe.transpose(ht_ps[:, n, k * P:(k + 1) * P],
                                          h[:, u % 2, n * HH + k * P:n * HH + (k + 1) * P], ident)
                    mm.then_inc(h_t, 1)
                pe.wait_ge(y_read, t + 1)
                pe.wait_ge(ht_act, t + 1)
                pe.wait_ge(ht_dve, t + 1)
                for k in range(HC):
                    mm = pe.matmul(y_ps[:, 0, 0:D], ht[:, u % 2, k * P:(k + 1) * P],
                                   w2[:, bass.ds(e * (HC * D) + k * D, D)], start=k == 0, stop=k == HC - 1)
                mm.then_inc(y_done, 1)

            hidden(0, 0)
            with pe.Fori(0, TURNS - 1) as it:
                for u in range(W):
                    hidden(it + (u + 1) // W, (u + 1) % W)
                    output(it, u)
            for u in range(W):
                if u + 1 < W:
                    hidden(TURNS - 1, u + 1)
                output(TURNS - 1, u)

        @block.scalar
        def _(act):
            def hidden(it, u):
                t = it * W + u
                act.wait_ge(x_t, t + 1)
                act.copy(xt[0:DH, u % 2], xt_ps[0:DH, 0, 0:2 * P].rearrange("p (c t) -> p c t", c=2)).then_inc(xt_ready, 1)
                for n in range(2):
                    act.wait_ge(h_done, 2 * t + n + 1)
                    act.activation(h[:, u % 2, n * HH:(n + 1) * HH], h_ps[:, 2 * (u % 2) + n, 0:HH],
                                   ACT.Gelu_apprx_tanh).then_inc(gelu_ready, 1)

            def output(it, u):
                t = it * W + u
                act.wait_ge(h_t, 2 * t + 1)
                act.copy(ht[:, u % 2, 0:HH], ht_ps[:, 0, 0:HH]).then_inc(ht_act, 1)

            act.wait_ge(ones_ready, 1)
            hidden(0, 0)
            with act.Fori(0, TURNS - 1) as it:
                for u in range(W):
                    hidden(it + (u + 1) // W, (u + 1) % W)
                    output(it, u)
            for u in range(W):
                if u + 1 < W:
                    hidden(TURNS - 1, u + 1)
                output(TURNS - 1, u)

        @block.vector
        def _(dve):
            dve.memset(xt[DH:DH + 1], 1.0).then_inc(ones_ready, 1)
            dve.memset(yb[0:1, 0, 0:1], 0.0).then_inc(y_read, 1)
            dve.wait_ge(weights_in, 3 * 16)

            def turn(it, first):
                for u in range(W):
                    t = it * W + u
                    e = dve.value_load(block_expert[0:1, bass.ds(t, 1)], min_val=0, max_val=NX - 1)
                    dve.wait_ge(h_t, 2 * t + 2)
                    dve.tensor_copy(ht[:, u % 2, HH:HID], ht_ps[:, 1, 0:HH]).then_inc(ht_dve, 1)
                    dve.wait_ge(y_done, t + 1)
                    dve.tensor_tensor(yb[:, u], y_ps[:, 0, 0:D], b2[:, bass.ds(e * D, D)], ALU.add).then_inc(y_read, 1)
                    dve.wait_ge(y_read, t + 2)
                    if not first:
                        dve.wait_ge(added[u], 16 * it)
                    dve.tensor_scalar(y[:, u], yb[:, u], x[:, u, bass.ds(e + D, 1)], None, ALU.mult)\
                       .then_inc(y_ready, 1)

            turn(0, True)
            with dve.Fori(1, TURNS) as it:
                turn(it, False)


def _consts():
    c = np.zeros((P, C_END), np.float32)
    i = np.arange(P)
    c[:, C_ID:C_ID + P] = np.eye(P)
    c[:, C_ONE:C_ONE + P] = 1
    c[:, C_TRS:C_TRS + P] = i[:, None] < i[None, :]
    c[:, C_TRI:C_TRI + P] = i[:, None] <= i[None, :]
    c[:, C_IOTA:C_IOTA + 256] = np.arange(256)
    c[:, C_CAUS:C_CAUS + 3 * P] = np.tile(np.where(i[None, :] > i[:, None], NEG, 0), (1, 3))
    c[:DH, C_BLKM:C_BLKM + DH] = np.where(i[:DH, None] // 24 == i[None, :DH] // 24, 0, NEG)
    m = np.zeros((2, 16, 2, 16))
    m += 1
    m.reshape(32, 32)[8:24, 8:24] = 2
    for a in range(2):
        for b in range(2):
            for ch in range(NCH):
                y = 8 * (ch % 2)
                c[:, C_MULT + (2 * a + b) * NCH + ch] = m[a, y:y + 8, b].reshape(P)
    c[:, C_EPS] = LN_EPS
    c[:, C_VALID] = i < T
    c[:, C_FAR] = np.where(i < T, 0, FAR)
    c[:, C_SENT:C_SENT + 4] = [-1, -2, -3, -4]
    c[:, C_NHALF] = -0.5
    c[:, C_VM1] = c[:, C_VALID] - 1
    c[:, C_DUMMY] = NB * T + i + 1
    c[:, C_ROW1] = i + 1
    return c


def _blocks(w):
    w = w.reshape(2, 2, 8, 2, 16, 3, -1)
    return np.ascontiguousarray(w.transpose(2, 4, 0, 3, 5, 1, 6).reshape(P, NK, -1))


def _windows(w):
    w = w.reshape(16, 16, 5, 3, -1)
    shifted = np.zeros((2, 16, 2, 16, 3, w.shape[-1]), w.dtype)
    for part, (a, b) in ((1, (0, 0)), (2, (1, 1)), (3, (0, 1)), (4, (1, 0))):
        shifted[a, :, b] = w[:, :, part]
    base = np.zeros((32, 32, 3, w.shape[-1]), w.dtype)
    base[8:24, 8:24] = w[:, :, 0]
    return _blocks(shifted), _blocks(base)


def kernel(**inputs):
    import concourse.bacc as bacc
    from concourse.bass_utils import run_bass_kernel_spmd as run

    a = {k: np.asarray(v) for k, v in inputs.items()}
    x = np.zeros((NGRP * GRP, 3, 112, 112), np.float32)
    x[:NB, :, 8:104, 8:104] = a["x"]
    x = x.reshape(NGRP, GRP, 3, BLK, 2, 8, BLK, 16).transpose(0, 5, 7, 2, 4, 1, 3, 6)
    feed = {"x_blocks": x.reshape(NGRP, P, NCH * GRP, BLK * BLK), "txt": a["txt"], "consts": _consts()}
    feed["w_shift"], feed["w_base"] = _windows(a["L0_tok_W"].T)
    for name, key in (("g", "L0_tok_ln_gamma"), ("b", "L0_tok_ln_beta")):
        s, b = _windows(a[key][:, None])
        feed[name + "_shift"], feed[name + "_base"] = s[:, :, 0], b[:, :, 0]
    feed["tok_b"] = a["L0_tok_b"][None]
    half = lambda w: w.reshape(2, DH, -1).transpose(1, 0, 2)
    w = a["L0_attn_W_qkv"]
    feed["wqk"] = half(np.concatenate([w[:, 0::3], w[:, 1::3]], 1))
    feed["wv"] = half(w[:, 2::3])
    feed["wp"] = half(a["L0_attn_W_proj"])
    feed["bp"] = a["L0_attn_b_proj"][None]
    feed["temp"] = np.broadcast_to(a["L0_attn_temp"].reshape(2, 4, 1), (2, 4, 24)).reshape(2, DH).T
    feed["emb"] = np.stack([a["L0_ffn_emb_fk"], a["L0_ffn_emb_rk"]], 1)
    feed["wcat"] = half(np.concatenate([a["L0_ffn_W_fk"], a["L0_ffn_W_rk"]], 1))
    feed["bcat"] = np.concatenate([a["L0_ffn_b_fk"], a["L0_ffn_b_rk"]])[:, None]
    feed["f_know"], feed["r_know"] = a["L0_ffn_f_know"], a["L0_ffn_r_know"]
    for name, key in (("wq1", "L1_attn_w_query"), ("wk1", "L1_attn_w_key")):
        w = np.zeros((D, 12, 32), np.float32)
        w[:, :, :16] = a[key].reshape(D, 12, 16)
        feed[name] = half(w.reshape(D, 3 * P))
    feed["wv1"], feed["wo1"], feed["bo1"] = half(a["L1_attn_w_value"]), half(a["L1_attn_w_out"]), a["L1_attn_b_out"][None]
    feed["gate_w"] = half(a["L1_ffn_gate_weight"].T)
    w1 = np.zeros((DH + 1, NX, 2, HID), np.float32)
    w1[:DH] = a["L1_ffn_w1"].reshape(NX, 2, DH, HID).transpose(2, 0, 1, 3)
    w1[DH, :, 1] = a["L1_ffn_b1"]
    feed["w1"] = w1.reshape(DH + 1, -1)
    feed["w2"] = a["L1_ffn_w2"].reshape(NX, HC, P, D).transpose(2, 0, 1, 3).reshape(P, -1)
    feed["b2"] = np.broadcast_to(a["L1_ffn_b2"].reshape(1, -1), (P, NX * D))
    feed["bits"] = np.broadcast_to(np.int32(1) << np.arange(29, -1, -1, dtype=np.int32), (P, 30))
    nc = bacc.Bacc("TRN2", target_bir_lowering=False, num_devices=1)
    feed = {k: np.ascontiguousarray(v) for k, v in feed.items()}
    aps = {k: nc.dram_tensor("in_" + k, v.shape, mybir.dt.from_np(v.dtype), kind="ExternalInput").ap()
           for k, v in feed.items()}
    out = nc.dram_tensor("out", (NB, T, D), F32, kind="ExternalOutput").ap()
    program(nc, **aps, out=out)
    r = run(nc, [{"in_" + k: v for k, v in feed.items()}], core_ids=[0])
    return r.results[0]["out"]
```

```python
from contextlib import ExitStack, contextmanager
import numpy as np
import concourse.bass as bass
from concourse import mybir

F32 = mybir.dt.float32
BF16 = mybir.dt.bfloat16
I32 = mybir.dt.int32
U32 = mybir.dt.uint32
ALU = mybir.AluOpType
ACT = mybir.ActivationFunctionType
AX = mybir.AxisListType

P = 128
NB = 32
TI, TT = 36, 77
T = TI + TT
D = 192
DH = D // 2
LN_EPS = 1e-5
NEG = -1e30

BLK = 7
NCH = 6
NK = 4 * NCH
PATCH_DIM = 3840
GRP = 3
GM = GRP * TI
NGRP = 11

NE, TOPK = 128, 4
R = 128
NBLK0 = (NB * T * TOPK + NE * (P - 1)) // P
GROUP = 4
KPARTS = 8

NX, HID = 8, 768
HC = HID // P
K1 = 2 * NB * T
NBLK1 = (K1 + NX * (P - 1)) // P
FAR = 1 << 20

C_ID, C_ONE, C_TRS, C_TRI, C_IOTA, C_CAUS, C_BLKM, C_MULT, C_EPS, C_VALID, C_FAR, C_SENT, C_NHALF, C_VM1, C_DUMMY, C_ROW1, C_END = np.cumsum(
    [0, P, P, P, P, 256, 3 * P, DH, NK, 1, 1, 1, 4, 1, 1, 1, 1]).tolist()


@contextmanager
def semaphores(nc):
    taken = []

    def take(name):
        taken.append(nc.alloc_semaphore(name))
        return taken[-1]

    yield take
    nc.clear_and_free_semaphores(taken)
    nc.all_engine_barrier()


class Link:

    def __init__(self, eng, sem):
        self.eng, self.sem, self.base, self.n = eng, sem, 0, 0

    def done(self, ins):
        self.n += 1
        ins.then_inc(self.sem, 1)
        self.eng.wait_ge(self.sem, self.base + self.n)

    def loop(self, it, per):
        self.start, self.per, self.n, self.base = self.base + self.n, per, 0, self.base + self.n + it * per

    def end(self, turns):
        assert self.n == self.per, (self.n, self.per)
        self.base, self.n = self.start + turns * self.per, 0


def program(nc, x_blocks, txt, w_shift, w_base, g_shift, g_base, b_shift, b_base, tok_b,
            wqk, wv, wp, bp, temp, emb, wcat, bcat, f_know, r_know, wq1, wk1, wv1, wo1, bo1, gate_w, w1, b2, w2, bits, consts, out):
    with ExitStack() as top:
        resid = top.enter_context(nc.sbuf_tensor("resid", [P, NB * D], F32))
        cst = top.enter_context(nc.sbuf_tensor("cst", [P, C_END], F32))
        mean = top.enter_context(nc.sbuf_tensor("mean", [P, NB], F32))
        rstd = top.enter_context(nc.sbuf_tensor("rstd", [P, NB], F32))
        tok_rows = nc.dram_tensor("tok_rows", (NGRP * GRP * TI, D), F32, kind="Internal").ap()
        cstb = top.enter_context(nc.sbuf_tensor("cstb", [P, 4, P], BF16))
        slot_mem = nc.dram_tensor("slot_mem", (NBLK0 * P * D,), F32, kind="Internal").ap()
        embed_patches(nc, x_blocks, txt, w_shift, w_base, g_shift, g_base, b_shift, b_base, tok_b, consts,
                      cst, cstb, resid, tok_rows, slot_mem)
        layer_norm_stats(nc, "ln0", resid, cst, mean, rstd)
        channel_attention(nc, wqk, wv, wp, bp, temp, cst, resid, mean, rstd)
        layer_norm_stats(nc, "ln1", resid, cst, mean, rstd)
        sparse_ffn(nc, emb, wcat, bcat, f_know, r_know, cst, cstb, resid, mean, rstd, slot_mem)
        layer_norm_stats(nc, "ln2", resid, cst, mean, rstd)
        causal_attention(nc, wq1, wk1, wv1, wo1, bo1, cst, cstb, resid, mean, rstd)
        layer_norm_stats(nc, "ln3", resid, cst, mean, rstd)
        expert_ffn(nc, gate_w, w1, b2, w2, bits, cst, cstb, resid, mean, rstd, out)


def sparse_ffn(nc, emb, wcat, bcat, f_know, r_know, cst, cstb, resid, mean, rstd, slot_mem):
    with ExitStack() as ctx:
        def sb(name, shape, dt=F32):
            return ctx.enter_context(nc.sbuf_tensor("sf_" + name, shape, dt))

        take = ctx.enter_context(semaphores(nc))
        know = sb("know", [P, NE * 2 * R])
        embt = sb("embt", [P, 2 * NE])
        weight, index = sb("weight", [P, 2 * NB, 4]), sb("index", [P, 2 * NB, 4])
        slot = sb("slot", [P, NB, 8], I32)
        block_expert = sb("block_expert", [1, 2, 256], I32)
        know_in = [take("f_know_in"), take("r_know_in")]
        n = NBLK0 * P
        wide_rows = slot_mem.rearrange("(s d) -> s d", d=D)
        narrow_rows = slot_mem[0:n * R].rearrange("(s d) -> s d", d=R)
        feature_rows = nc.dram_tensor("feature_rows", (n, R), F32, kind="Internal").ap()
        restore_rows = nc.dram_tensor("restore_rows", (n, D), F32, kind="Internal").ap()
        with ExitStack() as routing:
            chosen = routing.enter_context(nc.sbuf_tensor("sf_chosen", [P, 2 * NB, NE], BF16))
            seg_start = routing.enter_context(nc.sbuf_tensor("sf_seg_start", [P, 2, P], BF16))
            route_tokens(nc, emb, wcat, bcat, cst, resid, mean, rstd, embt, chosen, weight, index)
            block_tables(nc, cst, cstb, chosen, seg_start, block_expert)
            place_tokens(nc, cst, cstb, resid, mean, rstd, chosen, index, seg_start, slot, wide_rows,
                         know, f_know, know_in[0])
        blocks_product(nc, "feature", cst, block_expert, 0, wide_rows, know, know_in[0], feature_rows, D, R)
        combine_rows(nc, "mid", cst, slot, weight, 0, feature_rows, R, resid, narrow_rows, know, r_know, know_in[1])
        blocks_product(nc, "restore", cst, block_expert, 1, narrow_rows, know, know_in[1], restore_rows, R, D)
        combine_rows(nc, "end", cst, slot, weight, 1, restore_rows, D, resid, None)


def embed_patches(nc, x_blocks, txt, w_shift, w_base, g_shift, g_base, b_shift, b_base, tok_b, consts,
                  cst, cstb, resid, tok_rows, slot_mem):
    with ExitStack() as ctx:
        take = ctx.enter_context(semaphores(nc))
        def sb(name, shape, dt=F32):
            return ctx.enter_context(nc.sbuf_tensor(name, shape, dt))

        def sem(name):
            return take(name)

        ws = sb("ws", [P, NK, D])
        wb = sb("wb", [P, NK, D])
        weff = sb("weff", [P, NK, D + 1])
        gain = sb("gain", [P, 4, NK])
        bias = sb("bias", [1, D])
        xg = sb("xg", [P, 2, NCH * GRP, BLK * BLK])
        xw = sb("xw", [P, 2, NK, GRP * TI])
        xsq = sb("xsq", [P, 2, NK, GRP * TI])
        colsum = sb("colsum", [P, D])
        shift = sb("shift", [P, D])
        ZN = 2 * D * 8
        zrow = sb("zrow", [P, ZN])
        st = sb("st", [P, 2, 8])
        tok = sb("tok", [P, 2, D])
        rows = sb("rows", [P, 2, D])
        y_ps = ctx.enter_context(nc.psum_tensor("y_ps", [P, 2, 512], F32))
        q_ps = ctx.enter_context(nc.psum_tensor("q_ps", [P, 2, 512], F32))
        c_ps = ctx.enter_context(nc.psum_tensor("c_ps", [P, 2, 512], F32))
        w_in, cst_in, txt_in, zeroed = sem("w_in"), sem("cst_in"), sem("txt_in"), sem("zeroed")
        x_in = [sem("x_in0"), sem("x_in1")]
        weff_ready, sums_ready, sums_out, products_done = (
            sem("weff_ready"), sem("sums_ready"), sem("sums_out"), sem("products_done"))
        windows_ready, squared, var_ready, rstd_ready = sem("windows_ready"), sem("squared"), sem("var_ready"), sem("rstd_ready")
        tok_ready, tok_in, chain = sem("tok_ready"), sem("tok_in"), sem("chain")
        slots_clear = sem("slots_clear")
        rows_stored = [sem("rows_stored0"), sem("rows_stored1")]
        eps_added, y_used = sem("eps_added"), sem("y_used")
        block = ctx.enter_context(nc.Block())

        @block.sync
        def _(sp):
            sp.dma_start(cst[:], consts).then_inc(cst_in, 16)
            for n, g in enumerate((g_shift, g_base, b_shift, b_base)):
                sp.dma_start(gain[:, n, :], g).then_inc(w_in, 16)
            sp.dma_start(bias[:], tok_b).then_inc(w_in, 16)
            sp.dma_start(ws[:], w_shift).then_inc(w_in, 16)
            sp.dma_start(wb[:], w_base).then_inc(w_in, 16)
            for u in range(2):
                sp.dma_start(xg[:, u], x_blocks[u]).then_inc(x_in[u], 16)

            def more(it, u):
                sp.wait_ge(windows_ready, 2 * it + u + 1)
                sp.wait_ge(squared, 2 * it + u + 1)
                sp.dma_start(xg[:, u], x_blocks[bass.ds(2 * it + u + 2, 1)]).then_inc(x_in[u], 16)

            with sp.Fori(0, NGRP // 2 - 1) as it:
                for u in range(2):
                    more(it, u)
            more(NGRP // 2 - 1, 0)
            sp.wait_ge(rows_stored[0], 16 * (NGRP // 2 + 2))
            sp.wait_ge(rows_stored[1], 16 * (NGRP // 2 + 1))
            sp.wait_ge(zeroed, 1)
            sp.dma_start(resid[0:TI, :].rearrange("t (b d) -> t b d", b=NB),
                         tok_rows[0:NB * TI].rearrange("(b t) d -> t b d", t=TI)).then_inc(tok_in, 16)
            sp.wait_ge(tok_in, 16)
            sp.wait_ge(txt_in, 16)

        @block.gpsimd
        def _(pool):
            pool.memset(resid[:], 0.0).then_inc(zeroed, 1)
            pool.memset(zrow[:], 0.0).then_inc(zeroed, 1)
            pool.wait_ge(zeroed, 2)
            pool.dma_start(slot_mem.rearrange("(p a n) -> p a n", p=P, n=ZN),
                           zrow[:].unsqueeze(1).to_broadcast([P, NBLK0 * D // ZN, ZN])).then_inc(slots_clear, 16)
            pool.dma_start(resid[TI:T, :].rearrange("t (b d) -> t b d", b=NB),
                           txt.rearrange("b t d -> t b d")).then_inc(txt_in, 16)
            pool.wait_ge(cst_in, 16)

            def inverse_deviation(it, u):
                s = st[0:GM, u]
                pool.wait_ge(var_ready, 2 * it + u + 1)
                pool.tensor_tensor(s[:, 3:4], s[:, 2:3], cst[0:GM, C_EPS:C_EPS + 1], ALU.add).then_inc(eps_added, 1)
                pool.wait_ge(eps_added, 2 * it + u + 1)
                pool.tensor_tensor(s[:, 4:5], s[:, 3:4], cst[0:GM, C_NHALF:C_NHALF + 1], ALU.pow).then_inc(rstd_ready, 1)

            with pool.Fori(0, NGRP // 2) as it:
                for u in range(2):
                    inverse_deviation(it, u)
            inverse_deviation(NGRP // 2, 0)
            pool.wait_ge(slots_clear, 16)

        def window(u, q):
            a, b = q // 2, q % 2
            return xg[:, u].rearrange("p g (i j) -> p g i j", i=BLK)[:, :, a:a + 6, b:b + 6]

        def windows(x, u, q):
            return x[:, u, q * NCH:(q + 1) * NCH].rearrange("p c (s i j) -> p (c s) i j", s=GRP, i=6)

        @block.vector
        def _(dve):
            link = Link(dve, chain)

            def lay_windows(it, u):
                dve.wait_ge(x_in[u], 16 * it + 16)
                for q in range(4):
                    ins = dve.tensor_copy(windows(xw, u, q), window(u, q))
                ins.then_inc(windows_ready, 1)

            for u in range(2):
                lay_windows(0, u)
            dve.wait_ge(w_in, 7 * 16)

            def wide(n):
                return gain[:, n, :].unsqueeze(2).to_broadcast([P, NK, D])

            dve.tensor_tensor(weff[:, :, 0:D], ws[:], wide(0), ALU.mult).then_inc(chain, 1)
            dve.wait_ge(sums_ready, 1)
            dve.wait_ge(cst_in, 16)
            dve.tensor_tensor(wb[:], wb[:], wide(1), ALU.mult).then_inc(chain, 1)
            dve.wait_ge(chain, 2)
            dve.tensor_tensor(weff[:, :, 0:D], weff[:, :, 0:D], wb[:], ALU.add).then_inc(weff_ready, 1)
            dve.tensor_copy(weff[:, :, D], cst[:, C_MULT:C_MULT + NK]).then_inc(weff_ready, 1)
            link.base = 2
            dve.tensor_copy(shift[:], c_ps[:, 0, 0:D]).then_inc(sums_out, 1)
            dve.wait_ge(sums_ready, 2)
            dve.tensor_copy(colsum[:], c_ps[:, 1, 0:D]).then_inc(sums_out, 1)
            dve.wait_ge(sums_out, 2)

            for n, c in enumerate((C_ID, C_ONE, C_TRI, C_TRS)):
                dve.tensor_copy(cstb[:, n], cst[:, c:c + P])
            dve.memset(st[:, 0], 0.0).then_inc(y_used, 2)
            for u in range(2):
                dve.memset(rows[:, u], 0.0).then_inc(rows_stored[u], 16)

            def normalise(it, u):
                s = st[0:GM, u]
                dve.wait_ge(products_done, 2 * it + u + 1)
                link.done(dve.tensor_scalar(s[:, 0:1], y_ps[0:GM, u, D:D + 1], -1.0 / PATCH_DIM, None, ALU.mult))
                link.done(dve.tensor_tensor(s[:, 1:2], s[:, 0:1], s[:, 0:1], ALU.mult))
                dve.scalar_tensor_tensor(s[:, 2:3], q_ps[0:GM, u, 0:1], 1.0 / PATCH_DIM, s[:, 1:2],
                                         ALU.mult, ALU.subtract).then_inc(var_ready, 1)
                dve.scalar_tensor_tensor(tok[0:GM, u], colsum[0:GM], s[:, 0:1], y_ps[0:GM, u, 0:D],
                                         ALU.mult, ALU.add).then_inc(y_used, 1)
                dve.wait_ge(y_used, 2 * it + u + 3)
                dve.wait_ge(rstd_ready, 2 * it + u + 1)
                dve.wait_ge(rows_stored[u], 16 * it + 16)
                dve.scalar_tensor_tensor(rows[0:GM, u], tok[0:GM, u], s[:, 4:5], shift[0:GM], ALU.mult, ALU.add)\
                   .then_inc(tok_ready, 1)

            with dve.Fori(0, NGRP // 2 - 1) as it:
                link.loop(it, 4)
                for u in range(2):
                    normalise(it, u)
                    lay_windows(it + 1, u)
            link.end(NGRP // 2 - 1)
            last = NGRP // 2 - 1
            normalise(last, 0)
            lay_windows(last + 1, 0)
            normalise(last, 1)
            normalise(last + 1, 0)

        @block.scalar
        def _(act):
            def square(it, u):
                act.wait_ge(x_in[u], 16 * it + 16)
                for q in range(4):
                    ins = act.activation(windows(xsq, u, q), window(u, q), ACT.Square)
                ins.then_inc(squared, 1)

            def finish(it, u):
                g1 = 2 * it + u + 1
                act.wait_ge(tok_ready, g1)
                n = GRP * TI
                act.dma_start(tok_rows[bass.ds((2 * it + u) * n, n), :], rows[0:n, u, :])\
                   .then_inc(rows_stored[u], 16)

            for u in range(2):
                square(0, u)
            with act.Fori(0, NGRP // 2 - 1) as it:
                for u in range(2):
                    act.wait_ge(products_done, 2 * it + u + 1)
                    square(it + 1, u)
                    finish(it, u)
            it = NGRP // 2 - 1
            act.wait_ge(products_done, 2 * it + 1)
            square(it + 1, 0)
            finish(it, 0)
            finish(it, 1)
            finish(it + 1, 0)

        @block.tensor
        def _(pe):
            ones = cst[:, C_ONE:C_ONE + P]
            pe.wait_ge(w_in, 7 * 16)
            pe.wait_ge(cst_in, 16)
            pe.matmul(c_ps[:, 0, 0:D], ones[0:1, :], bias[:], start=True, stop=False)
            for part, w in ((2, ws), (3, wb)):
                for k in range(NK):
                    mm = pe.matmul(c_ps[:, 0, 0:D], gain[:, part, k:k + 1].to_broadcast([P, P]), w[:, k, :],
                                   start=False, stop=part == 3 and k == NK - 1)
            mm.then_inc(sums_ready, 1)
            pe.wait_ge(weff_ready, 2)
            for k in range(NK):
                mm = pe.matmul(c_ps[:, 1, 0:D], ones, weff[:, k, 0:D], start=k == 0, stop=k == NK - 1)
            mm.then_inc(sums_ready, 1)

            def group(it, u):
                m = GRP * TI
                pe.wait_ge(windows_ready, 2 * it + u + 1)
                for k in range(NK):
                    pe.matmul(y_ps[0:m, u, 0:D + 1], xw[:, u, k, :], weff[:, k, :], start=k == 0, stop=k == NK - 1)
                pe.wait_ge(squared, 2 * it + u + 1)
                for k in range(NK):
                    mm = pe.matmul(q_ps[0:m, u, 0:1], xsq[:, u, k, :], weff[:, k, D:D + 1],
                                   start=k == 0, stop=k == NK - 1)
                mm.then_inc(products_done, 1)

            with pe.Fori(0, NGRP // 2) as it:
                for u in range(2):
                    pe.wait_ge(y_used, 2 * it + u + 1)
                    group(it, u)
            pe.wait_ge(y_used, NGRP)
            group(NGRP // 2, 0)


def layer_norm_stats(nc, name, resid, cst, mean, rstd):
    with ExitStack() as ctx:
        take = ctx.enter_context(semaphores(nc))
        six = ctx.enter_context(nc.sbuf_tensor(name + "_six", [P, NB, 6], F32))
        ve = ctx.enter_context(nc.sbuf_tensor(name + "_ve", [P, NB], F32))
        six_ready = take(name + "_six_ready")
        var = ctx.enter_context(nc.sbuf_tensor(name + "_var", [P, NB], F32))
        tmp = ctx.enter_context(nc.sbuf_tensor(name + "_tmp", [P, 4, NB], F32))
        var_ready = take(name + "_var_ready")
        chain = take(name + "_chain")
        ve_ready = take(name + "_ve_ready")
        block = ctx.enter_context(nc.Block())

        @block.vector
        def _(dve):
            with dve.Fori(0, NB) as b:
                dve.bn_stats(six[:, bass.ds(b, 1), :], resid[:, bass.ds(b * D, D)]).then_inc(six_ready, 1)
            dve.wait_ge(six_ready, NB)
            link = Link(dve, chain)
            dve.tensor_tensor(tmp[:, 0], six[:, :, 1], six[:, :, 4], ALU.add).then_inc(chain, 1)
            dve.tensor_tensor(tmp[:, 1], six[:, :, 1], six[:, :, 4], ALU.subtract).then_inc(chain, 1)
            dve.tensor_tensor(tmp[:, 2], six[:, :, 2], six[:, :, 5], ALU.add).then_inc(chain, 1)
            dve.wait_ge(chain, 3)
            link.base = 3
            dve.tensor_scalar(mean[:], tmp[:, 0], 0.5, None, ALU.mult).then_inc(var_ready, 1)
            link.done(dve.scalar_tensor_tensor(tmp[:, 3], tmp[:, 1], 0.25, tmp[:, 1], ALU.mult, ALU.mult))
            dve.scalar_tensor_tensor(var[:], tmp[:, 2], 1.0 / D, tmp[:, 3], ALU.mult, ALU.add).then_inc(var_ready, 1)
            dve.wait_ge(var_ready, 2)

        @block.gpsimd
        def _(pool):
            pool.wait_ge(var_ready, 2)
            pool.tensor_scalar(ve[:], var[:], LN_EPS, None, ALU.add).then_inc(ve_ready, 1)
            pool.wait_ge(ve_ready, 1)
            pool.tensor_tensor(rstd[:], ve[:], cst[:, C_NHALF:C_NHALF + 1].to_broadcast([P, NB]), ALU.pow)\
                .then_inc(ve_ready, 1)
            pool.wait_ge(ve_ready, 2)


def channel_attention(nc, wqk_d, wv_d, wp_d, bp_d, temp_d, cst, resid, mean, rstd):
    U = 4
    with ExitStack() as ctx:
        take = ctx.enter_context(semaphores(nc))
        def sb(name, shape, dt=F32):
            return ctx.enter_context(nc.sbuf_tensor("ca_" + name, shape, dt))

        def sem(name):
            return take("ca_" + name)

        wqk, wv, wp = sb("wqk", [DH, 2, 2 * D]), sb("wv", [DH, 2, D]), sb("wp", [DH, 2, D])
        bp, temp = sb("bp", [1, D]), sb("temp", [DH, 2])
        hn = sb("hn", [P, U, D])
        hnt = sb("hnt", [DH, U, 2, P])
        qk = sb("qk", [P, U, 2 * D])
        sq = sb("sq", [P, U, 2 * D])
        vt = sb("vt", [DH, U, 2, P])
        ss = sb("ss", [DH, U, D + 2])
        rn = sb("rn", [DH, U, D + 2])
        rqt = sb("rqt", [DH, U, 2])
        sc = sb("sc", [DH, U, 2, DH])
        pr = sb("pr", [DH, U, 2, DH])
        nmx, sm, rs = sb("nmx", [DH, U, 2]), sb("sm", [DH, U, 2]), sb("rs", [DH, U, 2])
        mix = sb("mix", [DH, U, 2, D])
        pa = ctx.enter_context(nc.psum_tensor("ca_pa", [P, U, 512], F32))
        pb = ctx.enter_context(nc.psum_tensor("ca_pb", [P, U, 512], F32))
        w_in, hn_ready, hnt_ps, hnt_ready = sem("w_in"), sem("hn_ready"), sem("hnt_ps"), sem("hnt_ready")
        qk_ps, qk_ready, sq_ready, vt_ps = sem("qk_ps"), sem("qk_ready"), sem("sq_ready"), sem("vt_ps")
        vt_ready, gram_ps, ss_ready = sem("vt_ready"), sem("gram_ps"), sem("ss_ready")
        max_ready, exp_ready, attn_ready = sem("max_ready"), sem("exp_ready"), sem("attn_ready")
        mix_ps, mix_ready, out_ps, chain = sem("mix_ps"), sem("mix_ready"), sem("out_ps"), sem("chain")
        block = ctx.enter_context(nc.Block())

        @block.sync
        def _(sp):
            for dst, src in ((wqk, wqk_d), (wv, wv_d), (wp, wp_d), (bp, bp_d), (temp, temp_d)):
                sp.dma_start(dst[:], src).then_inc(w_in, 16)
            sp.wait_ge(w_in, 5 * 16)

        @block.tensor
        def _(pe):
            ident = cst[:, C_ID:C_ID + P]
            ones = cst[:, C_ONE:C_ONE + P]
            pe.wait_ge(w_in, 5 * 16)
            with pe.Fori(0, NB // U) as it:
                for u in range(U):
                    pe.wait_ge(hn_ready, it * U + u + 1)
                    for c in range(2):
                        mm = pe.transpose(pa[0:DH, u, c * P:(c + 1) * P], hn[:, u, c * DH:(c + 1) * DH], ident)
                    mm.then_inc(hnt_ps, 1)
                for u in range(U):
                    pe.wait_ge(hnt_ready, it * U + u + 1)
                    for c in range(2):
                        mm = pe.matmul(pb[:, u, 0:2 * D], hnt[:, u, c], wqk[:, c], start=c == 0, stop=c == 1)
                    mm.then_inc(qk_ps, 1)
                for u in range(U):
                    for g in range(2):
                        for c in range(2):
                            mm = pe.matmul(pa[0:DH, u, g * P:(g + 1) * P], wv[:, c, g * DH:(g + 1) * DH],
                                           hnt[:, u, c], start=c == 0, stop=c == 1)
                    mm.then_inc(vt_ps, 1)
                for u in range(U):
                    pe.wait_ge(qk_ready, it * U + u + 1)
                    for g in range(2):
                        pe.matmul(pb[0:DH, u, g * DH:(g + 1) * DH], qk[:, u, g * DH:(g + 1) * DH],
                                  qk[:, u, D + g * DH:D + (g + 1) * DH], start=True, stop=True)
                    pe.wait_ge(sq_ready, it * U + u + 1)
                    pe.matmul(pb[0:DH, u, D:2 * D], ones[:, 0:DH], sq[:, u, D:2 * D], start=True, stop=True)
                    for g in range(2):
                        mm = pe.matmul(pb[0:DH, u, 2 * D + g:2 * D + g + 1], sq[:, u, g * DH:(g + 1) * DH],
                                       ones[:, 0:1], start=True, stop=True)
                    mm.then_inc(gram_ps, 1)
                for u in range(U):
                    pe.wait_ge(vt_ready, it * U + u + 1)
                    pe.wait_ge(attn_ready, it * U + u + 1)
                    for g in range(2):
                        mm = pe.matmul(pa[0:DH, u, g * D:(g + 1) * D], pr[:, u, g], wp[:, g], start=True, stop=True)
                    mm.then_inc(mix_ps, 1)
                for u in range(U):
                    pe.wait_ge(mix_ready, it * U + u + 1)
                    for g in range(2):
                        pe.matmul(pb[0:T, u, 0:D], vt[:, u, g, 0:T], mix[:, u, g], start=g == 0, stop=False)
                    pe.matmul(pb[0:T, u, 0:D], ones[0:1, 0:T], bp[:], start=False, stop=True).then_inc(out_ps, 1)

        @block.scalar
        def _(act):
            with act.Fori(0, NB // U) as it:
                for u in range(U):
                    act.wait_ge(hnt_ps, it * U + u + 1)
                    act.copy(hnt[:, u], pa[0:DH, u, 0:2 * P].rearrange("p (c t) -> p c t", c=2)).then_inc(hnt_ready, 1)
                for u in range(U):
                    act.wait_ge(qk_ps, it * U + u + 1)
                    act.copy(qk[:, u], pb[:, u, 0:2 * D]).then_inc(qk_ready, 1)
                for u in range(U):
                    act.wait_ge(vt_ps, it * U + u + 1)
                    act.copy(vt[:, u], pa[0:DH, u, 0:2 * P].rearrange("p (c t) -> p c t", c=2)).then_inc(vt_ready, 1)
                for u in range(U):
                    act.wait_ge(gram_ps, it * U + u + 1)
                    act.activation(ss[:, u], pb[0:DH, u, D:2 * D + 2], ACT.Sqrt).then_inc(ss_ready, 1)
                for u in range(U):
                    act.wait_ge(max_ready, it * U + u + 1)
                    for g in range(2):
                        ins = act.activation(pr[:, u, g], sc[:, u, g], ACT.Exp, bias=nmx[:, u, g:g + 1],
                                             accum_out=sm[:, u, g:g + 1])
                        ins.then_inc(exp_ready, 1)
                for u in range(U):
                    act.wait_ge(mix_ps, it * U + u + 1)
                    act.copy(mix[:, u], pa[0:DH, u, 0:2 * D].rearrange("p (g d) -> p g d", g=2)).then_inc(mix_ready, 1)

        @block.gpsimd
        def _(pool):
            with pool.Fori(0, NB // U) as it:
                for u in range(U):
                    pool.wait_ge(qk_ready, it * U + u + 1)
                    pool.tensor_tensor(sq[:, u], qk[:, u], qk[:, u], ALU.mult).then_inc(sq_ready, 1)

        @block.vector
        def _(dve):
            link = Link(dve, chain)
            dve.wait_ge(w_in, 5 * 16)
            with dve.Fori(0, NB // U) as it:
                link.loop(it, U * 8)
                for u in range(U):
                    b = it * U + u
                    dve.tensor_scalar(hn[:, u], resid[:, bass.ds(b * D, D)], mean[:, bass.ds(b, 1)],
                                      rstd[:, bass.ds(b, 1)], ALU.subtract, ALU.mult).then_inc(hn_ready, 1)
                for u in range(U):
                    dve.wait_ge(ss_ready, it * U + u + 1)
                    link.done(dve.reciprocal(rn[:, u], ss[:, u]))
                    dve.tensor_tensor(rqt[:, u], rn[:, u, D:D + 2], temp[:], ALU.mult).then_inc(chain, 1)
                    link.n += 1
                    link.done(dve.tensor_tensor(sc[:, u].rearrange("p g d -> p (g d)"), pb[0:DH, u, 0:D], rn[:, u, 0:D],
                                                ALU.mult))
                    for g in range(2):
                        ins = dve.scalar_tensor_tensor(sc[:, u, g], sc[:, u, g], rqt[:, u, g:g + 1],
                                                       cst[0:DH, C_BLKM:C_BLKM + DH], ALU.mult, ALU.add)
                        if g == 0:
                            ins.then_inc(chain, 1)
                            link.n += 1
                    link.done(ins)
                    link.done(dve.tensor_reduce(rs[:, u], sc[:, u], AX.X, ALU.max))
                    dve.tensor_scalar(nmx[:, u], rs[:, u], -1.0, None, ALU.mult).then_inc(max_ready, 1)
                for u in range(U):
                    dve.wait_ge(max_ready, it * U + u + 1)
                    dve.wait_ge(exp_ready, 2 * (it * U + u) + 2)
                    link.done(dve.reciprocal(rs[:, u], sm[:, u]))
                    dve.tensor_tensor(pr[:, u], pr[:, u], rs[:, u].unsqueeze(2).to_broadcast([DH, 2, DH]), ALU.mult)\
                       .then_inc(attn_ready, 1)
                for u in range(U):
                    b = it * U + u
                    dve.wait_ge(out_ps, it * U + u + 1)
                    h = resid[0:T, bass.ds(b * D, D)]
                    link.done(dve.tensor_tensor(h, h, pb[0:T, u, 0:D], ALU.add))


def route_tokens(nc, emb_d, wcat_d, bcat_d, cst, resid, mean, rstd, embt, chosen, weight, index):
    U = 4
    with ExitStack() as ctx:
        take = ctx.enter_context(semaphores(nc))
        def sb(name, shape, dt=F32):
            return ctx.enter_context(nc.sbuf_tensor("rt_" + name, shape, dt))

        def sem(name):
            return take("rt_" + name)

        emb = sb("emb", [NE, 2, 64])
        junk, ess = sb("junk", [NE, 64]), sb("ess", [NE, 2])
        wcat, bcat = sb("wcat", [DH, 2, P]), sb("bcat", [P, 1])
        hn = sb("hn", [P, U, D])
        hnt = sb("hnt", [DH, U, 2, P])
        zt = sb("zt", [P, U, P])
        e = sb("e", [P, U * 2, NE + 4])
        zap = sb("zap", [P, U * 2, NE + 4])
        top8, taken = sb("top8", [P, U * 2, 8]), sb("taken", [P, U * 2, 8])
        ix = sb("ix", [P, U * 2, 8], U32)
        mx, nmx, z = sb("mx", [P, U, 2]), sb("nmx", [P, U, 2]), sb("z", [P, U * 2])
        zc = sb("zc", [P, U * 2])
        s4, den, rden = sb("s4", [P, U * 2]), sb("den", [P, U * 2]), sb("rden", [P, U * 2])
        pa = ctx.enter_context(nc.psum_tensor("rt_pa", [P, U, 512], F32))
        pb = ctx.enter_context(nc.psum_tensor("rt_pb", [P, U, 512], F32))
        w_in, setup, chain = sem("w_in"), sem("setup"), sem("chain")
        emb_sq, emb_norm, emb_unit, emb_ps, embt_ready = (
            sem("emb_sq"), sem("emb_norm"), sem("emb_unit"), sem("emb_ps"), sem("embt_ready"))
        hn_ready, hnt_ps, hnt_ready, z_ps, z_ready = (
            sem("hn_ready"), sem("hnt_ps"), sem("hnt_ready"), sem("z_ps"), sem("z_ready"))
        logit_ps, max_ready, exp_ready = sem("logit_ps"), sem("max_ready"), sem("exp_ready")
        block = ctx.enter_context(nc.Block())

        @block.sync
        def _(sp):
            for dst, src in ((emb, emb_d), (wcat, wcat_d), (bcat, bcat_d)):
                sp.dma_start(dst[:], src).then_inc(w_in, 16)
            sp.wait_ge(w_in, 3 * 16)

        @block.scalar
        def _(act):
            act.wait_ge(w_in, 3 * 16)
            for r in range(2):
                if r:
                    act.wait_ge(emb_sq, r)
                act.activation(junk[:], emb[:, r], ACT.Square, accum_out=ess[:, r:r + 1]).then_inc(emb_sq, 1)
            act.wait_ge(emb_sq, 2)
            act.activation(den[:, 0:2], ess[:], ACT.Sqrt).then_inc(emb_norm, 1)
            with act.Fori(0, NB // U) as it:
                for u in range(U):
                    act.wait_ge(hnt_ps, it * U + u + 1)
                    act.copy(hnt[:, u], pa[0:DH, u, 0:2 * P].rearrange("p (c t) -> p c t", c=2)).then_inc(hnt_ready, 1)
                for u in range(U):
                    act.wait_ge(z_ps, it * U + u + 1)
                    act.activation(zt[:, u], pb[:, u, 0:P], ACT.Identity, bias=bcat[:]).then_inc(z_ready, 1)
                for u in range(U):
                    act.wait_ge(max_ready, it * U + u + 1)
                    for r in range(2):
                        ins = act.activation(e[:, 2 * u + r, 0:NE], pa[:, u, r * NE:(r + 1) * NE], ACT.Exp,
                                             bias=nmx[:, u, r:r + 1], accum_out=z[:, 2 * u + r:2 * u + r + 1])
                    ins.then_inc(exp_ready, 1)

        @block.tensor
        def _(pe):
            ident = cst[:, C_ID:C_ID + P]
            pe.wait_ge(emb_unit, 1)
            pe.transpose(pa[:, 0, 0:P], emb[:].rearrange("n r d -> n (r d)"), ident).then_inc(emb_ps, 1)
            pe.wait_ge(embt_ready, 4)
            with pe.Fori(0, NB // U) as it:
                for u in range(U):
                    pe.wait_ge(hn_ready, it * U + u + 1)
                    for c in range(2):
                        mm = pe.transpose(pa[0:DH, u, c * P:(c + 1) * P], hn[:, u, c * DH:(c + 1) * DH], ident)
                    mm.then_inc(hnt_ps, 1)
                for u in range(U):
                    pe.wait_ge(hnt_ready, it * U + u + 1)
                    for c in range(2):
                        mm = pe.matmul(pb[:, u, 0:P], wcat[:, c], hnt[:, u, c], start=c == 0, stop=c == 1)
                    mm.then_inc(z_ps, 1)
                for u in range(U):
                    pe.wait_ge(z_ready, it * U + u + 1)
                    pe.matmul(pa[:, u, 0:2 * NE], zt[:, u], embt[:], start=True, stop=True).then_inc(logit_ps, 1)

        @block.vector
        def _(dve):
            link = Link(dve, chain)
            dve.memset(embt[0:64, NE:2 * NE], 0.0).then_inc(embt_ready, 1)
            dve.memset(embt[64:P, 0:NE], 0.0).then_inc(embt_ready, 1)
            dve.wait_ge(emb_norm, 1)
            link.done(dve.tensor_scalar(s4[:, 0:2], den[:, 0:2], 1e-8, None, ALU.add))
            link.done(dve.reciprocal(rden[:, 0:2], s4[:, 0:2]))
            dve.tensor_tensor(emb[:], emb[:], rden[:, 0:2].unsqueeze(2).to_broadcast([NE, 2, 64]), ALU.mult)\
               .then_inc(emb_unit, 1)
            dve.wait_ge(emb_ps, 1)
            dve.tensor_copy(embt[0:64, 0:NE], pa[0:64, 0, 0:NE]).then_inc(embt_ready, 1)
            dve.tensor_copy(embt[64:P, NE:2 * NE], pa[64:P, 0, 0:NE]).then_inc(embt_ready, 1)
            for buf, at in ((e, NE), (taken, 4)):
                link.done(dve.tensor_copy(buf[:, :, at:at + 4],
                                          cst[:, C_SENT:C_SENT + 4].unsqueeze(1).to_broadcast([P, 2 * U, 4])))
            with dve.Fori(0, NB // U) as it:
                link.loop(it, U + 1 + 4 + 1)
                for u in range(U):
                    b = it * U + u
                    dve.tensor_scalar(hn[:, u], resid[:, bass.ds(b * D, D)], mean[:, bass.ds(b, 1)],
                                      rstd[:, bass.ds(b, 1)], ALU.subtract, ALU.mult).then_inc(hn_ready, 1)
                for u in range(U):
                    dve.wait_ge(logit_ps, it * U + u + 1)
                    link.done(dve.tensor_reduce(mx[:, u], pa[:, u, 0:2 * NE].rearrange("p (r n) -> p r n", r=2),
                                                AX.X, ALU.max))
                    dve.tensor_scalar(nmx[:, u], mx[:, u], -1.0, None, ALU.mult).then_inc(max_ready, 1)
                for u in range(U):
                    dve.wait_ge(exp_ready, it * U + u + 1)
                    dve.tensor_copy(zc[:, 2 * u:2 * u + 2], z[:, 2 * u:2 * u + 2])
                    for r in range(2):
                        ins = dve.max(top8[:, 2 * u + r], e[:, 2 * u + r, 0:NE])
                link.done(ins)
                link.done(dve.tensor_copy(taken[:, :, 0:4], top8[:, :, 0:4]))
                dve.tensor_reduce(s4[:], top8[:, :, 0:4], AX.X, ALU.add)
                for k in range(2 * U):
                    dve.max_index(ix[:, k], top8[:, k], e[:, k, 0:NE])
                    ins = dve.match_replace(zap[:, k], taken[:, k], e[:, k], -9.0)
                link.done(ins)
                link.done(dve.scalar_tensor_tensor(den[:], zc[:], 1e-8, s4[:], ALU.mult, ALU.add))
                for k in range(2 * U):
                    dve.tensor_scalar(chosen[:, bass.ds((it * U + k // 2) * 2 + k % 2, 1), :],
                                      zap[:, k:k + 1, 0:NE], -5.0, cst[:, C_VALID:C_VALID + 1], ALU.is_lt, ALU.mult)
                link.done(dve.reciprocal(rden[:], den[:]))
                dve.tensor_copy(index[:, bass.ds(it * 2 * U, 2 * U), :], ix[:, :, 0:4])
                link.done(dve.tensor_tensor(weight[:, bass.ds(it * 2 * U, 2 * U), :], top8[:, :, 0:4],
                                            rden[:].unsqueeze(2).to_broadcast([P, 2 * U, 4]), ALU.mult))


def block_tables(nc, cst, cstb, chosen, seg_start, block_expert):
    with ExitStack() as ctx:
        take = ctx.enter_context(semaphores(nc))
        def sb(name, shape, dt=F32):
            return ctx.enter_context(nc.sbuf_tensor("bt_" + name, shape, dt))

        def sem(name):
            return take("bt_" + name)

        total = sb("total", [P, 2 * NE], BF16)
        more, blocks_i = sb("more", [P, 2], I32), sb("blocks_i", [P, 2], I32)
        blocks, blocks_b = sb("blocks", [P, 2]), sb("blocks_b", [P, 2], BF16)
        incl, before = sb("incl", [P, 2]), sb("before", [P, 2, 256], BF16)
        row = sb("row", [1, 2, 256])
        ps = ctx.enter_context(nc.psum_tensor("bt_ps", [P, 3, 512], F32))
        total_ready, count_ps, blocks_ready = sem("total_ready"), sem("count_ps"), sem("blocks_ready")
        incl_ps, before_ready, row_ps, chain = sem("incl_ps"), sem("before_ready"), sem("row_ps"), sem("chain")
        block = ctx.enter_context(nc.Block())

        @block.vector
        def _(dve):
            link = Link(dve, chain)
            link.done(dve.tensor_copy(total[:], chosen[:, 0:2].rearrange("p r n -> p (r n)")))
            with dve.Fori(1, NB) as b:
                link.loop(b - 1, 1)
                link.done(dve.tensor_tensor(total[:].rearrange("p (r n) -> p r n", r=2),
                                            total[:].rearrange("p (r n) -> p r n", r=2),
                                            chosen[:, bass.ds(2 * b, 2), :], ALU.add))
            link.end(NB - 1)
            dve.memset(row[:], 0.0).then_inc(total_ready, 1)
            dve.wait_ge(count_ps, 1)
            link.done(dve.tensor_scalar(more[:], ps[:, 0, 0:2], P - 1.0, None, ALU.add))
            link.done(dve.tensor_scalar(blocks_i[:], more[:], 7, None, ALU.arith_shift_right))
            link.done(dve.tensor_copy(blocks[:], blocks_i[:]))
            dve.tensor_copy(blocks_b[:], blocks[:]).then_inc(blocks_ready, 1)
            for r in range(2):
                dve.tensor_scalar(seg_start[:, r], cst[:, C_ONE:C_ONE + P], blocks[:, r:r + 1], float(P),
                                  ALU.mult, ALU.mult)
            dve.wait_ge(incl_ps, 1)
            link.done(dve.tensor_copy(incl[:], ps[:, 1, 0:2]))
            for r in range(2):
                dve.tensor_scalar(before[:, r], cst[:, C_IOTA:C_IOTA + 256], incl[:, r:r + 1], None, ALU.is_ge)\
                   .then_inc(before_ready, 1)
            dve.wait_ge(row_ps, 1)
            link.done(dve.tensor_scalar(block_expert[:], ps[0:1, 2, 0:512].rearrange("p (r t) -> p r t", r=2),
                                        NE - 1.0, None, ALU.min))

        @block.tensor
        def _(pe):
            ones = cstb[:, 1]
            pe.wait_ge(total_ready, 1)
            for r in range(2):
                mm = pe.matmul(ps[:, 0, r:r + 1], total[:, r * NE:(r + 1) * NE], ones[:, 0:1], start=True, stop=True)
            mm.then_inc(count_ps, 1)
            pe.wait_ge(blocks_ready, 1)
            pe.matmul(ps[:, 1, 0:2], cstb[:, 2], blocks_b[:], start=True, stop=True).then_inc(incl_ps, 1)
            pe.wait_ge(before_ready, 2)
            pe.matmul(ps[0:1, 2, 0:512], ones[:, 0:1], before[:].rearrange("p r t -> p (r t)"), start=True, stop=True)\
              .then_inc(row_ps, 1)


def place_tokens(nc, cst, cstb, resid, mean, rstd, chosen, index, seg_start, slot, slot_rows,
                 know, f_know, know_in):
    U = 4
    with ExitStack() as ctx:
        take = ctx.enter_context(semaphores(nc))
        def sb(name, shape, dt=F32):
            return ctx.enter_context(nc.sbuf_tensor("pl_" + name, shape, dt))

        def sem(name):
            return take("pl_" + name)

        earlier = sb("earlier", [P, U + 1, 2, NE], BF16)
        junk = sb("junk", [P, 8, NE], BF16)
        slot_f = sb("slot_f", [P, U, 8])
        slot_i = sb("slot_i", [P, U, 8], I32)
        hn = sb("hn", [P, U, D])
        rank = ctx.enter_context(nc.psum_tensor("pl_rank", [P, U, 512], F32))
        in_block, low, high = sb("in_block", [P, U, 8], I32), sb("low", [P, U, 8], I32), sb("high", [P, U, 8], I32)
        chain, summed, rank_ps, slot_ready = sem("chain"), sem("summed"), sem("rank_ps"), sem("slot_ready")
        scattered = [sem(f"scattered{u}") for u in range(U)]
        block = ctx.enter_context(nc.Block())

        @block.sync
        def _(sp):
            load_knowledge(sp, know, f_know, D, R, know_in)

        @block.tensor
        def _(pe):
            with pe.Fori(0, NB // U) as it:
                for u in range(U):
                    b2 = 2 * (it * U + u)
                    pe.wait_ge(summed, it * U + u + 1)
                    pe.matmul(rank[:, u, 0:2 * NE], cstb[:, 3], chosen[:, bass.ds(b2, 2), :], start=True, stop=False)
                    pe.matmul(rank[:, u, 0:2 * NE], cstb[:, 1], earlier[:, u], start=False, stop=False)
                    for r in range(2):
                        mm = pe.matmul(rank[:, u, r * NE:(r + 1) * NE], seg_start[:, r], cstb[:, 3],
                                       start=False, stop=r == 1)
                    mm.then_inc(rank_ps, 1)

        @block.vector
        def _(dve):
            link = Link(dve, chain)
            link.done(dve.memset(earlier[:, U], 0.0))

            def turn(it, first):
                for u in range(U):
                    if u == 0:
                        ins = dve.tensor_copy(earlier[:, 0], earlier[:, U])
                    else:
                        ins = dve.tensor_tensor(earlier[:, u], earlier[:, u - 1],
                                                chosen[:, bass.ds(2 * (it * U + u - 1), 2), :], ALU.add)
                    ins.then_inc(summed, 1)
                    dve.wait_ge(summed, it * U + u + 1)
                for u in range(U):
                    b = it * U + u
                    if u == 0:
                        link.done(dve.tensor_tensor(earlier[:, U], earlier[:, U - 1],
                                                    chosen[:, bass.ds(2 * (it * U + U - 1), 2), :], ALU.add))
                    if not first:
                        dve.wait_ge(scattered[u], 64 * it)
                    dve.tensor_scalar(hn[:, u], resid[:, bass.ds(b * D, D)], mean[:, bass.ds(b, 1)],
                                      rstd[:, bass.ds(b, 1)], ALU.subtract, ALU.mult).then_inc(slot_ready, 1)
                    dve.wait_ge(rank_ps, b + 1)
                    for k in range(8):
                        r, j = k // 4, k % 4
                        ins = dve.scalar_tensor_tensor(junk[:, k], cst[:, C_IOTA:C_IOTA + NE],
                                                       index[:, bass.ds(2 * b + r, 1), j], rank[:, u, r * NE:(r + 1) * NE],
                                                       ALU.is_equal, ALU.mult, accum_out=slot_f[:, u, k:k + 1])
                    link.done(ins)
                    link.done(dve.tensor_scalar(high[:, u], slot_f[:, u], cst[:, C_FAR:C_FAR + 1], None, ALU.add))
                    dve.tensor_scalar(in_block[:, u], high[:, u], P - 1, 2, ALU.bitwise_and, ALU.logical_shift_left)
                    dve.tensor_scalar(low[:, u], high[:, u], 7, GROUP - 1, ALU.arith_shift_right, ALU.bitwise_and)
                    link.done(dve.tensor_scalar(high[:, u], high[:, u], -GROUP * P, None, ALU.bitwise_and))
                    link.done(dve.tensor_tensor(high[:, u], high[:, u], in_block[:, u], ALU.bitwise_or))
                    ins = dve.tensor_tensor(slot_i[:, u], high[:, u], low[:, u], ALU.bitwise_or)
                    ins.then_inc(slot_ready, 1)
                    dve.wait_ge(slot_ready, 2 * b + 2)
                    link.done(dve.tensor_copy(slot[:, bass.ds(b, 1), :], slot_i[:, u:u + 1]))

            turn(0, True)
            with dve.Fori(1, NB // U) as it:
                link.loop(it - 1, 1 + 5 * U)
                turn(it, False)

        @block.gpsimd
        def _(pool):
            last_slot = pool.to_reg(NBLK0 * P - 1)
            for it in range(NB // U):
                for u in range(U):
                    pool.wait_ge(slot_ready, 2 * (it * U + u) + 2)
                    for j in range(4):
                        pool.indirect_dma_start(slot_rows, bass.IndirectOffsetOnAxis(slot_i[:, u, j:j + 1], 0),
                                                hn[:, u], None, bounds_check=last_slot, oob_is_err=False)\
                            .then_inc(scattered[u], 16)
            for u in range(U):
                pool.wait_ge(scattered[u], 64 * (NB // U))


def load_experts(nc, engine, table, top):
    return nc.values_load_multi_w_load_instructions(
        table, engines=(engine,), min_val=0, max_val=top,
        skip_runtime_bounds_check_because="the table was written with a minimum against top")[1]


def load_knowledge(eng, know, weights, k, n, loaded):
    kc = -(-k // P)
    for part in range(KPARTS):
        m = NE // KPARTS
        eng.dma_start(know[0:k // kc, part * m * kc * n:(part + 1) * m * kc * n].rearrange("p (a n) -> p a n", n=n),
                      weights[part * m:(part + 1) * m].rearrange("e (c p) n -> p (e c) n", c=kc)).then_inc(loaded, 16)


def blocks_product(nc, name, cst, block_expert, part, rows_in, know, know_in, rows_out, k, n):
    XG, YG = 4, 2
    W = XG * GROUP
    AHEAD = 2
    kc = -(-k // P)
    kp = k // kc
    turns = NBLK0 // W
    with ExitStack() as ctx:
        take = ctx.enter_context(semaphores(nc))
        def sb(nm, shape, dt=F32):
            return ctx.enter_context(nc.sbuf_tensor(f"{name}_{nm}", shape, dt))

        def sem(nm):
            return take(f"{name}_{nm}")

        x = sb("x", [P, XG, GROUP * k])
        xt = sb("xt", [kp, 4, kc, P])
        y = sb("y", [P, YG, GROUP * n])
        start = sb("start", [1, 1])
        t_ps = ctx.enter_context(nc.psum_tensor(name + "_t_ps", [P, 4, 512], F32))
        y_ps = ctx.enter_context(nc.psum_tensor(name + "_y_ps", [P, 4, 512], F32))
        x_t, xt_ready, product, y_ready = sem("x_t"), sem("xt_ready"), sem("product"), sem("y_ready")
        loaded = [sem(f"loaded{g}") for g in range(XG)]
        stored = [sem(f"stored{g}") for g in range(YG)]
        block = ctx.enter_context(nc.Block())

        def group_rows(rows, g):
            return rows[bass.ds(g * GROUP * P, GROUP * P), :].rearrange("(p j) d -> p (j d)", j=GROUP)

        @block.sync
        def _(sp):
            for g in range(XG):
                sp.dma_start(x[:, g], group_rows(rows_in, g)).then_inc(loaded[g], 16)
            with sp.Fori(0, turns - 1) as it:
                for g in range(XG):
                    sp.wait_ge(x_t, it * W + (g + 1) * GROUP)
                    sp.dma_start(x[:, g], group_rows(rows_in, it * XG + XG + g)).then_inc(loaded[g], 16)

        @block.tensor
        def _(pe):
            ident = cst[:, C_ID:C_ID + P]
            e_group = None

            def turn_over(it, u):
                if u % GROUP == 0:
                    pe.wait_ge(loaded[u // GROUP], 16 * it + 16)
                for c in range(kc):
                    at = (u % GROUP) * k + c * kp
                    mm = pe.transpose(t_ps[0:kp, u % 4, c * P:(c + 1) * P], x[:, u // GROUP, at:at + kp], ident)
                mm.then_inc(x_t, 1)

            def multiply(it, u):
                nonlocal e_group
                t = it * W + u
                if u % GROUP == 0:
                    e_group = load_experts(nc, mybir.EngineType.PE,
                                           block_expert[0:1, part, bass.ds(t, GROUP)], NE - 1)
                e = e_group[u % GROUP]
                pe.wait_ge(xt_ready, t + 1)
                pe.wait_ge(y_ready, t + 1)
                for c in range(kc):
                    mm = pe.matmul(y_ps[:, u % 4, 0:n], xt[:, u % 4, c],
                                   know[0:kp, bass.ds(e * (kc * n) + c * n, n)], start=c == 0, stop=c == kc - 1)
                mm.then_inc(product, 1)

            for u in range(AHEAD):
                turn_over(0, u)
            pe.wait_ge(know_in, 16 * KPARTS)
            with pe.Fori(0, turns - 1) as it:
                for u in range(W):
                    turn_over(it + (u + AHEAD) // W, (u + AHEAD) % W)
                    multiply(it, u)
            for u in range(W):
                if u + AHEAD < W:
                    turn_over(turns - 1, u + AHEAD)
                multiply(turns - 1, u)

        @block.scalar
        def _(act):
            def send(it, g):
                act.wait_ge(y_ready, 4 + it * W + (g + 1) * GROUP)
                act.dma_start(group_rows(rows_out, it * XG + g), y[:, g % YG]).then_inc(stored[g % YG], 16)

            def copy(it, u):
                act.wait_ge(x_t, it * W + u + 1)
                act.copy(xt[:, u % 4], t_ps[0:kp, u % 4, 0:kc * P].rearrange("p (c t) -> p c t", c=kc))\
                    .then_inc(xt_ready, 1)

            SEND = AHEAD + 1
            for u in range(SEND):
                copy(0, u)
            with act.Fori(0, turns - 1) as it:
                for u in range(W):
                    copy(it + (u + SEND) // W, (u + SEND) % W)
                    if u % GROUP == GROUP - 1:
                        send(it, u // GROUP)
            for u in range(W):
                if u + SEND < W:
                    copy(turns - 1, u + SEND)
                if u % GROUP == GROUP - 1:
                    send(turns - 1, u // GROUP)
            for g in range(YG):
                act.wait_ge(stored[g], 16 * (turns * XG // YG + 1))

        @block.vector
        def _(dve):
            for g in range(YG):
                dve.memset(y[:, g], 0.0).then_inc(stored[g], 16)
            dve.memset(start[:], 0.0).then_inc(y_ready, 4)
            with dve.Fori(0, turns) as it:
                for u in range(W):
                    g, j = u // GROUP, u % GROUP
                    dve.wait_ge(product, it * W + u + 1)
                    if j == 0:
                        dve.wait_ge(stored[g % YG], 16 * (XG // YG) * it + 16 * (g // YG) + 16)
                    dve.tensor_copy(y[:, g % YG, j * n:(j + 1) * n], y_ps[:, u % 4, 0:n]).then_inc(y_ready, 1)


def combine_rows(nc, name, cst, slot, weight, part, rows, n, resid, next_rows, know=None, r_know=None, know_in=None):
    U = 4
    with ExitStack() as ctx:
        take = ctx.enter_context(semaphores(nc))
        def sb(nm, shape, dt=F32):
            return ctx.enter_context(nc.sbuf_tensor(f"{name}_{nm}", shape, dt))

        def sem(nm):
            return take(f"{name}_{nm}")

        g = sb("g", [P, U, 4, n])
        acc = sb("acc", [P, U, n])
        idx = sb("idx", [P, U, 8], I32)
        gathered = [sem(f"gathered{u}") for u in range(U)]
        scattered = [sem(f"scattered{u}") for u in range(U)]
        idx_ready, cleared, summed, chain = sem("idx_ready"), sem("cleared"), sem("summed"), sem("chain")
        block = ctx.enter_context(nc.Block())

        @block.sync
        def _(sp):
            if next_rows is not None:
                load_knowledge(sp, know, r_know, R, D, know_in)

        @block.gpsimd
        def _(pool):
            last_slot = pool.to_reg(NBLK0 * P - 1)

            def gather(it, u):
                pool.wait_ge(idx_ready, it * U + u + 1)
                for j in range(4):
                    pool.indirect_dma_start(g[:, u, j], None, rows,
                                            bass.IndirectOffsetOnAxis(idx[:, u, 4 * part + j:4 * part + j + 1], 0),
                                            bounds_check=last_slot, oob_is_err=False).then_inc(gathered[u], 16)

            def scatter(it, u):
                pool.wait_ge(summed, it * U + u + 1)
                for j in range(4):
                    pool.indirect_dma_start(next_rows, bass.IndirectOffsetOnAxis(idx[:, u, 4 + j:5 + j], 0),
                                            acc[:, u], None, bounds_check=last_slot, oob_is_err=False)\
                        .then_inc(scattered[u], 16)

            pool.wait_ge(cleared, 1)
            for it in range(NB // U):
                for u in range(U):
                    gather(it, u)
                    if next_rows is not None and u:
                        scatter(it, u - 1)
                if next_rows is not None:
                    scatter(it, U - 1)
            if next_rows is not None:
                for u in range(U):
                    pool.wait_ge(scattered[u], 64 * (NB // U))

        @block.vector
        def _(dve):
            link = Link(dve, chain)
            link.done(dve.memset(g[:], 0.0))
            link.done(dve.memset(acc[:], 0.0))
            dve.memset(idx[:], 0).then_inc(cleared, 1)
            dve.wait_ge(cleared, 1)

            def turn(it, first):
                for u in range(U):
                    if next_rows is not None and not first:
                        dve.wait_ge(scattered[u], 64 * it)
                    dve.tensor_copy(idx[:, u:u + 1], slot[:, bass.ds(it * U + u, 1), :]).then_inc(idx_ready, 1)
                for u in range(U):
                    b = it * U + u
                    wt = weight[0:T, bass.ds(2 * b + part, 1), :]
                    dve.wait_ge(gathered[u], 64 * it + 64)
                    link.done(dve.tensor_scalar(acc[0:T, u], g[0:T, u, 0], wt[:, :, 0], None, ALU.mult))
                    for j in range(1, 4):
                        ins = dve.scalar_tensor_tensor(acc[0:T, u], g[0:T, u, j], wt[:, :, j], acc[0:T, u],
                                                       ALU.mult, ALU.add)
                        if j < 3:
                            link.done(ins)
                    ins.then_inc(summed, 1)
                    if next_rows is None:
                        dve.wait_ge(summed, b + 1)
                        h = resid[0:T, bass.ds(b * D, D)]
                        link.done(dve.tensor_tensor(h, h, acc[0:T, u], ALU.add))

            turn(0, True)
            with dve.Fori(1, NB // U) as it:
                link.loop(it - 1, (4 if next_rows is None else 3) * U)
                turn(it, False)


def causal_attention(nc, wq_d, wk_d, wv_d, wo_d, bo_d, cst, cstb, resid, mean, rstd):
    U = 2
    NH, HD, HG = 12, 16, 3
    with ExitStack() as ctx:
        take = ctx.enter_context(semaphores(nc))
        def sb(name, shape, dt=F32):
            return ctx.enter_context(nc.sbuf_tensor("at_" + name, shape, dt))

        def sem(name):
            return take("at_" + name)

        wq, wk = sb("wq", [DH, 2, HG * P]), sb("wk", [DH, 2, HG * P])
        wv, wo, bo = sb("wv", [DH, 2, D]), sb("wo", [DH, 2, D]), sb("bo", [1, D])
        caus = sb("caus", [P, HG * P], BF16)
        hn, hnt = sb("hn", [P, U, D]), sb("hnt", [DH, U, 2, P])
        qt, kt = sb("qt", [P, U, HG * P]), sb("kt", [P, U, HG * P])
        v1 = sb("v1", [P, U, NH, HD + 1])
        mx, p, pt = sb("mx", [P, U, 4, HG]), sb("p", [P, U, 4, HG, P]), sb("pt", [P, U, HG, 4 * P])
        rec, av = sb("rec", [P, U, NH]), sb("av", [P, U, D])
        avt = sb("avt", [DH, U, 2, P])
        ps = ctx.enter_context(nc.psum_tensor("at_ps", [P, 4 * U, 512], F32))
        w_in, hn_ready, hnt_ps, hnt_ready = sem("w_in"), sem("hn_ready"), sem("hnt_ps"), sem("hnt_ready")
        qk_ps, v_ps, q_ready, kv_ready, score_ps = sem("qk_ps"), sem("v_ps"), sem("q_ready"), sem("kv_ready"), sem("score_ps")
        max_ready, added = sem("max_ready"), sem("added")
        shifted, exp_ready, pt_ps = sem("shifted"), sem("exp_ready"), sem("pt_ps")
        pt_act, pt_dve, av_ps, av_ready = sem("pt_act"), sem("pt_dve"), sem("av_ps"), sem("av_ready")
        avt_ps, avt_ready, out_ps, chain = sem("avt_ps"), sem("avt_ready"), sem("out_ps"), sem("chain")
        ones_ready = sem("ones_ready")
        block = ctx.enter_context(nc.Block())

        @block.sync
        def _(sp):
            for dst, src in ((wq, wq_d), (wk, wk_d), (wv, wv_d), (wo, wo_d), (bo, bo_d)):
                sp.dma_start(dst[:], src).then_inc(w_in, 16)
            sp.wait_ge(w_in, 5 * 16)

        @block.tensor
        def _(pe):
            ident = cst[:, C_ID:C_ID + P]
            pe.wait_ge(w_in, 5 * 16)
            pe.wait_ge(ones_ready, 2)
            def turn_over(t, u):
                pe.wait_ge(hn_ready, t + 1)
                for c in range(2):
                    mm = pe.transpose(ps[0:DH, 4 * u + 2, c * P:(c + 1) * P], hn[:, u, c * DH:(c + 1) * DH], ident)
                mm.then_inc(hnt_ps, 1)

            def project(t, u):
                pe.wait_ge(hnt_ready, t + 1)
                for n, w in ((1, wq), (2, wk)):
                    for g in range(HG):
                        for c in range(2):
                            mm = pe.matmul(ps[:, 4 * u + n, g * P:(g + 1) * P], w[:, c, g * P:(g + 1) * P],
                                           hnt[:, u, c], start=c == 0, stop=c == 1)
                    mm.then_inc(qk_ps, 1)
                pe.wait_ge(added, t + 1)
                for c in range(2):
                    mm = pe.matmul(ps[:, 4 * u + 3, 0:D], hnt[:, u, c], wv[:, c], start=c == 0, stop=c == 1)
                mm.then_inc(v_ps, 1)

            def scores(t, u):
                pe.wait_ge(q_ready, t + 1)
                pe.wait_ge(kv_ready, 2 * t + 2)
                for j in range(4):
                    pe.matmul(ps[:, 4 * u + j, 0:HG * P], cstb[:, 0], caus[:], start=True, stop=False)
                for g in range(HG):
                    for j in range(4):
                        mm = pe.matmul(ps[:, 4 * u + j, g * P:(g + 1) * P],
                                       qt[32 * j:32 * j + 32, u, g * P:(g + 1) * P],
                                       kt[32 * j:32 * j + 32, u, g * P:(g + 1) * P], start=False, stop=g == HG - 1)
                mm.then_inc(score_ps, 1)

            def turn_probs(t, u):
                pe.wait_ge(exp_ready, t + 1)
                for g in range(HG):
                    for j in range(4):
                        mm = pe.transpose(ps[:, 4 * u + g, j * P:(j + 1) * P], p[:, u, j, g], ident)
                    mm.then_inc(pt_ps, 1)

            def weigh(t, u):
                pe.wait_ge(pt_act, 2 * t + 2)
                pe.wait_ge(pt_dve, t + 1)
                for h in range(NH):
                    mm = pe.matmul(ps[:, 4 * u + 3, h * (HD + 1):(h + 1) * (HD + 1)],
                                   pt[:, u, h // 4, (h % 4) * P:(h % 4 + 1) * P], v1[:, u, h], start=True, stop=True)
                mm.then_inc(av_ps, 1)

            def turn_values(t, u):
                pe.wait_ge(av_ready, t + 1)
                for c in range(2):
                    mm = pe.transpose(ps[0:DH, 4 * u, c * P:(c + 1) * P], av[:, u, c * DH:(c + 1) * DH], ident)
                mm.then_inc(avt_ps, 1)

            def output(t, u):
                pe.matmul(ps[0:T, 4 * u + 3, 0:D], cst[0:1, C_ONE:C_ONE + T], bo[:], start=True, stop=False)
                pe.wait_ge(avt_ready, t + 1)
                for c in range(2):
                    mm = pe.matmul(ps[0:T, 4 * u + 3, 0:D], avt[:, u, c, 0:T], wo[:, c], start=False, stop=c == 1)
                mm.then_inc(out_ps, 1)

            def turn(t, u, ahead=2):
                if ahead > 0:
                    project(t + 1, 1 - u)
                turn_probs(t, u)
                if ahead > 0:
                    scores(t + 1, 1 - u)
                weigh(t, u)
                turn_values(t, u)
                if ahead > 1:
                    turn_over(t + 2, u)
                output(t, u)

            turn_over(0, 0)
            turn_over(1, 1)
            project(0, 0)
            scores(0, 0)
            with pe.Fori(0, NB // U - 1) as it:
                for u in range(U):
                    turn(it * U + u, u)
            for u in range(U):
                turn(NB - U + u, u, 1 - u)

        @block.scalar
        def _(act):
            def turn_over(t, u):
                act.wait_ge(hnt_ps, t + 1)
                act.copy(hnt[:, u], ps[0:DH, 4 * u + 2, 0:2 * P].rearrange("p (c t) -> p c t", c=2)).then_inc(hnt_ready, 1)

            def queries(t, u):
                act.wait_ge(qk_ps, 2 * t + 1)
                act.copy(qt[:, u], ps[:, 4 * u + 1, 0:HG * P]).then_inc(q_ready, 1)

            def exponentials(t, u):
                for j in range(4):
                    act.wait_ge(shifted, 4 * t + j + 1)
                    ins = act.activation(p[:, u, j], p[:, u, j], ACT.Exp, scale=HD ** -0.5)
                ins.then_inc(exp_ready, 1)

            def probs(t, u):
                for g in (0, 2):
                    act.wait_ge(pt_ps, 3 * t + g + 1)
                    act.copy(pt[:, u, g], ps[:, 4 * u + g]).then_inc(pt_act, 1)

            def values(t, u):
                act.wait_ge(avt_ps, t + 1)
                act.copy(avt[:, u], ps[0:DH, 4 * u, 0:2 * P].rearrange("p (c t) -> p c t", c=2)).then_inc(avt_ready, 1)

            def turn(t, u, ahead=2):
                if ahead > 0:
                    queries(t + 1, 1 - u)
                probs(t, u)
                values(t, u)
                if ahead > 1:
                    turn_over(t + 2, u)
                if ahead > 0:
                    exponentials(t + 1, 1 - u)

            turn_over(0, 0)
            turn_over(1, 1)
            queries(0, 0)
            exponentials(0, 0)
            with act.Fori(0, NB // U - 1) as it:
                for u in range(U):
                    turn(it * U + u, u)
            for u in range(U):
                turn(NB - U + u, u, 1 - u)

        @block.vector
        def _(dve):
            link = Link(dve, chain)
            dve.memset(v1[:], 1.0).then_inc(ones_ready, 1)
            dve.tensor_copy(caus[:], cst[:, C_CAUS:C_CAUS + HG * P]).then_inc(ones_ready, 1)
            dve.wait_ge(ones_ready, 2)
            dve.memset(hn[0:1, 0, 0:1], 0.0).then_inc(added, 2)

            def normalise(t, u):
                dve.tensor_scalar(hn[:, u], resid[:, bass.ds(t * D, D)], mean[:, bass.ds(t, 1)],
                                  rstd[:, bass.ds(t, 1)], ALU.subtract, ALU.mult).then_inc(hn_ready, 1)

            def keys_values(t, u):
                dve.wait_ge(qk_ps, 2 * t + 2)
                dve.tensor_copy(kt[:, u], ps[:, 4 * u + 2, 0:HG * P]).then_inc(kv_ready, 1)
                dve.wait_ge(v_ps, t + 1)
                dve.tensor_copy(v1[:, u, :, 0:HD], ps[:, 4 * u + 3, 0:D].rearrange("p (h d) -> p h d", h=NH))\
                   .then_inc(kv_ready, 1)

            def score(u, j):
                return ps[:, 4 * u + j, 0:HG * P].rearrange("p (g k) -> p g k", g=HG)

            def maxima(t, u):
                dve.wait_ge(score_ps, t + 1)
                for j in range(4):
                    ins = dve.tensor_reduce(mx[:, u, j], score(u, j), AX.X, ALU.max)
                ins.then_inc(max_ready, 1)

            def shift(t, u):
                dve.wait_ge(max_ready, t + 1)
                for j in range(4):
                    dve.tensor_tensor(p[:, u, j], score(u, j), mx[:, u, j].unsqueeze(2).to_broadcast([P, HG, P]),
                                      ALU.subtract).then_inc(shifted, 1)

            def probs(t, u):
                dve.wait_ge(pt_ps, 3 * t + 2)
                dve.tensor_copy(pt[:, u, 1], ps[:, 4 * u + 1]).then_inc(pt_dve, 1)

            def values(t, u):
                dve.wait_ge(av_ps, t + 1)
                o = ps[:, 4 * u + 3, 0:NH * (HD + 1)].rearrange("p (h d) -> p h d", h=NH)
                link.done(dve.reciprocal(rec[:, u], o[:, :, HD]))
                dve.tensor_tensor(av[:, u].rearrange("p (h d) -> p h d", h=NH), o[:, :, 0:HD],
                                  rec[:, u].unsqueeze(2).to_broadcast([P, NH, HD]), ALU.mult).then_inc(av_ready, 1)

            def add(t, u):
                dve.wait_ge(out_ps, t + 1)
                h = resid[0:T, bass.ds(t * D, D)]
                dve.tensor_tensor(h, h, ps[0:T, 4 * u + 3, 0:D], ALU.add).then_inc(added, 1)

            def turn(t, u, ahead=2):
                if ahead > 1:
                    normalise(t + 2, u)
                if ahead > 0:
                    keys_values(t + 1, 1 - u)
                probs(t, u)
                if ahead > 0:
                    maxima(t + 1, 1 - u)
                values(t, u)
                if ahead > 0:
                    shift(t + 1, 1 - u)
                add(t, u)

            dve.wait_ge(added, 2)
            for u in range(U):
                normalise(u, u)
            keys_values(0, 0)
            maxima(0, 0)
            shift(0, 0)
            with dve.Fori(0, NB // U - 1) as it:
                link.loop(it, U)
                for u in range(U):
                    turn(it * U + u, u)
            link.end(NB // U - 1)
            for u in range(U):
                turn(NB - U + u, u, 1 - u)
            dve.wait_ge(added, NB + 2)


def expert_ffn(nc, gate_d, w1_d, b2_d, w2_d, bits_d, cst, cstb, resid, mean, rstd, out):
    with ExitStack() as ctx:
        def sb(name, shape, dt=F32):
            return ctx.enter_context(nc.sbuf_tensor("mo_" + name, shape, dt))

        take = ctx.enter_context(semaphores(nc))
        rows_x = nc.dram_tensor("rows_x", (NB * T + P, D + NX), F32, kind="Internal").ap()
        rows_y = nc.dram_tensor("rows_y", (NB * T + P, D), F32, kind="Internal").ap()
        w1 = sb("w1", [DH + 1, NX * 2 * HID])
        w2 = sb("w2", [P, NX * HC * D])
        b2 = sb("b2", [P, NX * D])
        score = sb("score", [P, NX, NB])
        row_of = sb("row_of", [P, NBLK1], I32)
        block_expert = sb("block_expert", [1, NBLK1], I32)
        weights_in = take("weights_in")
        gate_scores(nc, gate_d, ((w1, w1_d), (w2, w2_d), (b2, b2_d)), weights_in, cst, resid, mean, rstd, score,
                    rows_x, rows_y)
        pick_pairs(nc, bits_d, cst, cstb, score, row_of, block_expert)
        run_experts(nc, cst, w1, w2, b2, weights_in, row_of, block_expert, rows_x, rows_y, out)


def gate_scores(nc, gate_d, weights, weights_in, cst, resid, mean, rstd, score, rows_x, rows_y):
    U = 4
    with ExitStack() as ctx:
        take = ctx.enter_context(semaphores(nc))

        def sb(name, shape, dt=F32):
            return ctx.enter_context(nc.sbuf_tensor("ga_" + name, shape, dt))

        gate = sb("gate", [DH, 2, NX])
        hn, hnt = sb("hn", [P, U, D]), sb("hnt", [DH, U, 2, P])
        logit = sb("logit", [P, NX, NB])
        mx, z, rz = sb("mx", [P, NB]), sb("z", [P, NB]), sb("rz", [P, NB])
        by_token = sb("by_token", [P, NB, NX])
        zeros = sb("zeros", [P, D + NX])
        pa = ctx.enter_context(nc.psum_tensor("ga_pa", [P, U, 512], F32))
        pb = ctx.enter_context(nc.psum_tensor("ga_pb", [P, U, 512], F32))
        w_in, hn_ready, hnt_ps, hnt_ready = take("ga_w_in"), take("ga_hn_ready"), take("ga_hnt_ps"), take("ga_hnt_ready")
        logit_ps, chain, shifted, exp_ready = take("ga_logit_ps"), take("ga_chain"), take("ga_shifted"), take("ga_exp")
        score_ready, cleared, tables = take("ga_score_ready"), take("ga_cleared"), take("ga_tables")
        hn_stored = [take(f"ga_hn_stored{u}") for u in range(U)]
        block = ctx.enter_context(nc.Block())

        @block.sync
        def _(sp):
            sp.dma_start(gate[:], gate_d).then_inc(w_in, 16)
            sp.dma_start(rows_y[0:NB * T].rearrange("(b t) d -> t b d", t=T),
                         resid[0:T, :].rearrange("t (b d) -> t b d", b=NB)).then_inc(tables, 16)
            sp.wait_ge(cleared, 1)
            sp.dma_start(rows_y[NB * T:NB * T + P], zeros[:, 0:D]).then_inc(tables, 16)
            sp.dma_start(rows_x[NB * T:NB * T + P], zeros[:]).then_inc(tables, 16)
            with sp.Fori(0, NB // U) as it:
                for u in range(U):
                    sp.wait_ge(hn_ready, it * U + u + 1)
                    sp.dma_start(rows_x[bass.ds((it * U + u) * T, T), 0:D], hn[0:T, u]).then_inc(hn_stored[u], 16)
            sp.wait_ge(score_ready, 1)
            sp.dma_start(rows_x[0:NB * T, D:D + NX].rearrange("(b t) e -> t b e", t=T), by_token[0:T])\
              .then_inc(tables, 16)
            for dst, src in weights:
                sp.dma_start(dst[:], src).then_inc(weights_in, 16)
            sp.wait_ge(tables, 4 * 16)
            for u in range(U):
                sp.wait_ge(hn_stored[u], 16 * (NB // U + 1))

        @block.tensor
        def _(pe):
            ident = cst[:, C_ID:C_ID + P]
            pe.wait_ge(w_in, 16)
            with pe.Fori(0, NB // U) as it:
                for u in range(U):
                    pe.wait_ge(hn_ready, it * U + u + 1)
                    for c in range(2):
                        mm = pe.transpose(pa[0:DH, u, c * P:(c + 1) * P], hn[:, u, c * DH:(c + 1) * DH], ident)
                    mm.then_inc(hnt_ps, 1)
                for u in range(U):
                    pe.wait_ge(hnt_ready, it * U + u + 1)
                    for c in range(2):
                        mm = pe.matmul(pb[:, u, 0:NX], hnt[:, u, c], gate[:, c], start=c == 0, stop=c == 1)
                    mm.then_inc(logit_ps, 1)

        @block.scalar
        def _(act):
            with act.Fori(0, NB // U) as it:
                for u in range(U):
                    act.wait_ge(hnt_ps, it * U + u + 1)
                    act.copy(hnt[:, u], pa[0:DH, u, 0:2 * P].rearrange("p (c t) -> p c t", c=2)).then_inc(hnt_ready, 1)
            act.wait_ge(shifted, 1)
            act.activation(logit[:], logit[:], ACT.Exp).then_inc(exp_ready, 1)

        @block.vector
        def _(dve):
            link = Link(dve, chain)
            dve.memset(zeros[:], 0.0).then_inc(cleared, 1)
            for u in range(U):
                dve.memset(hn[:, u], 0.0).then_inc(hn_stored[u], 16)
            with dve.Fori(0, NB // U) as it:
                link.loop(it, U)
                for u in range(U):
                    b = it * U + u
                    dve.wait_ge(hn_stored[u], 16 * it + 16)
                    dve.tensor_scalar(hn[:, u], resid[:, bass.ds(b * D, D)], mean[:, bass.ds(b, 1)],
                                      rstd[:, bass.ds(b, 1)], ALU.subtract, ALU.mult).then_inc(hn_ready, 1)
                for u in range(U):
                    b = it * U + u
                    dve.wait_ge(logit_ps, it * U + u + 1)
                    link.done(dve.tensor_copy(logit[:, :, bass.ds(b, 1)], pb[:, u, 0:NX].unsqueeze(2)))
            link.end(NB // U)
            by_e = "p e b -> p b e"
            link.done(dve.tensor_reduce(mx[:], logit[:].rearrange(by_e), AX.X, ALU.max))
            dve.tensor_tensor(logit[:], logit[:], mx[:].unsqueeze(1).to_broadcast([P, NX, NB]), ALU.subtract)\
               .then_inc(shifted, 1)
            dve.wait_ge(exp_ready, 1)
            link.done(dve.tensor_reduce(z[:], logit[:].rearrange(by_e), AX.X, ALU.add))
            link.done(dve.reciprocal(rz[:], z[:]))
            link.done(dve.tensor_tensor(score[:], logit[:], rz[:].unsqueeze(1).to_broadcast([P, NX, NB]), ALU.mult))
            dve.tensor_copy(by_token[:], score[:].rearrange(by_e)).then_inc(score_ready, 1)
            dve.wait_ge(score_ready, 1)
            link.done(dve.tensor_scalar(score[:], score[:], cst[:, C_VALID:C_VALID + 1], cst[:, C_VM1:C_VM1 + 1],
                                        ALU.mult, ALU.add))


def pick_pairs(nc, bits_d, cst, cstb, score, row_of, block_expert):
    NC = NX * NB
    BITS = 30
    W = 8
    with ExitStack() as ctx:
        take = ctx.enter_context(semaphores(nc))

        def sb(name, shape, dt=F32):
            return ctx.enter_context(nc.sbuf_tensor("pk_" + name, shape, dt))

        bits = sb("bits", [P, BITS], I32)
        found, cand = sb("found", [P, 1], I32), sb("cand", [P, 1], I32)
        hits, cnt, enough = sb("hits", [P, NC]), sb("cnt", [P, 1]), sb("enough", [P, 1])
        above, tie = sb("above", [P, NC]), sb("tie", [P, NC])
        mask_b = sb("mask_b", [P, 2, NC], BF16)
        ones = sb("ones", [P, NC])
        incl, rank, left, kept = sb("incl", [P, NC]), sb("rank", [P, NC]), sb("left", [P, 1]), sb("kept", [P, NC])
        cntx, inclx, startx = sb("cntx", [P, NX]), sb("inclx", [P, NX]), sb("startx", [P, NX])
        ceil_i, blk_i, blk = sb("ceil_i", [P, NX], I32), sb("blk_i", [P, NX], I32), sb("blk", [P, NX])
        iblk, shift = sb("iblk", [P, NX]), sb("shift", [P, NX])
        slot, slot_i, q_i, p_i = sb("slot", [P, NC]), sb("slot_i", [P, NC], I32), sb("q_i", [P, NC], I32), sb("p_i", [P, NC], I32)
        qf, pf = sb("qf", [P, NC]), sb("pf", [P, NC])
        row1 = sb("row1", [P, NC])
        past, nblk = sb("past", [1, NBLK1, NX]), sb("nblk", [1, NBLK1])
        hot_p, hot_q = sb("hot_p", [P, W, P]), sb("hot_q", [P, W, NBLK1])
        listed, empty = sb("listed", [P, NBLK1]), sb("empty", [P, NBLK1])
        ps = ctx.enter_context(nc.psum_tensor("pk_ps", [P, 4, 512], F32))
        bits_in, chain, counted, total_ps = take("pk_bits_in"), take("pk_chain"), take("pk_counted"), take("pk_total_ps")
        mask_ready, prefix_ps, hot_ready, used = take("pk_mask_ready"), take("pk_prefix_ps"), take("pk_hot"), take("pk_used")
        listed_ps = take("pk_listed_ps")
        block = ctx.enter_context(nc.Block())
        dummy = cst[:, C_DUMMY:C_DUMMY + 1]

        @block.sync
        def _(sp):
            sp.dma_start(bits[:], bits_d).then_inc(bits_in, 16)
            sp.wait_ge(bits_in, 16)

        @block.tensor
        def _(pe):
            with pe.Fori(0, BITS) as i:
                pe.wait_ge(counted, i + 1)
                pe.matmul(ps[:, 0, 0:1], cst[:, C_ONE:C_ONE + P], cnt[:], start=True, stop=True).then_inc(total_ps, 1)
            pe.wait_ge(counted, BITS + 1)
            pe.matmul(ps[:, 0, 0:1], cst[:, C_ONE:C_ONE + P], cnt[:], start=True, stop=True).then_inc(total_ps, 1)
            for n in range(2):
                pe.wait_ge(mask_ready, n + 1)
                pe.matmul(ps[:, 1, 0:NC], cstb[:, 1], mask_b[:, n], start=True, stop=True)
                pe.matmul(ps[:, 2, 0:NC], cstb[:, 3], mask_b[:, n], start=True, stop=True).then_inc(prefix_ps, 1)

            def column(it, w, first, last):
                pe.wait_ge(hot_ready, 2 * (it * W + w) + 2)
                pe.matmul(ps[:, 3, 0:NBLK1], hot_p[:, w], hot_q[:, w], start=first, stop=last).then_inc(used, 1)

            for w in range(W):
                column(0, w, w == 0, False)
            with pe.Fori(1, NC // W - 1) as it:
                for w in range(W):
                    column(it, w, False, False)
            for w in range(W):
                column(NC // W - 1, w, False, w == W - 1)

        @block.vector
        def _(dve):
            link = Link(dve, chain)
            s = score[:].rearrange("p e b -> p (e b)")
            by_e = "p (e b) -> p e b"
            dve.memset(ones[:], 1.0)
            link.done(dve.memset(found[:], 0))
            dve.wait_ge(bits_in, 16)
            with dve.Fori(0, BITS) as i:
                link.loop(i, 3)
                link.done(dve.tensor_tensor(cand[:], found[:], bits[:, bass.ds(i, 1)], ALU.bitwise_or))
                dve.tensor_scalar(hits[:], s, cand[:].bitcast(F32), None, ALU.is_ge, ALU.add, accum_out=cnt[:])\
                   .then_inc(counted, 1)
                dve.wait_ge(total_ps, i + 1)
                link.done(dve.tensor_scalar(enough[:], ps[:, 0, 0:1], float(K1), None, ALU.is_ge))
                link.done(dve.scalar_tensor_tensor(found[:].bitcast(F32), cand[:].bitcast(F32), enough[:],
                                                   found[:].bitcast(F32), ALU.mult, ALU.max))
            link.end(BITS)
            kth = found[:].bitcast(F32)
            dve.tensor_scalar(above[:], s, kth, None, ALU.is_gt, ALU.add, accum_out=cnt[:]).then_inc(counted, 1)
            link.done(dve.tensor_scalar(tie[:], s, kth, None, ALU.is_equal))
            dve.tensor_copy(mask_b[:, 0], tie[:]).then_inc(mask_ready, 1)
            dve.wait_ge(total_ps, BITS + 1)
            link.done(dve.tensor_scalar(left[:], ps[:, 0, 0:1], -1.0, float(K1), ALU.mult, ALU.add))

            def prefix(n):
                dve.wait_ge(prefix_ps, n + 1)
                link.done(dve.tensor_tensor_scan(incl[:], ones[:], ps[:, 1, 0:NC], 0.0, ALU.mult, ALU.add))
                link.done(dve.tensor_tensor(rank[:], incl[:], ps[:, 1, 0:NC], ALU.subtract))
                link.done(dve.tensor_tensor(rank[:], rank[:], ps[:, 2, 0:NC], ALU.add))

            prefix(0)
            link.done(dve.scalar_tensor_tensor(kept[:], rank[:], left[:], tie[:], ALU.is_lt, ALU.mult))
            link.done(dve.tensor_tensor(kept[:], kept[:], above[:], ALU.add))
            dve.tensor_copy(mask_b[:, 1], kept[:]).then_inc(mask_ready, 1)
            prefix(1)
            link.done(dve.tensor_reduce(cntx[:], ps[:, 1, 0:NC].rearrange(by_e, e=NX), AX.X, ALU.add))
            link.done(dve.tensor_tensor_scan(inclx[:], ones[:, 0:NX], cntx[:], 0.0, ALU.mult, ALU.add))
            link.done(dve.tensor_tensor(startx[:], inclx[:], cntx[:], ALU.subtract))
            link.done(dve.tensor_scalar(ceil_i[:], cntx[:], P - 1.0, None, ALU.add))
            link.done(dve.tensor_scalar(blk_i[:], ceil_i[:], 7, None, ALU.arith_shift_right))
            link.done(dve.tensor_copy(blk[:], blk_i[:]))
            link.done(dve.tensor_tensor_scan(iblk[:], ones[:, 0:NX], blk[:], 0.0, ALU.mult, ALU.add))
            link.done(dve.tensor_tensor(shift[:], iblk[:], blk[:], ALU.subtract))
            link.done(dve.scalar_tensor_tensor(shift[:], shift[:], float(P), startx[:], ALU.mult, ALU.subtract))
            link.done(dve.tensor_tensor(slot[:].rearrange(by_e, e=NX), rank[:].rearrange(by_e, e=NX),
                                        shift[:].unsqueeze(2).to_broadcast([P, NX, NB]), ALU.add))
            link.done(dve.scalar_tensor_tensor(slot[:], slot[:], 1.0, kept[:], ALU.add, ALU.mult))
            link.done(dve.tensor_scalar(slot_i[:], slot[:], -1.0, None, ALU.add))
            link.done(dve.tensor_scalar(q_i[:], slot_i[:], 7, None, ALU.arith_shift_right))
            link.done(dve.tensor_scalar(p_i[:], slot_i[:], P - 1, None, ALU.bitwise_and))
            link.done(dve.tensor_copy(qf[:], q_i[:]))
            link.done(dve.tensor_copy(pf[:], p_i[:]))
            link.done(dve.tensor_scalar(row1[:].rearrange(by_e, e=NX),
                                        cst[:, C_IOTA:C_IOTA + NB].unsqueeze(1).to_broadcast([P, NX, NB]),
                                        float(T), cst[:, C_ROW1:C_ROW1 + 1], ALU.mult, ALU.add))
            link.done(dve.tensor_tensor(past[:], cst[0:1, C_IOTA:C_IOTA + NBLK1].unsqueeze(2).to_broadcast([1, NBLK1, NX]),
                                        iblk[0:1, :].unsqueeze(1).to_broadcast([1, NBLK1, NX]), ALU.is_ge))
            link.done(dve.tensor_reduce(nblk[:], past[:], AX.X, ALU.add))
            link.done(dve.tensor_scalar(block_expert[:], nblk[:], NX - 1.0, None, ALU.min))

            def column(it, w, first):
                k = it * W + w
                if not first:
                    dve.wait_ge(used, k - W + 1)
                dve.tensor_scalar(hot_p[:, w], cst[:, C_IOTA:C_IOTA + P], pf[:, bass.ds(k, 1)], None, ALU.is_equal)\
                   .then_inc(hot_ready, 1)
                dve.tensor_scalar(hot_q[:, w], cst[:, C_IOTA:C_IOTA + NBLK1], qf[:, bass.ds(k, 1)],
                                  row1[:, bass.ds(k, 1)], ALU.is_equal, ALU.mult).then_inc(hot_ready, 1)

            for w in range(W):
                column(0, w, True)
            with dve.Fori(1, NC // W) as it:
                for w in range(W):
                    column(it, w, False)
            dve.wait_ge(used, NC)
            link.done(dve.tensor_scalar(empty[:], ps[:, 3, 0:NBLK1], 0.0, dummy, ALU.is_equal, ALU.mult))
            link.done(dve.scalar_tensor_tensor(row_of[:], ps[:, 3, 0:NBLK1], -1.0, empty[:], ALU.add, ALU.add))


def run_experts(nc, cst, w1, w2, b2, weights_in, row_of, block_expert, rows_x, rows_y, out):
    W = 4
    TURNS = NBLK1 // W
    HH = HID // 2
    with ExitStack() as ctx:
        take = ctx.enter_context(semaphores(nc))

        def sb(name, shape, dt=F32):
            return ctx.enter_context(nc.sbuf_tensor("ex_" + name, shape, dt))

        x = sb("x", [P, W, D + NX])
        xt = sb("xt", [DH + 1, 2, 2, P])
        h = sb("h", [P, 2, HID])
        ht = sb("ht", [P, 2, HID])
        yb = sb("yb", [P, W, D])
        y = sb("y", [P, W, D])
        xt_ps = ctx.enter_context(nc.psum_tensor("ex_xt_ps", [P, 2, 512], F32))
        h_ps = ctx.enter_context(nc.psum_tensor("ex_h_ps", [P, 2, 512], F32))
        ht_ps = ctx.enter_context(nc.psum_tensor("ex_ht_ps", [P, 2, 512], F32))
        y_ps = ctx.enter_context(nc.psum_tensor("ex_y_ps", [P, 1, 512], F32))
        x_t, xt_ready, h_done, gelu_ready = take("ex_x_t"), take("ex_xt_ready"), take("ex_h_done"), take("ex_gelu")
        h_t, ht_act, ht_dve, y_done = take("ex_h_t"), take("ex_ht_act"), take("ex_ht_dve"), take("ex_y_done")
        y_read, y_ready, ones_ready, stored = take("ex_y_read"), take("ex_y_ready"), take("ex_ones"), take("ex_stored")
        gathered = [take(f"ex_gathered{u}") for u in range(W)]
        added = [take(f"ex_added{u}") for u in range(W)]
        block = ctx.enter_context(nc.Block())

        @block.gpsimd
        def _(pool):
            last = pool.to_reg(NB * T + P - 1)

            def gather(t):
                if t >= W:
                    pool.wait_ge(y_ready, t - W + 1)
                pool.indirect_dma_start(x[:, t % W], None, rows_x, bass.IndirectOffsetOnAxis(row_of[:, t:t + 1], 0),
                                        bounds_check=last, oob_is_err=True).then_inc(gathered[t % W], 16)

            for t in range(W - 1):
                gather(t)
            for t in range(NBLK1):
                if t + W - 1 < NBLK1:
                    gather(t + W - 1)
                pool.wait_ge(y_ready, t + 1)
                if t:
                    pool.wait_ge(added[(t - 1) % W], 16 * ((t - 1) // W + 1))
                pool.indirect_dma_start(rows_y, bass.IndirectOffsetOnAxis(row_of[:, t:t + 1], 0), y[:, t % W], None,
                                        bounds_check=last, oob_is_err=True, compute_op=ALU.add)\
                    .then_inc(added[t % W], 16)
            for u in range(W):
                pool.wait_ge(added[u], 16 * TURNS)
            pool.dma_start(out.rearrange("b t d -> (b t) d"), rows_y[0:NB * T]).then_inc(stored, 16)
            pool.wait_ge(stored, 16)

        @block.tensor
        def _(pe):
            ident = cst[:, C_ID:C_ID + P]
            pe.wait_ge(weights_in, 3 * 16)
            pe.wait_ge(ones_ready, 1)

            def experts(it, n):
                return load_experts(nc, mybir.EngineType.PE, block_expert[0:1, bass.ds(it * W, n)], NX - 1)

            def turn_over(it, u):
                pe.wait_ge(gathered[u], 16 * it + 16)
                for c in range(2):
                    mm = pe.transpose(xt_ps[0:DH, u % 2, c * P:(c + 1) * P], x[:, u, c * DH:(c + 1) * DH], ident)
                mm.then_inc(x_t, 1)

            def hidden(it, u, e):
                t = it * W + u
                pe.wait_ge(xt_ready, t + 1)
                for n in range(2):
                    for c in range(2):
                        k = DH + c
                        mm = pe.matmul(h_ps[:, n, 0:HH], xt[0:k, u % 2, c],
                                       w1[0:k, bass.ds(e * (2 * HID) + c * HID + n * HH, HH)],
                                       start=c == 0, stop=c == 1)
                    mm.then_inc(h_done, 1)

            def turn_hidden(it, u):
                t = it * W + u
                for n in range(2):
                    pe.wait_ge(gelu_ready, 2 * t + n + 1)
                    for k in range(3):
                        mm = pe.transpose(ht_ps[:, n, k * P:(k + 1) * P],
                                          h[:, u % 2, n * HH + k * P:n * HH + (k + 1) * P], ident)
                    mm.then_inc(h_t, 1)

            def output(it, u, e):
                t = it * W + u
                pe.wait_ge(y_read, t + 1)
                pe.wait_ge(ht_act, t + 1)
                pe.wait_ge(ht_dve, t + 1)
                for k in range(HC):
                    mm = pe.matmul(y_ps[:, 0, 0:D], ht[:, u % 2, k * P:(k + 1) * P],
                                   w2[:, bass.ds(e * (HC * D) + k * D, D)], start=k == 0, stop=k == HC - 1)
                mm.then_inc(y_done, 1)

            def turn(it, u, es, left=2):
                turn_hidden(it, u)
                if left > 1:
                    turn_over(it + (u + 2) // W, (u + 2) % W)
                if left > 0:
                    hidden(it + (u + 1) // W, (u + 1) % W, es[u + 1])
                output(it, u, es[u])

            turn_over(0, 0)
            turn_over(0, 1)
            hidden(0, 0, experts(0, 1)[0])
            with pe.Fori(0, TURNS - 1) as it:
                es = experts(it, W) + experts(it + 1, 1)
                for u in range(W):
                    turn(it, u, es)
            es = experts(TURNS - 1, W)
            for u in range(W):
                turn(TURNS - 1, u, es, W - 1 - u)

        @block.scalar
        def _(act):
            def turn_over(it, u):
                act.wait_ge(x_t, it * W + u + 1)
                act.copy(xt[0:DH, u % 2], xt_ps[0:DH, u % 2, 0:2 * P].rearrange("p (c t) -> p c t", c=2)).then_inc(xt_ready, 1)

            def hidden(it, u):
                for n in range(2):
                    act.wait_ge(h_done, 2 * (it * W + u) + n + 1)
                    act.activation(h[:, u % 2, n * HH:(n + 1) * HH], h_ps[:, n, 0:HH],
                                   ACT.Gelu_apprx_tanh).then_inc(gelu_ready, 1)

            def turn_hidden(it, u):
                act.wait_ge(h_t, 2 * (it * W + u) + 1)
                act.copy(ht[:, u % 2, 0:HH], ht_ps[:, 0, 0:HH]).then_inc(ht_act, 1)

            def turn(it, u, left=2):
                turn_hidden(it, u)
                if left > 1:
                    turn_over(it + (u + 2) // W, (u + 2) % W)
                if left > 0:
                    hidden(it + (u + 1) // W, (u + 1) % W)

            act.wait_ge(ones_ready, 1)
            turn_over(0, 0)
            turn_over(0, 1)
            hidden(0, 0)
            with act.Fori(0, TURNS - 1) as it:
                for u in range(W):
                    turn(it, u)
            for u in range(W):
                turn(TURNS - 1, u, W - 1 - u)

        @block.vector
        def _(dve):
            dve.memset(xt[DH:DH + 1], 1.0).then_inc(ones_ready, 1)
            dve.memset(yb[0:1, 0, 0:1], 0.0).then_inc(y_read, 1)
            dve.wait_ge(weights_in, 3 * 16)

            def turn(it, first):
                es = load_experts(nc, mybir.EngineType.DVE, block_expert[0:1, bass.ds(it * W, W)], NX - 1)
                for u in range(W):
                    t, e = it * W + u, es[u]
                    dve.wait_ge(h_t, 2 * t + 2)
                    dve.tensor_copy(ht[:, u % 2, HH:HID], ht_ps[:, 1, 0:HH]).then_inc(ht_dve, 1)
                    dve.wait_ge(y_done, t + 1)
                    dve.tensor_tensor(yb[:, u], y_ps[:, 0, 0:D], b2[:, bass.ds(e * D, D)], ALU.add).then_inc(y_read, 1)
                    dve.wait_ge(y_read, t + 2)
                    if not first:
                        dve.wait_ge(added[u], 16 * it)
                    dve.tensor_scalar(y[:, u], yb[:, u], x[:, u, bass.ds(e + D, 1)], None, ALU.mult)\
                       .then_inc(y_ready, 1)

            turn(0, True)
            with dve.Fori(1, TURNS) as it:
                turn(it, False)


def _consts():
    c = np.zeros((P, C_END), np.float32)
    i = np.arange(P)
    c[:, C_ID:C_ID + P] = np.eye(P)
    c[:, C_ONE:C_ONE + P] = 1
    c[:, C_TRS:C_TRS + P] = i[:, None] < i[None, :]
    c[:, C_TRI:C_TRI + P] = i[:, None] <= i[None, :]
    c[:, C_IOTA:C_IOTA + 256] = np.arange(256)
    c[:, C_CAUS:C_CAUS + 3 * P] = np.tile(np.where(i[None, :] > i[:, None], NEG, 0), (1, 3))
    c[:DH, C_BLKM:C_BLKM + DH] = np.where(i[:DH, None] // 24 == i[None, :DH] // 24, 0, NEG)
    m = np.zeros((2, 16, 2, 16))
    m += 1
    m.reshape(32, 32)[8:24, 8:24] = 2
    for a in range(2):
        for b in range(2):
            for ch in range(NCH):
                y = 8 * (ch % 2)
                c[:, C_MULT + (2 * a + b) * NCH + ch] = m[a, y:y + 8, b].reshape(P)
    c[:, C_EPS] = LN_EPS
    c[:, C_VALID] = i < T
    c[:, C_FAR] = np.where(i < T, 0, FAR)
    c[:, C_SENT:C_SENT + 4] = [-1, -2, -3, -4]
    c[:, C_NHALF] = -0.5
    c[:, C_VM1] = c[:, C_VALID] - 1
    c[:, C_DUMMY] = NB * T + i + 1
    c[:, C_ROW1] = i + 1
    return c


def _blocks(w):
    w = w.reshape(2, 2, 8, 2, 16, 3, -1)
    return np.ascontiguousarray(w.transpose(2, 4, 0, 3, 5, 1, 6).reshape(P, NK, -1))


def _windows(w):
    w = w.reshape(16, 16, 5, 3, -1)
    shifted = np.zeros((2, 16, 2, 16, 3, w.shape[-1]), w.dtype)
    for part, (a, b) in ((1, (0, 0)), (2, (1, 1)), (3, (0, 1)), (4, (1, 0))):
        shifted[a, :, b] = w[:, :, part]
    base = np.zeros((32, 32, 3, w.shape[-1]), w.dtype)
    base[8:24, 8:24] = w[:, :, 0]
    return _blocks(shifted), _blocks(base)


def kernel(**inputs):
    import concourse.bacc as bacc
    from concourse.bass_utils import run_bass_kernel_spmd as run

    a = {k: np.asarray(v) for k, v in inputs.items()}
    x = np.zeros((NGRP * GRP, 3, 112, 112), np.float32)
    x[:NB, :, 8:104, 8:104] = a["x"]
    x = x.reshape(NGRP, GRP, 3, BLK, 2, 8, BLK, 16).transpose(0, 5, 7, 2, 4, 1, 3, 6)
    feed = {"x_blocks": x.reshape(NGRP, P, NCH * GRP, BLK * BLK), "txt": a["txt"], "consts": _consts()}
    feed["w_shift"], feed["w_base"] = _windows(a["L0_tok_W"].T)
    for name, key in (("g", "L0_tok_ln_gamma"), ("b", "L0_tok_ln_beta")):
        s, b = _windows(a[key][:, None])
        feed[name + "_shift"], feed[name + "_base"] = s[:, :, 0], b[:, :, 0]
    feed["tok_b"] = a["L0_tok_b"][None]
    half = lambda w: w.reshape(2, DH, -1).transpose(1, 0, 2)
    w = a["L0_attn_W_qkv"]
    feed["wqk"] = half(np.concatenate([w[:, 0::3], w[:, 1::3]], 1))
    feed["wv"] = half(w[:, 2::3])
    feed["wp"] = half(a["L0_attn_W_proj"])
    feed["bp"] = a["L0_attn_b_proj"][None]
    feed["temp"] = np.broadcast_to(a["L0_attn_temp"].reshape(2, 4, 1), (2, 4, 24)).reshape(2, DH).T
    feed["emb"] = np.stack([a["L0_ffn_emb_fk"], a["L0_ffn_emb_rk"]], 1)
    feed["wcat"] = half(np.concatenate([a["L0_ffn_W_fk"], a["L0_ffn_W_rk"]], 1))
    feed["bcat"] = np.concatenate([a["L0_ffn_b_fk"], a["L0_ffn_b_rk"]])[:, None]
    feed["f_know"], feed["r_know"] = a["L0_ffn_f_know"], a["L0_ffn_r_know"]
    for name, key in (("wq1", "L1_attn_w_query"), ("wk1", "L1_attn_w_key")):
        w = np.zeros((D, 12, 32), np.float32)
        w[:, :, :16] = a[key].reshape(D, 12, 16)
        feed[name] = half(w.reshape(D, 3 * P))
    feed["wv1"], feed["wo1"], feed["bo1"] = half(a["L1_attn_w_value"]), half(a["L1_attn_w_out"]), a["L1_attn_b_out"][None]
    feed["gate_w"] = half(a["L1_ffn_gate_weight"].T)
    w1 = np.zeros((DH + 1, NX, 2, HID), np.float32)
    w1[:DH] = a["L1_ffn_w1"].reshape(NX, 2, DH, HID).transpose(2, 0, 1, 3)
    w1[DH, :, 1] = a["L1_ffn_b1"]
    feed["w1"] = w1.reshape(DH + 1, -1)
    feed["w2"] = a["L1_ffn_w2"].reshape(NX, HC, P, D).transpose(2, 0, 1, 3).reshape(P, -1)
    feed["b2"] = np.broadcast_to(a["L1_ffn_b2"].reshape(1, -1), (P, NX * D))
    feed["bits"] = np.broadcast_to(np.int32(1) << np.arange(29, -1, -1, dtype=np.int32), (P, 30))
    nc = bacc.Bacc("TRN2", target_bir_lowering=False, num_devices=1)
    feed = {k: np.ascontiguousarray(v) for k, v in feed.items()}
    aps = {k: nc.dram_tensor("in_" + k, v.shape, mybir.dt.from_np(v.dtype), kind="ExternalInput").ap()
           for k, v in feed.items()}
    out = nc.dram_tensor("out", (NB, T, D), F32, kind="ExternalOutput").ap()
    program(nc, **aps, out=out)
    r = run(nc, [{"in_" + k: v for k, v in feed.items()}], core_ids=[0])
    return r.results[0]["out"]
```

```python
from contextlib import ExitStack, contextmanager
import numpy as np
import concourse.bass as bass
from concourse import mybir

F32 = mybir.dt.float32
BF16 = mybir.dt.bfloat16
I32 = mybir.dt.int32
U32 = mybir.dt.uint32
ALU = mybir.AluOpType
ACT = mybir.ActivationFunctionType
AX = mybir.AxisListType

P = 128
NB = 32
TI, TT = 36, 77
T = TI + TT
D = 192
DH = D // 2
LN_EPS = 1e-5
NEG = -1e30

BLK = 7
NCH = 6
NK = 4 * NCH
PATCH_DIM = 3840
GRP = 3
GM = GRP * TI
NGRP = 11

NE, TOPK = 128, 4
R = 128
NBLK0 = (NB * T * TOPK + NE * (P - 1)) // P
GROUP = 4
KPARTS = 8

NX, HID = 8, 768
HC = HID // P
K1 = 2 * NB * T
NBLK1 = (K1 + NX * (P - 1)) // P
STEPS = 15
FAR = 1 << 20

(C_ID, C_ONE, C_TRS, C_TRI, C_IOTA, C_CAUS, C_BLKM, C_MULT, C_EPS, C_VALID, C_FAR, C_SENT, C_NHALF, C_VM1,
 C_DUMMY, C_ROW1, C_EVEN, C_ODD, C_END) = np.cumsum(
    [0, P, P, P, P, 256, P, DH, NK, 1, 1, 1, 4, 1, 1, 1, 1, 1, 1]).tolist()


@contextmanager
def semaphores(nc):
    taken = []

    def take(name):
        taken.append(nc.alloc_semaphore(name))
        return taken[-1]

    yield take
    nc.clear_and_free_semaphores(taken)
    nc.all_engine_barrier()


class Link:

    def __init__(self, eng, sem):
        self.eng, self.sem, self.base, self.n = eng, sem, 0, 0

    def done(self, ins):
        self.n += 1
        ins.then_inc(self.sem, 1)
        self.eng.wait_ge(self.sem, self.base + self.n)

    def loop(self, it, per):
        self.start, self.per, self.n, self.base = self.base + self.n, per, 0, self.base + self.n + it * per

    def end(self, turns):
        assert self.n == self.per, (self.n, self.per)
        self.base, self.n = self.start + turns * self.per, 0


def program(nc, x_blocks, txt, w_shift, w_base, g_shift, g_base, b_shift, b_base, tok_b,
            wqk, wv, wp, bp, temp, emb, wcat, bcat, f_know, r_know, wq1, wk1, wv1, wo1, gate_w, w1, b2, w2, bits, consts, out):
    with ExitStack() as top:
        resid = top.enter_context(nc.sbuf_tensor("resid", [P, NB * D], F32))
        cst = top.enter_context(nc.sbuf_tensor("cst", [P, C_END], F32))
        norm = Norm(nc, top, cst, resid)
        tok_rows = nc.dram_tensor("tok_rows", (NGRP * GRP * TI, D), F32, kind="Internal").ap()
        cstb = top.enter_context(nc.sbuf_tensor("cstb", [P, 4, P], BF16))
        slot_mem = nc.dram_tensor("slot_mem", (NBLK0 * P * D,), F32, kind="Internal").ap()
        embed_patches(nc, x_blocks, txt, w_shift, w_base, g_shift, g_base, b_shift, b_base, tok_b, consts,
                      cst, cstb, resid, tok_rows)
        channel_attention(nc, wqk, wv, wp, bp, temp, cst, resid, norm, slot_mem)
        sparse_ffn(nc, emb, wcat, bcat, f_know, r_know, cst, cstb, resid, norm, slot_mem)
        causal_attention(nc, wq1, wk1, wv1, wo1, cst, cstb, resid, norm)
        expert_ffn(nc, gate_w, w1, b2, w2, bits, cst, cstb, resid, norm, out)


def sparse_ffn(nc, emb, wcat, bcat, f_know, r_know, cst, cstb, resid, norm, slot_mem):
    with ExitStack() as ctx:
        def sb(name, shape, dt=F32):
            return ctx.enter_context(nc.sbuf_tensor("sf_" + name, shape, dt))

        take = ctx.enter_context(semaphores(nc))
        know = sb("know", [P, NE * 2 * R])
        embt = sb("embt", [P, 2 * NE])
        weight, index = sb("weight", [P, 2 * NB, 4]), sb("index", [P, 2 * NB, 4])
        slot = sb("slot", [P, NB, 8], I32)
        block_expert = sb("block_expert", [1, 2, 256], I32)
        know_in = [take("f_know_in"), take("r_know_in")]
        n = NBLK0 * P
        wide_rows = slot_mem.rearrange("(s d) -> s d", d=D)
        narrow_rows = slot_mem[0:n * R].rearrange("(s d) -> s d", d=R)
        feature_rows = nc.dram_tensor("feature_rows", (n, R), F32, kind="Internal").ap()
        restore_rows = nc.dram_tensor("restore_rows", (n, D), F32, kind="Internal").ap()
        with ExitStack() as routing:
            chosen = routing.enter_context(nc.sbuf_tensor("sf_chosen", [P, 2 * NB, NE], BF16))
            count = routing.enter_context(nc.sbuf_tensor("sf_count", [P, 2], F32))
            seg_start = routing.enter_context(nc.sbuf_tensor("sf_seg_start", [P, 2, P], BF16))
            route_tokens(nc, emb, wcat, bcat, cst, cstb, norm, embt, chosen, weight, index, count,
                         know, f_know, know_in[0])
            block_tables(nc, cst, cstb, count, seg_start, block_expert)
            place_tokens(nc, cst, cstb, norm, chosen, index, seg_start, slot, wide_rows)
        blocks_product(nc, "feature", cst, block_expert, 0, wide_rows, know, know_in[0], feature_rows, D, R)
        combine_rows(nc, "mid", slot, weight, 0, feature_rows, R, resid, norm, narrow_rows, know, r_know, know_in[1])
        blocks_product(nc, "restore", cst, block_expert, 1, narrow_rows, know, know_in[1], restore_rows, R, D)
        combine_rows(nc, "end", slot, weight, 1, restore_rows, D, resid, norm, None)


def embed_patches(nc, x_blocks, txt, w_shift, w_base, g_shift, g_base, b_shift, b_base, tok_b, consts,
                  cst, cstb, resid, tok_rows):
    with ExitStack() as ctx:
        take = ctx.enter_context(semaphores(nc))
        def sb(name, shape, dt=F32):
            return ctx.enter_context(nc.sbuf_tensor(name, shape, dt))

        def sem(name):
            return take(name)

        ws = sb("ws", [P, NK, D])
        wb = sb("wb", [P, NK, D])
        weff = sb("weff", [P, NK, D + 1])
        gain = sb("gain", [P, 4, NK])
        bias = sb("bias", [1, D])
        xg = sb("xg", [P, 2, NCH * GRP, BLK * BLK])
        xw = sb("xw", [P, 2, NK, GRP * TI])
        sq = sb("sq", [P, 2, NCH, GRP * BLK * BLK])
        sq3 = sb("sq3", [P, 2, 2, GRP * BLK * BLK])
        xsq = sb("xsq", [P, 2, 4 * 2, GRP * TI])
        wbg = sb("wbg", [P, NK, D])
        wsum = sb("wsum", [P, D])
        colsum = sb("colsum", [P, D])
        shift = sb("shift", [P, D])
        st = sb("st", [P, 2, 8])
        tok = sb("tok", [P, 2, D])
        rows = sb("rows", [P, 2, D])
        y_ps = ctx.enter_context(nc.psum_tensor("y_ps", [P, 2, 512], F32))
        q_ps = ctx.enter_context(nc.psum_tensor("q_ps", [P, 2, 512], F32))
        c_ps = ctx.enter_context(nc.psum_tensor("c_ps", [P, 2, 512], F32))
        ws_in, wb_in = sem("ws_in"), sem("wb_in")
        w_in, cst_in, txt_in, zeroed = sem("w_in"), sem("cst_in"), sem("txt_in"), sem("zeroed")
        x_in = [sem("x_in0"), sem("x_in1")]
        weff_ready, sums_ready, sums_out, products_done = (
            sem("weff_ready"), sem("sums_ready"), sem("sums_out"), sem("products_done"))
        sq_ready, sq3_ready, wsum_ready = sem("sq_ready"), sem("sq3_ready"), sem("wsum_ready")
        windows_ready, squared, var_ready, rstd_ready = sem("windows_ready"), sem("squared"), sem("var_ready"), sem("rstd_ready")
        tok_ready, tok_in, chain = sem("tok_ready"), sem("tok_in"), sem("chain")
        rows_stored = [sem("rows_stored0"), sem("rows_stored1")]
        eps_added, y_used = sem("eps_added"), sem("y_used")
        block = ctx.enter_context(nc.Block())

        @block.sync
        def _(sp):
            sp.dma_start(cst[:], consts).then_inc(cst_in, 16)
            for n, g in enumerate((g_shift, g_base, b_shift, b_base)):
                sp.dma_start(gain[:, n, :], g).then_inc(w_in, 16)
            sp.dma_start(bias[:], tok_b).then_inc(w_in, 16)
            sp.dma_start(ws[:], w_shift).then_inc(ws_in, 16)
            for u in range(2):
                sp.dma_start(xg[:, u], x_blocks[u]).then_inc(x_in[u], 16)
            sp.dma_start(wb[:], w_base).then_inc(wb_in, 16)

            def more(it, u):
                sp.wait_ge(windows_ready, 2 * it + u + 1)
                sp.wait_ge(sq_ready, 2 * it + u + 1)
                sp.dma_start(xg[:, u], x_blocks[bass.ds(2 * it + u + 2, 1)]).then_inc(x_in[u], 16)

            with sp.Fori(0, NGRP // 2 - 1) as it:
                for u in range(2):
                    more(it, u)
            more(NGRP // 2 - 1, 0)
            sp.wait_ge(rows_stored[0], 16 * (NGRP // 2 + 2))
            sp.wait_ge(rows_stored[1], 16 * (NGRP // 2 + 1))
            sp.wait_ge(zeroed, 1)
            sp.dma_start(resid[0:TI, :].rearrange("t (b d) -> t b d", b=NB),
                         tok_rows[0:NB * TI].rearrange("(b t) d -> t b d", t=TI)).then_inc(tok_in, 16)
            sp.wait_ge(tok_in, 16)
            sp.wait_ge(txt_in, 16)

        @block.gpsimd
        def _(pool):
            pool.memset(resid[:], 0.0).then_inc(zeroed, 1)
            pool.wait_ge(zeroed, 1)
            pool.dma_start(resid[TI:T, :].rearrange("t (b d) -> t b d", b=NB),
                           txt.rearrange("b t d -> t b d")).then_inc(txt_in, 16)
            pool.wait_ge(cst_in, 16)

            def inverse_deviation(it, u):
                s = st[0:GM, u]
                pool.wait_ge(var_ready, 2 * it + u + 1)
                pool.tensor_tensor(s[:, 3:4], s[:, 2:3], cst[0:GM, C_EPS:C_EPS + 1], ALU.add).then_inc(eps_added, 1)
                pool.wait_ge(eps_added, 2 * it + u + 1)
                pool.tensor_tensor(s[:, 4:5], s[:, 3:4], cst[0:GM, C_NHALF:C_NHALF + 1], ALU.pow).then_inc(rstd_ready, 1)

            with pool.Fori(0, NGRP // 2) as it:
                for u in range(2):
                    inverse_deviation(it, u)
            inverse_deviation(NGRP // 2, 0)

        def window(u, q):
            a, b = q // 2, q % 2
            return xg[:, u].rearrange("p g (i j) -> p g i j", i=BLK)[:, :, a:a + 6, b:b + 6]

        def windows(x, u, q):
            return x[:, u, q * NCH:(q + 1) * NCH].rearrange("p c (s i j) -> p (c s) i j", s=GRP, i=6)

        @block.vector
        def _(dve):
            link = Link(dve, chain)

            def lay_windows(it, u):
                dve.wait_ge(x_in[u], 16 * it + 16)
                for q in range(4):
                    ins = dve.tensor_copy(windows(xw, u, q), window(u, q))
                ins.then_inc(windows_ready, 1)

            def sum_colours(it, u):
                dve.wait_ge(sq_ready, 2 * it + u + 1)
                dve.tensor_reduce(sq3[:, u], sq[:, u].rearrange("p (c h) n -> p h n c", c=3), AX.X, ALU.add)\
                   .then_inc(sq3_ready, 1)

            def wide(n):
                return gain[:, n, :].unsqueeze(2).to_broadcast([P, NK, D])

            dve.wait_ge(w_in, 5 * 16)
            dve.wait_ge(ws_in, 16)
            dve.tensor_tensor(weff[:, :, 0:D], ws[:], wide(0), ALU.mult).then_inc(chain, 1)
            for u in range(2):
                lay_windows(0, u)
            for u in range(2):
                sum_colours(0, u)
            dve.wait_ge(wb_in, 16)
            dve.tensor_tensor(wbg[:], wb[:], wide(1), ALU.mult).then_inc(chain, 1)
            dve.wait_ge(chain, 2)
            dve.tensor_tensor(weff[:, :, 0:D], weff[:, :, 0:D], wbg[:], ALU.add).then_inc(weff_ready, 1)
            dve.wait_ge(cst_in, 16)
            dve.tensor_copy(weff[:, :, D], cst[:, C_MULT:C_MULT + NK]).then_inc(weff_ready, 1)
            link.base = 2
            dve.wait_ge(weff_ready, 2)
            dve.tensor_reduce(wsum[:], weff[:, :, 0:D].rearrange("p k d -> p d k"), AX.X, ALU.add).then_inc(wsum_ready, 1)
            dve.wait_ge(sums_ready, 1)
            dve.tensor_copy(shift[:], c_ps[:, 0, 0:D]).then_inc(sums_out, 1)
            dve.wait_ge(sums_ready, 2)
            dve.tensor_copy(colsum[:], c_ps[:, 1, 0:D]).then_inc(sums_out, 1)
            dve.wait_ge(sums_out, 2)

            for n, c in enumerate((C_ID, C_ONE, C_TRI, C_TRS)):
                dve.tensor_copy(cstb[:, n], cst[:, c:c + P])
            dve.memset(st[:, 0], 0.0).then_inc(y_used, 2)
            dve.wait_ge(y_used, 2)
            for u in range(2):
                dve.memset(rows[:, u], 0.0).then_inc(rows_stored[u], 16)

            def normalise(it, u):
                s = st[0:GM, u]
                dve.wait_ge(products_done, 2 * it + u + 1)
                link.done(dve.tensor_scalar(s[:, 0:1], y_ps[0:GM, u, D:D + 1], -1.0 / PATCH_DIM, None, ALU.mult))
                link.done(dve.tensor_tensor(s[:, 1:2], s[:, 0:1], s[:, 0:1], ALU.mult))
                dve.scalar_tensor_tensor(s[:, 2:3], q_ps[0:GM, u, 0:1], 1.0 / PATCH_DIM, s[:, 1:2],
                                         ALU.mult, ALU.subtract).then_inc(var_ready, 1)
                dve.scalar_tensor_tensor(tok[0:GM, u], colsum[0:GM], s[:, 0:1], y_ps[0:GM, u, 0:D],
                                         ALU.mult, ALU.add).then_inc(y_used, 1)
                dve.wait_ge(y_used, 2 * it + u + 3)
                dve.wait_ge(rstd_ready, 2 * it + u + 1)
                dve.wait_ge(rows_stored[u], 16 * it + 16)
                dve.scalar_tensor_tensor(rows[0:GM, u], tok[0:GM, u], s[:, 4:5], shift[0:GM], ALU.mult, ALU.add)\
                   .then_inc(tok_ready, 1)

            with dve.Fori(0, NGRP // 2 - 1) as it:
                link.loop(it, 4)
                for u in range(2):
                    normalise(it, u)
                    lay_windows(it + 1, u)
                    sum_colours(it + 1, u)
            link.end(NGRP // 2 - 1)
            last = NGRP // 2 - 1
            normalise(last, 0)
            lay_windows(last + 1, 0)
            sum_colours(last + 1, 0)
            normalise(last, 1)
            normalise(last + 1, 0)

        @block.scalar
        def _(act):
            def square(it, u):
                act.wait_ge(x_in[u], 16 * it + 16)
                act.activation(sq[:, u].rearrange("p c n -> p (c n)"), xg[:, u].rearrange("p c n -> p (c n)"),
                               ACT.Square).then_inc(sq_ready, 1)

            def square_windows(it, u):
                act.wait_ge(sq3_ready, 2 * it + u + 1)
                x = sq3[:, u].rearrange("p h (s i j) -> p (h s) i j", s=GRP, i=BLK)
                for q in range(4):
                    a, b = q // 2, q % 2
                    ins = act.copy(xsq[:, u, 2 * q:2 * q + 2].rearrange("p h (s i j) -> p (h s) i j", s=GRP, i=6),
                                   x[:, :, a:a + 6, b:b + 6])
                ins.then_inc(squared, 1)

            def finish(it, u):
                g1 = 2 * it + u + 1
                act.wait_ge(tok_ready, g1)
                n = GRP * TI
                act.dma_start(tok_rows[bass.ds((2 * it + u) * n, n), :], rows[0:n, u, :])\
                   .then_inc(rows_stored[u], 16)

            for u in range(2):
                square(0, u)
            for u in range(2):
                square_windows(0, u)
            with act.Fori(0, NGRP // 2 - 1) as it:
                for u in range(2):
                    square(it + 1, u)
                    act.wait_ge(products_done, 2 * it + u + 1)
                    square_windows(it + 1, u)
                    finish(it, u)
            it = NGRP // 2 - 1
            square(it + 1, 0)
            act.wait_ge(products_done, 2 * it + 1)
            square_windows(it + 1, 0)
            finish(it, 0)
            finish(it, 1)
            finish(it + 1, 0)

        @block.tensor
        def _(pe):
            ones = cst[:, C_ONE:C_ONE + P]
            pe.wait_ge(w_in, 5 * 16)
            pe.wait_ge(cst_in, 16)
            pe.matmul(c_ps[:, 0, 0:D], ones[0:1, :], bias[:], start=True, stop=False)
            for part, w, loaded in ((2, ws, ws_in), (3, wb, wb_in)):
                pe.wait_ge(loaded, 16)
                for k in range(NK):
                    mm = pe.matmul(c_ps[:, 0, 0:D], gain[:, part, k:k + 1].to_broadcast([P, P]), w[:, k, :],
                                   start=False, stop=part == 3 and k == NK - 1)
            mm.then_inc(sums_ready, 1)
            def group(it, u):
                m = GRP * TI
                pe.wait_ge(windows_ready, 2 * it + u + 1)
                for k in range(NK):
                    pe.matmul(y_ps[0:m, u, 0:D + 1], xw[:, u, k, :], weff[:, k, :], start=k == 0, stop=k == NK - 1)
                pe.wait_ge(squared, 2 * it + u + 1)
                for k in range(8):
                    mm = pe.matmul(q_ps[0:m, u, 0:1], xsq[:, u, k, :], weff[:, k // 2 * NCH + k % 2, D:D + 1],
                                   start=k == 0, stop=k == 7)
                mm.then_inc(products_done, 1)

            pe.wait_ge(weff_ready, 2)
            group(0, 0)
            pe.wait_ge(wsum_ready, 1)
            pe.matmul(c_ps[:, 1, 0:D], ones, wsum[:], start=True, stop=True).then_inc(sums_ready, 1)
            group(0, 1)
            with pe.Fori(1, NGRP // 2) as it:
                for u in range(2):
                    pe.wait_ge(y_used, 2 * it + u + 1)
                    group(it, u)
            pe.wait_ge(y_used, NGRP)
            group(NGRP // 2, 0)


class Norm:

    FIRST = 4

    def __init__(self, nc, stack, cst, resid):
        def sb(name, shape):
            return stack.enter_context(nc.sbuf_tensor("ln_" + name, shape, F32))

        self.cst, self.resid = cst, resid
        self.mean, self.rstd, self.var, self.ve = sb("mean", [P, NB]), sb("rstd", [P, NB]), sb("var", [P, NB]), sb("ve", [P, NB])
        self.six, self.tmp = sb("six", [P, NB, 6]), sb("tmp", [P, 4, NB])

    def begin(self, take, name):
        self.chain, self.var_ready, self.ve_ready, self.rstd_ready = (
            take(name + "_ln_chain"), take(name + "_ln_var"), take(name + "_ln_ve"), take(name + "_ln_rstd"))

    def add_rows(self, dve, t):
        return dve.bn_stats(self.six[:, bass.ds(t, 1), :], self.resid[:, bass.ds(t * D, D)])

    def statistics(self, dve, a=0, b=NB, n=0):
        six, tmp = self.six[:, a:b], self.tmp[:, :, a:b]
        dve.tensor_tensor(tmp[:, 0], six[:, :, 1], six[:, :, 4], ALU.add).then_inc(self.chain, 1)
        dve.tensor_tensor(tmp[:, 1], six[:, :, 1], six[:, :, 4], ALU.subtract).then_inc(self.chain, 1)
        dve.tensor_tensor(tmp[:, 2], six[:, :, 2], six[:, :, 5], ALU.add).then_inc(self.chain, 1)
        dve.wait_ge(self.chain, 4 * n + 3)
        dve.scalar_tensor_tensor(tmp[:, 3], tmp[:, 1], 0.25, tmp[:, 1], ALU.mult, ALU.mult).then_inc(self.chain, 1)
        dve.tensor_scalar(self.mean[:, a:b], tmp[:, 0], 0.5, None, ALU.mult).then_inc(self.var_ready, 1)
        dve.wait_ge(self.chain, 4 * n + 4)
        dve.scalar_tensor_tensor(self.var[:, a:b], tmp[:, 2], 1.0 / D, tmp[:, 3], ALU.mult, ALU.add)\
           .then_inc(self.var_ready, 1)
        dve.wait_ge(self.var_ready, 2 * n + 2)
        dve.wait_ge(self.rstd_ready, n + 1)

    def deviations(self, pool, calls=1):
        for n, (a, b) in enumerate(((0, self.FIRST), (self.FIRST, NB))):
            pool.wait_ge(self.var_ready, 2 * min(n + 1, calls))
            pool.tensor_scalar(self.ve[:, a:b], self.var[:, a:b], LN_EPS, None, ALU.add).then_inc(self.ve_ready, 1)
            pool.wait_ge(self.ve_ready, n + 1)
            pool.tensor_tensor(self.rstd[:, a:b], self.ve[:, a:b],
                               self.cst[:, C_NHALF:C_NHALF + 1].to_broadcast([P, b - a]), ALU.pow)\
                .then_inc(self.rstd_ready, 1)

    def apply(self, dve, out, t):
        return dve.tensor_scalar(out, self.resid[:, bass.ds(t * D, D)], self.mean[:, bass.ds(t, 1)],
                                 self.rstd[:, bass.ds(t, 1)], ALU.subtract, ALU.mult)


def channel_attention(nc, wqk_d, wv_d, wp_d, bp_d, temp_d, cst, resid, norm, slot_mem):
    U, G = 4, 2
    PAIRS = NB // G
    with ExitStack() as ctx:
        take = ctx.enter_context(semaphores(nc))
        def sb(name, shape, dt=F32):
            return ctx.enter_context(nc.sbuf_tensor("ca_" + name, shape, dt))

        def sem(name):
            return take("ca_" + name)

        wqk, wv, wp = sb("wqk", [DH, 2, 2 * D]), sb("wv", [DH, 2, D]), sb("wp", [DH, 2, D])
        temp = sb("temp", [DH, 2])
        hn = sb("hn", [P, U, D])
        hnt = sb("hnt", [DH, U, 2, P])
        qk = sb("qk", [P, U, 2 * D])
        sq = sb("sq", [P, U, 2 * D])
        vt = sb("vt", [DH + 1, U, 2, P])
        ss = sb("ss", [DH, U, D + 2])
        rn = sb("rn", [DH, U, D + 2])
        rqt = sb("rqt", [DH, U, 2])
        sc = sb("sc", [DH, U, 2, DH])
        pr = sb("pr", [DH, U, 2, DH])
        nmx, sm, rs = sb("nmx", [DH, U, 2]), sb("sm", [DH, U, 2]), sb("rs", [DH, U, 2])
        mix = sb("mix", [DH + 1, U, 2, D])
        pa = ctx.enter_context(nc.psum_tensor("ca_pa", [P, U, 512], F32))
        pb = ctx.enter_context(nc.psum_tensor("ca_pb", [P, U, 512], F32))
        w_in, hn_ready, hnt_ps, hnt_ready = sem("w_in"), sem("hn_ready"), sem("hnt_ps"), sem("hnt_ready")
        qk_ps, qk_ready, sq_ready, vt_ps = sem("qk_ps"), sem("qk_ready"), sem("sq_ready"), sem("vt_ps")
        vt_ready, gram_ps, ss_ready = sem("vt_ready"), sem("gram_ps"), sem("ss_ready")
        max_ready, exp_ready, attn_ready = sem("max_ready"), sem("exp_ready"), sem("attn_ready")
        mix_ps, mix_ready, out_ps, chain = sem("mix_ps"), sem("mix_ready"), sem("out_ps"), sem("chain")
        added, rn_ready = sem("added"), sem("rn_ready")
        norm.begin(take, "ca")
        ZN = 16 * D
        zrow = sb("zrow", [P, ZN])
        zeroed, slots_clear = sem("zeroed"), sem("slots_clear")
        six_ready = sem("six_ready")
        block = ctx.enter_context(nc.Block())

        def each(g, s):
            return [(g * G + v, s * G + v) for v in range(G)]

        def both(x, s):
            return x[:, s * G:(s + 1) * G]

        @block.sync
        def _(sp):
            for dst, src in ((wqk, wqk_d), (wv, wv_d), (wp, wp_d), (temp, temp_d)):
                sp.dma_start(dst[:], src).then_inc(w_in, 16)
            sp.dma_start(mix[DH:DH + 1, :, 1, :], bp_d.unsqueeze(0)).then_inc(w_in, 16)
            sp.wait_ge(zeroed, 1)
            sp.dma_start(slot_mem.rearrange("(p a n) -> p a n", p=P, n=ZN),
                         zrow[:].unsqueeze(1).to_broadcast([P, NBLK0 * D // ZN, ZN])).then_inc(slots_clear, 16)
            sp.wait_ge(w_in, 5 * 16)
            sp.wait_ge(slots_clear, 16)

        @block.tensor
        def _(pe):
            ident = cst[:, C_ID:C_ID + P]
            ones = cst[:, C_ONE:C_ONE + P]
            pe.wait_ge(w_in, 5 * 16)

            def turn_over(g, s):
                for t, u in each(g, s):
                    pe.wait_ge(hn_ready, t + 1)
                    for c in range(2):
                        mm = pe.transpose(pa[0:DH, u, c * P:(c + 1) * P], hn[:, u, c * DH:(c + 1) * DH], ident)
                    mm.then_inc(hnt_ps, 1)

            def project(g, s):
                for t, u in each(g, s):
                    pe.wait_ge(hnt_ready, t + 1)
                    pe.wait_ge(added, t + 1)
                    for c in range(2):
                        mm = pe.matmul(pb[:, u, 0:2 * D], hnt[:, u, c], wqk[:, c], start=c == 0, stop=c == 1)
                    mm.then_inc(qk_ps, 1)
                for t, u in each(g, s):
                    for h in range(2):
                        for c in range(2):
                            mm = pe.matmul(pa[0:DH, u, h * P:(h + 1) * P], wv[:, c, h * DH:(h + 1) * DH],
                                           hnt[:, u, c], start=c == 0, stop=c == 1)
                    mm.then_inc(vt_ps, 1)

            def scores(g, s):
                for t, u in each(g, s):
                    pe.wait_ge(qk_ready, t + 1)
                    for h in range(2):
                        pe.matmul(pb[0:DH, u, h * DH:(h + 1) * DH], qk[:, u, h * DH:(h + 1) * DH],
                                  qk[:, u, D + h * DH:D + (h + 1) * DH], start=True, stop=True)
                    pe.wait_ge(sq_ready, t + 1)
                    pe.matmul(pb[0:DH, u, D:2 * D], ones[:, 0:DH], sq[:, u, D:2 * D], start=True, stop=True)
                    for h in range(2):
                        mm = pe.matmul(pb[0:DH, u, 2 * D + h:2 * D + h + 1], sq[:, u, h * DH:(h + 1) * DH],
                                       ones[:, 0:1], start=True, stop=True)
                    mm.then_inc(gram_ps, 1)

            def mix_weights(g, s):
                pe.wait_ge(attn_ready, g + 1)
                for t, u in each(g, s):
                    pe.wait_ge(vt_ready, t + 1)
                    for h in range(2):
                        mm = pe.matmul(pa[0:DH, u, h * D:(h + 1) * D], pr[:, u, h], wp[:, h], start=True, stop=True)
                    mm.then_inc(mix_ps, 1)

            def output(g, s):
                for t, u in each(g, s):
                    pe.wait_ge(mix_ready, t + 1)
                    for h in range(2):
                        k = DH + h
                        mm = pe.matmul(pb[0:T, u, 0:D], vt[0:k, u, h, 0:T], mix[0:k, u, h], start=h == 0, stop=h == 1)
                    mm.then_inc(out_ps, 1)

            def turn(g, s, ahead=2):
                if ahead > 0:
                    project(g + 1, 1 - s)
                    scores(g + 1, 1 - s)
                mix_weights(g, s)
                output(g, s)
                if ahead > 1:
                    turn_over(g + 2, s)

            turn_over(0, 0)
            turn_over(1, 1)
            project(0, 0)
            scores(0, 0)
            with pe.Fori(0, PAIRS // 2 - 1) as it:
                for s in range(2):
                    turn(it * 2 + s, s)
            for s in range(2):
                turn(PAIRS - 2 + s, s, 1 - s)

        @block.scalar
        def _(act):
            def turn_over(g, s):
                for t, u in each(g, s):
                    act.wait_ge(hnt_ps, t + 1)
                    act.copy(hnt[:, u], pa[0:DH, u, 0:2 * P].rearrange("p (c t) -> p c t", c=2)).then_inc(hnt_ready, 1)

            def projected(g, s):
                for t, u in each(g, s):
                    act.wait_ge(qk_ps, t + 1)
                    act.copy(qk[:, u], pb[:, u, 0:2 * D]).then_inc(qk_ready, 1)
                for t, u in each(g, s):
                    act.wait_ge(vt_ps, t + 1)
                    act.copy(vt[0:DH, u], pa[0:DH, u, 0:2 * P].rearrange("p (c t) -> p c t", c=2)).then_inc(vt_ready, 1)

            def norms(g, s):
                for t, u in each(g, s):
                    act.wait_ge(gram_ps, t + 1)
                    act.activation(ss[:, u], pb[0:DH, u, D:2 * D + 2], ACT.Sqrt).then_inc(ss_ready, 1)

            def exponentials(g, s):
                act.wait_ge(max_ready, g + 1)
                for t, u in each(g, s):
                    for h in range(2):
                        ins = act.activation(pr[:, u, h], sc[:, u, h], ACT.Exp, bias=nmx[:, u, h:h + 1],
                                             accum_out=sm[:, u, h:h + 1])
                    ins.then_inc(exp_ready, 1)

            def mixed(g, s):
                for t, u in each(g, s):
                    act.wait_ge(mix_ps, t + 1)
                    act.copy(mix[0:DH, u], pa[0:DH, u, 0:2 * D].rearrange("p (g d) -> p g d", g=2)).then_inc(mix_ready, 1)

            def turn(g, s, ahead=2):
                if ahead > 0:
                    projected(g + 1, 1 - s)
                    norms(g + 1, 1 - s)
                mixed(g, s)
                if ahead > 1:
                    turn_over(g + 2, s)
                if ahead > 0:
                    exponentials(g + 1, 1 - s)

            turn_over(0, 0)
            turn_over(1, 1)
            projected(0, 0)
            norms(0, 0)
            exponentials(0, 0)
            with act.Fori(0, PAIRS // 2 - 1) as it:
                for s in range(2):
                    turn(it * 2 + s, s)
            for s in range(2):
                turn(PAIRS - 2 + s, s, 1 - s)

        @block.gpsimd
        def _(pool):
            norm.deviations(pool, calls=2)
            pool.memset(zrow[:], 0.0).then_inc(zeroed, 1)
            with pool.Fori(0, NB // U) as it:
                for u in range(U):
                    pool.wait_ge(qk_ready, it * U + u + 1)
                    pool.tensor_tensor(sq[:, u], qk[:, u], qk[:, u], ALU.mult).then_inc(sq_ready, 1)

        @block.vector
        def _(dve):
            link = Link(dve, chain)
            dve.memset(vt[DH:DH + 1], 1.0).then_inc(added, U)
            dve.wait_ge(added, U)
            for t in range(norm.FIRST):
                norm.add_rows(dve, t).then_inc(six_ready, 1)
            dve.wait_ge(six_ready, norm.FIRST)
            norm.statistics(dve, 0, norm.FIRST, 0)

            def normalise(g, s):
                for t, u in each(g, s):
                    norm.apply(dve, hn[:, u], t).then_inc(hn_ready, 1)

            def inverse_norms(g, s):
                for t, u in each(g, s):
                    dve.wait_ge(ss_ready, t + 1)
                    dve.reciprocal(rn[:, u], ss[:, u]).then_inc(rn_ready, 1)

            def scores(g, s):
                dve.wait_ge(rn_ready, g * G + G)
                dve.tensor_tensor(both(rqt, s), both(rn, s)[:, :, D:D + 2],
                                  temp[:].unsqueeze(1).to_broadcast([DH, G, 2]), ALU.mult).then_inc(chain, 1)
                link.n += 1
                link.done(dve.tensor_tensor(both(sc, s).rearrange("p u h d -> p u (h d)"), both(pb[0:DH], s)[:, :, 0:D],
                                            both(rn, s)[:, :, 0:D], ALU.mult))
                for t, u in each(g, s):
                    for h in range(2):
                        ins = dve.scalar_tensor_tensor(sc[:, u, h], sc[:, u, h], rqt[:, u, h:h + 1],
                                                       cst[0:DH, C_BLKM:C_BLKM + DH], ALU.mult, ALU.add)
                        ins.then_inc(chain, 1)
                        link.n += 1
                dve.wait_ge(chain, link.base + link.n)
                link.done(dve.tensor_reduce(both(rs, s), both(sc, s), AX.X, ALU.max))
                dve.tensor_scalar(both(nmx, s), both(rs, s), -1.0, None, ALU.mult).then_inc(max_ready, 1)

            def weights(g, s):
                dve.wait_ge(max_ready, g + 1)
                dve.wait_ge(exp_ready, g * G + G)
                link.done(dve.reciprocal(both(rs, s), both(sm, s)))
                dve.tensor_tensor(both(pr, s), both(pr, s), both(rs, s).unsqueeze(3).to_broadcast([DH, G, 2, DH]),
                                  ALU.mult).then_inc(attn_ready, 1)

            def add(g, s):
                for t, u in each(g, s):
                    dve.wait_ge(out_ps, t + 1)
                    h = resid[0:T, bass.ds(t * D, D)]
                    dve.tensor_tensor(h, h, pb[0:T, u, 0:D], ALU.add).then_inc(added, 1)
                for t, u in each(g, s):
                    dve.wait_ge(added, U + t + 1)
                    norm.add_rows(dve, t).then_inc(six_ready, 1)

            def turn(g, s, ahead=2):
                weights(g, s)
                if ahead > 1:
                    normalise(g + 2, s)
                if ahead > 0:
                    inverse_norms(g + 1, 1 - s)
                add(g, s)
                if ahead > 0:
                    scores(g + 1, 1 - s)

            normalise(0, 0)
            normalise(1, 1)
            with dve.Fori(0, 4) as it:
                for n in range((NB - norm.FIRST) // 4):
                    norm.add_rows(dve, it * ((NB - norm.FIRST) // 4) + n + norm.FIRST).then_inc(six_ready, 1)
            dve.wait_ge(six_ready, NB)
            norm.statistics(dve, norm.FIRST, NB, 1)
            dve.wait_ge(w_in, 5 * 16)
            inverse_norms(0, 0)
            scores(0, 0)
            link.base, link.n = link.n, 0
            with dve.Fori(0, PAIRS // 2 - 1) as it:
                link.loop(it, 2 * 8)
                for s in range(2):
                    turn(it * 2 + s, s)
            link.end(PAIRS // 2 - 1)
            for s in range(2):
                turn(PAIRS - 2 + s, s, 1 - s)
            dve.wait_ge(six_ready, 2 * NB)


def route_tokens(nc, emb_d, wcat_d, bcat_d, cst, cstb, norm, embt, chosen, weight, index, count,
                 know, f_know, know_in):
    U, G = 4, 2
    PAIRS = NB // G
    with ExitStack() as ctx:
        take = ctx.enter_context(semaphores(nc))
        def sb(name, shape, dt=F32):
            return ctx.enter_context(nc.sbuf_tensor("rt_" + name, shape, dt))

        def sem(name):
            return take("rt_" + name)

        emb = sb("emb", [NE, 2, 64])
        junk, ess = sb("junk", [NE, 64]), sb("ess", [NE, 2])
        wcat, bcat = sb("wcat", [DH, 2, P]), sb("bcat", [P, 1])
        hn = sb("hn", [P, U, D])
        hnt = sb("hnt", [DH, U, 2, P])
        zt = sb("zt", [P, U, P])
        e = sb("e", [P, U * 2, NE + 4])
        zap = sb("zap", [P, U * 2, NE + 4])
        top8, taken = sb("top8", [P, U * 2, 8]), sb("taken", [P, U * 2, 8])
        ix = sb("ix", [P, U * 2, 8], U32)
        mx, nmx, z = sb("mx", [P, U, 2]), sb("nmx", [P, U, 2]), sb("z", [P, U * 2])
        zc = sb("zc", [P, U * 2])
        s4, den, rden = sb("s4", [P, U * 2]), sb("den", [P, U * 2]), sb("rden", [P, U * 2])
        pa = ctx.enter_context(nc.psum_tensor("rt_pa", [P, U, 512], F32))
        pb = ctx.enter_context(nc.psum_tensor("rt_pb", [P, 2, 512], F32))
        tokens = ctx.enter_context(nc.psum_tensor("rt_tokens", [P, 512], F32))
        chosen_ready, tokens_ps = sem("chosen_ready"), sem("tokens_ps")
        w_in, chain = sem("w_in"), sem("chain")
        emb_sq, emb_norm, emb_unit, emb_ps, embt_ready = (
            sem("emb_sq"), sem("emb_norm"), sem("emb_unit"), sem("emb_ps"), sem("embt_ready"))
        hn_ready, hnt_ps, hnt_ready, z_ps, z_ready = (
            sem("hn_ready"), sem("hnt_ps"), sem("hnt_ready"), sem("z_ps"), sem("z_ready"))
        logit_ps, max_ready, exp_ready = sem("logit_ps"), sem("max_ready"), sem("exp_ready")
        norm.begin(take, "rt")
        block = ctx.enter_context(nc.Block())

        def each(g, s):
            return [(g * G + v, s * G + v) for v in range(G)]

        @block.gpsimd
        def _(pool):
            norm.deviations(pool)

        @block.sync
        def _(sp):
            for dst, src in ((emb, emb_d), (wcat, wcat_d), (bcat, bcat_d)):
                sp.dma_start(dst[:], src).then_inc(w_in, 16)
            sp.wait_ge(w_in, 3 * 16)
            for part in range(KPARTS):
                load_knowledge(sp, know, f_know, D, R, part, know_in)

        @block.scalar
        def _(act):
            act.wait_ge(w_in, 3 * 16)
            for r in range(2):
                if r:
                    act.wait_ge(emb_sq, r)
                act.activation(junk[:], emb[:, r], ACT.Square, accum_out=ess[:, r:r + 1]).then_inc(emb_sq, 1)
            act.wait_ge(emb_sq, 2)
            act.activation(den[:, 0:2], ess[:], ACT.Sqrt).then_inc(emb_norm, 1)

            def logits(g, s):
                for t, u in each(g, s):
                    act.wait_ge(hnt_ps, t + 1)
                    act.copy(hnt[:, u], pa[0:DH, u, 0:2 * P].rearrange("p (c t) -> p c t", c=2)).then_inc(hnt_ready, 1)
                for t, u in each(g, s):
                    act.wait_ge(z_ps, t + 1)
                    act.activation(zt[:, u], pb[:, u % 2, 0:P], ACT.Identity, bias=bcat[:]).then_inc(z_ready, 1)

            def exponentials(g, s):
                act.wait_ge(max_ready, g + 1)
                for t, u in each(g, s):
                    for r in range(2):
                        ins = act.activation(e[:, 2 * u + r, 0:NE], pa[:, u, r * NE:(r + 1) * NE], ACT.Exp,
                                             bias=nmx[:, u, r:r + 1], accum_out=z[:, 2 * u + r:2 * u + r + 1])
                ins.then_inc(exp_ready, 1)

            for s in range(2):
                logits(s, s)
            exponentials(0, 0)
            with act.Fori(0, PAIRS // 2 - 1) as it:
                for s in range(2):
                    logits(it * 2 + s + 2, s)
                    exponentials(it * 2 + s + 1, 1 - s)
            exponentials(PAIRS - 1, 1)

        @block.tensor
        def _(pe):
            ident = cst[:, C_ID:C_ID + P]
            pe.wait_ge(emb_unit, 1)
            pe.transpose(pa[:, 0, 0:P], emb[:].rearrange("n r d -> n (r d)"), ident).then_inc(emb_ps, 1)
            pe.wait_ge(embt_ready, 4)

            def logits(g, s):
                for t, u in each(g, s):
                    pe.wait_ge(hn_ready, t + 1)
                    for c in range(2):
                        mm = pe.transpose(pa[0:DH, u, c * P:(c + 1) * P], hn[:, u, c * DH:(c + 1) * DH], ident)
                    mm.then_inc(hnt_ps, 1)
                for t, u in each(g, s):
                    pe.wait_ge(hnt_ready, t + 1)
                    for c in range(2):
                        mm = pe.matmul(pb[:, u % 2, 0:P], wcat[:, c], hnt[:, u, c], start=c == 0, stop=c == 1)
                    mm.then_inc(z_ps, 1)
                for t, u in each(g, s):
                    pe.wait_ge(z_ready, t + 1)
                    pe.matmul(pa[:, u, 0:2 * NE], zt[:, u], embt[:], start=True, stop=True).then_inc(logit_ps, 1)

            def tokens_of(g):
                pe.wait_ge(chosen_ready, g + 1)
                for n in range(2 * G):
                    mm = pe.matmul(tokens[:, bass.ds(g * 2 * G + n, 1)], chosen[:, bass.ds(g * 2 * G + n, 1), :].rearrange("p a n -> p (a n)"),
                                   cstb[:, 1, 0:1], start=True, stop=True)
                mm.then_inc(tokens_ps, 1)

            for s in range(2):
                logits(s, s)
            with pe.Fori(1, PAIRS // 2) as it:
                for s in range(2):
                    logits(it * 2 + s, s)
                    tokens_of((it - 1) * 2 + s)
            for s in range(2):
                tokens_of(PAIRS - 2 + s)

        @block.vector
        def _(dve):
            link = Link(dve, chain)
            norm.statistics(dve)
            dve.memset(embt[0:64, NE:2 * NE], 0.0).then_inc(embt_ready, 1)
            dve.memset(embt[64:P, 0:NE], 0.0).then_inc(embt_ready, 1)
            dve.wait_ge(emb_norm, 1)
            link.done(dve.tensor_scalar(s4[:, 0:2], den[:, 0:2], 1e-8, None, ALU.add))
            link.done(dve.reciprocal(rden[:, 0:2], s4[:, 0:2]))
            dve.tensor_tensor(emb[:], emb[:], rden[:, 0:2].unsqueeze(2).to_broadcast([NE, 2, 64]), ALU.mult)\
               .then_inc(emb_unit, 1)
            dve.wait_ge(emb_ps, 1)
            dve.tensor_copy(embt[0:64, 0:NE], pa[0:64, 0, 0:NE]).then_inc(embt_ready, 1)
            dve.tensor_copy(embt[64:P, NE:2 * NE], pa[64:P, 0, 0:NE]).then_inc(embt_ready, 1)
            for buf, at in ((e, NE), (taken, 4)):
                link.done(dve.tensor_copy(buf[:, :, at:at + 4],
                                          cst[:, C_SENT:C_SENT + 4].unsqueeze(1).to_broadcast([P, 2 * U, 4])))

            def normalise(g, s):
                for t, u in each(g, s):
                    norm.apply(dve, hn[:, u], t).then_inc(hn_ready, 1)

            def maxima(g, s):
                dve.wait_ge(logit_ps, g * G + G)
                us = slice(s * G, (s + 1) * G)
                link.done(dve.tensor_reduce(mx[:, us], pa[:, us, 0:2 * NE].rearrange("p u (r n) -> p u r n", r=2),
                                            AX.X, ALU.max))
                dve.tensor_scalar(nmx[:, us], mx[:, us], -1.0, None, ALU.mult).then_inc(max_ready, 1)

            def choose(g, s):
                ks = slice(2 * G * s, 2 * G * (s + 1))
                at = bass.ds(g * 2 * G, 2 * G)
                dve.tensor_copy(zc[:, ks], z[:, ks])
                for k in range(2 * G * s, 2 * G * (s + 1)):
                    ins = dve.max(top8[:, k], e[:, k, 0:NE])
                link.done(ins)
                link.done(dve.tensor_copy(taken[:, ks, 0:4], top8[:, ks, 0:4]))
                dve.tensor_reduce(s4[:, ks], top8[:, ks, 0:4], AX.X, ALU.add)
                for k in range(2 * G * s, 2 * G * (s + 1)):
                    dve.max_index(ix[:, k], top8[:, k], e[:, k, 0:NE])
                    ins = dve.match_replace(zap[:, k], taken[:, k], e[:, k], -9.0)
                link.done(ins)
                link.done(dve.scalar_tensor_tensor(den[:, ks], zc[:, ks], 1e-8, s4[:, ks], ALU.mult, ALU.add))
                dve.tensor_scalar(chosen[:, at, :], zap[:, ks, 0:NE], -5.0, cst[:, C_VALID:C_VALID + 1],
                                  ALU.is_lt, ALU.mult).then_inc(chosen_ready, 1)
                link.done(dve.reciprocal(rden[:, ks], den[:, ks]))
                dve.tensor_copy(index[:, at, :], ix[:, ks, 0:4])
                link.done(dve.tensor_tensor(weight[:, at, :], top8[:, ks, 0:4],
                                            rden[:, ks].unsqueeze(2).to_broadcast([P, 2 * G, 4]), ALU.mult))

            def turn(g, s, ahead=2):
                dve.wait_ge(exp_ready, g + 1)
                if ahead > 1:
                    normalise(g + 2, s)
                if ahead > 0:
                    maxima(g + 1, 1 - s)
                choose(g, s)

            normalise(0, 0)
            normalise(1, 1)
            dve.wait_ge(norm.rstd_ready, 2)
            maxima(0, 0)
            link.base, link.n = link.base + link.n, 0
            with dve.Fori(0, PAIRS // 2 - 1) as it:
                link.loop(it, 2 * 7)
                for s in range(2):
                    turn(it * 2 + s, s)
            link.end(PAIRS // 2 - 1)
            for s in range(2):
                turn(PAIRS - 2 + s, s, 1 - s)
            dve.wait_ge(tokens_ps, PAIRS)
            link.done(dve.tensor_reduce(count[:], tokens[:, 0:2 * NB].rearrange("p (b r) -> p r b", r=2), AX.X, ALU.add))


def block_tables(nc, cst, cstb, count, seg_start, block_expert):
    with ExitStack() as ctx:
        take = ctx.enter_context(semaphores(nc))
        def sb(name, shape, dt=F32):
            return ctx.enter_context(nc.sbuf_tensor("bt_" + name, shape, dt))

        def sem(name):
            return take("bt_" + name)

        more, blocks_i = sb("more", [P, 2], I32), sb("blocks_i", [P, 2], I32)
        blocks, blocks_b = sb("blocks", [P, 2]), sb("blocks_b", [P, 2], BF16)
        incl, before = sb("incl", [P, 2]), sb("before", [P, 2, 256], BF16)
        ps = ctx.enter_context(nc.psum_tensor("bt_ps", [P, 3, 512], F32))
        blocks_ready = sem("blocks_ready")
        incl_ps, before_ready, row_ps, chain = sem("incl_ps"), sem("before_ready"), sem("row_ps"), sem("chain")
        block = ctx.enter_context(nc.Block())

        @block.vector
        def _(dve):
            link = Link(dve, chain)
            link.done(dve.tensor_scalar(more[:], count[:], P - 1.0, None, ALU.add))
            link.done(dve.tensor_scalar(blocks_i[:], more[:], 7, None, ALU.arith_shift_right))
            link.done(dve.tensor_copy(blocks[:], blocks_i[:]))
            dve.tensor_copy(blocks_b[:], blocks[:]).then_inc(blocks_ready, 1)
            for r in range(2):
                dve.tensor_scalar(seg_start[:, r], cst[:, C_ONE:C_ONE + P], blocks[:, r:r + 1], float(P),
                                  ALU.mult, ALU.mult)
            dve.wait_ge(incl_ps, 1)
            link.done(dve.tensor_copy(incl[:], ps[:, 1, 0:2]))
            for r in range(2):
                dve.tensor_scalar(before[:, r], cst[:, C_IOTA:C_IOTA + 256], incl[:, r:r + 1], None, ALU.is_ge)\
                   .then_inc(before_ready, 1)
            dve.wait_ge(row_ps, 1)
            link.done(dve.tensor_scalar(block_expert[:], ps[0:1, 2, 0:512].rearrange("p (r t) -> p r t", r=2),
                                        NE - 1.0, None, ALU.min))

        @block.tensor
        def _(pe):
            ones = cstb[:, 1]
            pe.wait_ge(blocks_ready, 1)
            pe.matmul(ps[:, 1, 0:2], cstb[:, 2], blocks_b[:], start=True, stop=True).then_inc(incl_ps, 1)
            pe.wait_ge(before_ready, 2)
            pe.matmul(ps[0:1, 2, 0:512], ones[:, 0:1], before[:].rearrange("p r t -> p (r t)"), start=True, stop=True)\
              .then_inc(row_ps, 1)


def place_tokens(nc, cst, cstb, norm, chosen, index, seg_start, slot, slot_rows):
    U = 4
    with ExitStack() as ctx:
        take = ctx.enter_context(semaphores(nc))
        def sb(name, shape, dt=F32):
            return ctx.enter_context(nc.sbuf_tensor("pl_" + name, shape, dt))

        def sem(name):
            return take("pl_" + name)

        earlier = sb("earlier", [P, U + 1, 2, NE], BF16)
        junk = sb("junk", [P, 16, NE], BF16)
        slot_f = sb("slot_f", [P, U, 8])
        hn = sb("hn", [P, U, D])
        rank = ctx.enter_context(nc.psum_tensor("pl_rank", [P, U, 512], F32))
        in_block, low, high = sb("in_block", [P, U, 8], I32), sb("low", [P, U, 8], I32), sb("high", [P, U, 8], I32)
        hn_ready, chain, summed, rank_ps, slot_ready = sem("hn_ready"), sem("chain"), sem("summed"), sem("rank_ps"), sem("slot_ready")
        scattered = [sem(f"scattered{u}") for u in range(U)]
        block = ctx.enter_context(nc.Block())


        @block.tensor
        def _(pe):
            with pe.Fori(0, NB // U) as it:
                for u in range(U):
                    b2 = 2 * (it * U + u)
                    pe.wait_ge(summed, it * U + u + 1)
                    pe.matmul(rank[:, u, 0:2 * NE], cstb[:, 3], chosen[:, bass.ds(b2, 2), :], start=True, stop=False)
                    pe.matmul(rank[:, u, 0:2 * NE], cstb[:, 1], earlier[:, u], start=False, stop=False)
                    for r in range(2):
                        mm = pe.matmul(rank[:, u, r * NE:(r + 1) * NE], seg_start[:, r], cstb[:, 3],
                                       start=False, stop=r == 1)
                    mm.then_inc(rank_ps, 1)

        @block.vector
        def _(dve):
            link = Link(dve, chain)
            link.done(dve.memset(earlier[:, U], 0.0))

            def turn(it, first):
                for u in range(U):
                    if u == 0:
                        ins = dve.tensor_copy(earlier[:, 0], earlier[:, U])
                    else:
                        ins = dve.tensor_tensor(earlier[:, u], earlier[:, u - 1],
                                                chosen[:, bass.ds(2 * (it * U + u - 1), 2), :], ALU.add)
                    ins.then_inc(summed, 1)
                    dve.wait_ge(summed, it * U + u + 1)
                link.done(dve.tensor_tensor(earlier[:, U], earlier[:, U - 1],
                                            chosen[:, bass.ds(2 * (it * U + U - 1), 2), :], ALU.add))
                for pair in range(U // 2):
                    us = slice(2 * pair, 2 * pair + 2)
                    for u in range(2 * pair, 2 * pair + 2):
                        b = it * U + u
                        dve.wait_ge(rank_ps, b + 1)
                        for k in range(8):
                            r, j = k // 4, k % 4
                            ins = dve.scalar_tensor_tensor(junk[:, u % 2 * 8 + k], cst[:, C_IOTA:C_IOTA + NE],
                                                           index[:, bass.ds(2 * b + r, 1), j],
                                                           rank[:, u, r * NE:(r + 1) * NE],
                                                           ALU.is_equal, ALU.mult, accum_out=slot_f[:, u, k:k + 1])
                    link.done(ins)
                    link.done(dve.tensor_scalar(high[:, us], slot_f[:, us], cst[:, C_FAR:C_FAR + 1], None, ALU.add))
                    dve.tensor_scalar(in_block[:, us], high[:, us], P - 1, 2, ALU.bitwise_and, ALU.logical_shift_left)
                    dve.tensor_scalar(low[:, us], high[:, us], 7, GROUP - 1, ALU.arith_shift_right, ALU.bitwise_and)
                    link.done(dve.tensor_scalar(high[:, us], high[:, us], -GROUP * P, None, ALU.bitwise_and))
                    link.done(dve.tensor_tensor(high[:, us], high[:, us], in_block[:, us], ALU.bitwise_or))
                    dve.tensor_tensor(slot[:, bass.ds(it * U + 2 * pair, 2), :], high[:, us], low[:, us], ALU.bitwise_or)\
                       .then_inc(slot_ready, 1)
                    for u in range(2 * pair, 2 * pair + 2):
                        if not first:
                            dve.wait_ge(scattered[u], 64 * it)
                        norm.apply(dve, hn[:, u], it * U + u).then_inc(hn_ready, 1)

            turn(0, True)
            with dve.Fori(1, NB // U) as it:
                link.loop(it - 1, 1 + 4 * (U // 2))
                turn(it, False)

        @block.gpsimd
        def _(pool):
            last_slot = pool.to_reg(NBLK0 * P - 1)
            for it in range(NB // U):
                for u in range(U):
                    t = it * U + u
                    pool.wait_ge(slot_ready, t // 2 + 1)
                    pool.wait_ge(hn_ready, t + 1)
                    for j in range(4):
                        pool.indirect_dma_start(slot_rows, bass.IndirectOffsetOnAxis(slot[:, t, j:j + 1], 0),
                                                hn[:, u], None, bounds_check=last_slot, oob_is_err=False)\
                            .then_inc(scattered[u], 16)
            for u in range(U):
                pool.wait_ge(scattered[u], 64 * (NB // U))


def load_experts(nc, engine, table, top):
    return nc.values_load_multi_w_load_instructions(
        table, engines=(engine,), min_val=0, max_val=top,
        skip_runtime_bounds_check_because="the table was written with a minimum against top")[1]


def load_knowledge(eng, know, weights, k, n, part, loaded):
    kc = -(-k // P)
    m = NE // KPARTS
    eng.dma_start(know[0:k // kc, part * m * kc * n:(part + 1) * m * kc * n].rearrange("p (a n) -> p a n", n=n),
                  weights[part * m:(part + 1) * m].rearrange("e (c p) n -> p (e c) n", c=kc)).then_inc(loaded, 16)


def blocks_product(nc, name, cst, block_expert, part, rows_in, know, know_in, rows_out, k, n):
    XG, YG = 4, 4
    W = XG * GROUP
    AHEAD = 3
    kc = -(-k // P)
    kp = k // kc
    turns = NBLK0 // W
    with ExitStack() as ctx:
        take = ctx.enter_context(semaphores(nc))
        def sb(nm, shape, dt=F32):
            return ctx.enter_context(nc.sbuf_tensor(f"{name}_{nm}", shape, dt))

        def sem(nm):
            return take(f"{name}_{nm}")

        x = sb("x", [P, XG, GROUP * k])
        xt = sb("xt", [kp, 4, kc, P])
        y = sb("y", [P, YG, GROUP * n])
        start = sb("start", [1, 1])
        t_ps = ctx.enter_context(nc.psum_tensor(name + "_t_ps", [P, 4, 512], F32))
        y_ps = ctx.enter_context(nc.psum_tensor(name + "_y_ps", [P, 4, 512], F32))
        x_t, xt_ready, product, y_ready = sem("x_t"), sem("xt_ready"), sem("product"), sem("y_ready")
        loaded = [sem(f"loaded{g}") for g in range(XG)]
        stored = [sem(f"stored{g}") for g in range(YG)]
        block = ctx.enter_context(nc.Block())

        def group_rows(rows, g):
            return rows[bass.ds(g * GROUP * P, GROUP * P), :].rearrange("(p j) d -> p (j d)", j=GROUP)

        @block.sync
        def _(sp):
            for g in range(XG):
                sp.dma_start(x[:, g], group_rows(rows_in, g)).then_inc(loaded[g], 16)
            with sp.Fori(0, turns - 1) as it:
                for g in range(XG):
                    sp.wait_ge(x_t, it * W + (g + 1) * GROUP)
                    sp.dma_start(x[:, g], group_rows(rows_in, it * XG + XG + g)).then_inc(loaded[g], 16)

        @block.tensor
        def _(pe):
            ident = cst[:, C_ID:C_ID + P]
            e_group = None

            def turn_over(it, u):
                if u % GROUP == 0:
                    pe.wait_ge(loaded[u // GROUP], 16 * it + 16)
                for c in range(kc):
                    at = (u % GROUP) * k + c * kp
                    mm = pe.transpose(t_ps[0:kp, u % 4, c * P:(c + 1) * P], x[:, u // GROUP, at:at + kp], ident)
                mm.then_inc(x_t, 1)

            def multiply(it, u):
                nonlocal e_group
                t = it * W + u
                if u % GROUP == 0:
                    e_group = load_experts(nc, mybir.EngineType.PE,
                                           block_expert[0:1, part, bass.ds(t, GROUP)], NE - 1)
                e = e_group[u % GROUP]
                pe.wait_ge(xt_ready, t + 1)
                pe.wait_ge(y_ready, t + 1)
                for c in range(kc):
                    mm = pe.matmul(y_ps[:, u % 4, 0:n], xt[:, u % 4, c],
                                   know[0:kp, bass.ds(e * (kc * n) + c * n, n)], start=c == 0, stop=c == kc - 1)
                mm.then_inc(product, 1)

            for u in range(AHEAD):
                turn_over(0, u)
            pe.wait_ge(know_in, 16 * KPARTS)
            with pe.Fori(0, turns - 1) as it:
                for u in range(W):
                    turn_over(it + (u + AHEAD) // W, (u + AHEAD) % W)
                    multiply(it, u)
            for u in range(W):
                if u + AHEAD < W:
                    turn_over(turns - 1, u + AHEAD)
                multiply(turns - 1, u)

        @block.scalar
        def _(act):
            def send(it, g):
                act.wait_ge(y_ready, 4 + it * W + (g + 1) * GROUP)
                act.dma_start(group_rows(rows_out, it * XG + g), y[:, g % YG]).then_inc(stored[g % YG], 16)

            def copy(it, u):
                act.wait_ge(x_t, it * W + u + 1)
                act.copy(xt[:, u % 4], t_ps[0:kp, u % 4, 0:kc * P].rearrange("p (c t) -> p c t", c=kc))\
                    .then_inc(xt_ready, 1)

            SEND = AHEAD + 1
            for u in range(SEND):
                copy(0, u)
            with act.Fori(0, turns - 1) as it:
                for u in range(W):
                    copy(it + (u + SEND) // W, (u + SEND) % W)
                    if u % GROUP == GROUP - 1:
                        send(it, u // GROUP)
            for u in range(W):
                if u + SEND < W:
                    copy(turns - 1, u + SEND)
                if u % GROUP == GROUP - 1:
                    send(turns - 1, u // GROUP)
            for g in range(YG):
                act.wait_ge(stored[g], 16 * (turns * XG // YG + 1))

        @block.vector
        def _(dve):
            for g in range(YG):
                dve.memset(y[:, g], 0.0).then_inc(stored[g], 16)
            dve.memset(start[:], 0.0).then_inc(y_ready, 4)
            with dve.Fori(0, turns) as it:
                for u in range(W):
                    g, j = u // GROUP, u % GROUP
                    dve.wait_ge(product, it * W + u + 1)
                    if j == 0:
                        dve.wait_ge(stored[g % YG], 16 * (XG // YG) * it + 16 * (g // YG) + 16)
                    dve.tensor_copy(y[:, g % YG, j * n:(j + 1) * n], y_ps[:, u % 4, 0:n]).then_inc(y_ready, 1)


def combine_rows(nc, name, slot, weight, part, rows, n, resid, norm, next_rows, know=None, r_know=None,
                 know_in=None):
    U = 4
    with ExitStack() as ctx:
        take = ctx.enter_context(semaphores(nc))
        def sb(nm, shape, dt=F32):
            return ctx.enter_context(nc.sbuf_tensor(f"{name}_{nm}", shape, dt))

        def sem(nm):
            return take(f"{name}_{nm}")

        g = sb("g", [P, U, 4, n])
        acc = sb("acc", [P, U, n])
        gathered = [sem(f"gathered{u}") for u in range(U)]
        scattered = [sem(f"scattered{u}") for u in range(U)]
        cleared, summed, chain, added, six_ready = (
            sem("cleared"), sem("summed"), sem("chain"), sem("added"), sem("six_ready"))
        block = ctx.enter_context(nc.Block())

        @block.sync
        def _(sp):
            if next_rows is not None:
                for part in range(KPARTS):
                    sp.wait_ge(summed, 3 * part + 1)
                    load_knowledge(sp, know, r_know, R, D, part, know_in)

        @block.gpsimd
        def _(pool):
            last_slot = pool.to_reg(NBLK0 * P - 1)

            def gather(t):
                if t >= U:
                    pool.wait_ge(summed, t - U + 1)
                for j in range(4):
                    pool.indirect_dma_start(g[:, t % U, j], None, rows,
                                            bass.IndirectOffsetOnAxis(slot[:, t, 4 * part + j:4 * part + j + 1], 0),
                                            bounds_check=last_slot, oob_is_err=False).then_inc(gathered[t % U], 16)

            def scatter(t):
                pool.wait_ge(summed, t + 1)
                for j in range(4):
                    pool.indirect_dma_start(next_rows, bass.IndirectOffsetOnAxis(slot[:, t, 4 + j:5 + j], 0),
                                            acc[:, t % U], None, bounds_check=last_slot, oob_is_err=False)\
                        .then_inc(scattered[t % U], 16)

            pool.wait_ge(cleared, 2)
            for t in range(U - 1):
                gather(t)
            for t in range(NB):
                if t + U - 1 < NB:
                    gather(t + U - 1)
                if next_rows is not None:
                    scatter(t)
            if next_rows is not None:
                for u in range(U):
                    pool.wait_ge(scattered[u], 64 * (NB // U))

        @block.vector
        def _(dve):
            link = Link(dve, chain)
            dve.memset(g[:], 0.0).then_inc(cleared, 1)
            dve.memset(acc[:], 0.0).then_inc(cleared, 1)
            dve.wait_ge(cleared, 2)

            def turn(it, first):
                for u in range(U):
                    b = it * U + u
                    wt = weight[0:T, bass.ds(2 * b + part, 1), :]
                    dve.wait_ge(gathered[u], 64 * it + 64)
                    if next_rows is not None and not first:
                        dve.wait_ge(scattered[u], 64 * it)
                    link.done(dve.tensor_scalar(acc[0:T, u], g[0:T, u, 0], wt[:, :, 0], None, ALU.mult))
                    for j in range(1, 4):
                        ins = dve.scalar_tensor_tensor(acc[0:T, u], g[0:T, u, j], wt[:, :, j], acc[0:T, u],
                                                       ALU.mult, ALU.add)
                        if j < 3:
                            link.done(ins)
                    ins.then_inc(summed, 1)
                    if next_rows is None:
                        dve.wait_ge(summed, b + 1)
                        h = resid[0:T, bass.ds(b * D, D)]
                        dve.tensor_tensor(h, h, acc[0:T, u], ALU.add).then_inc(added, 1)
                        dve.wait_ge(added, b + 1)
                        norm.add_rows(dve, b).then_inc(six_ready, 1)

            turn(0, True)
            with dve.Fori(1, NB // U) as it:
                link.loop(it - 1, 3 * U)
                turn(it, False)
            if next_rows is None:
                dve.wait_ge(six_ready, NB)


def causal_attention(nc, wq_d, wk_d, wv_d, wo_d, cst, cstb, resid, norm):
    U = 2
    NH, HD, HG, HK = 12, 16, 3, 4
    head = lambda g, k: NH // 2 * (k // 2) + 2 * g + k % 2
    with ExitStack() as ctx:
        take = ctx.enter_context(semaphores(nc))
        def sb(name, shape, dt=F32):
            return ctx.enter_context(nc.sbuf_tensor("at_" + name, shape, dt))

        def sem(name):
            return take("at_" + name)

        wq, wk = sb("wq", [DH, 2, D]), sb("wk", [DH, 2, D])
        wv, wo = sb("wv", [DH, 2, D]), sb("wo", [DH + 1, 2, D])
        caus = sb("caus", [P, HK * P], BF16)
        hn, hnt = sb("hn", [P, U, D]), sb("hnt", [DH, U, 2, P])
        qt, kt = sb("qt", [DH, U, 2, 2 * P]), sb("kt", [DH, U, 2 * P])
        v1 = sb("v1", [P, U, NH, HD + 1])
        mx, p, pt = sb("mx", [P, U, HG, HK]), sb("p", [P, U, HG, HK, P]), sb("pt", [P, U, HG, HK * P])
        rec, av = sb("rec", [P, U, NH]), sb("av", [P, U, D])
        avt = sb("avt", [DH + 1, U, 2, P])
        ps = ctx.enter_context(nc.psum_tensor("at_ps", [P, 4 * U, 512], F32))
        w_in, hn_ready, hnt_ps, hnt_ready = sem("w_in"), sem("hn_ready"), sem("hnt_ps"), sem("hnt_ready")
        qk_ps, v_ps, q_ready, kv_ready, score_ps = sem("qk_ps"), sem("v_ps"), sem("q_ready"), sem("kv_ready"), sem("score_ps")
        max_ready, added = sem("max_ready"), sem("added")
        shifted, exp_ready, pt_ps = sem("shifted"), sem("exp_ready"), sem("pt_ps")
        pt_act, pt_dve, av_ps, av_ready = sem("pt_act"), sem("pt_dve"), sem("av_ps"), sem("av_ready")
        avt_ps, avt_ready, out_ps, chain = sem("avt_ps"), sem("avt_ready"), sem("out_ps"), sem("chain")
        ones_ready = sem("ones_ready")
        six_ready = sem("six_ready")
        norm.begin(take, "at")
        block = ctx.enter_context(nc.Block())

        @block.gpsimd
        def _(pool):
            norm.deviations(pool)

        @block.sync
        def _(sp):
            for dst, src in ((wq, wq_d), (wk, wk_d), (wv, wv_d), (wo, wo_d)):
                sp.dma_start(dst[:], src).then_inc(w_in, 16)
            sp.wait_ge(w_in, 4 * 16)

        @block.tensor
        def _(pe):
            ident = cst[:, C_ID:C_ID + P]
            pe.wait_ge(w_in, 4 * 16)
            pe.wait_ge(ones_ready, 3)
            def turn_over(t, u):
                pe.wait_ge(hn_ready, t + 1)
                for c in range(2):
                    mm = pe.transpose(ps[0:DH, 4 * u + 2, c * P:(c + 1) * P], hn[:, u, c * DH:(c + 1) * DH], ident)
                mm.then_inc(hnt_ps, 1)

            def project(t, u):
                pe.wait_ge(hnt_ready, t + 1)
                for n, w in ((1, wq), (2, wk)):
                    for m in range(2):
                        for c in range(2):
                            mm = pe.matmul(ps[0:DH, 4 * u + n, m * P:(m + 1) * P], w[:, c, m * DH:(m + 1) * DH],
                                           hnt[:, u, c], start=c == 0, stop=c == 1)
                    mm.then_inc(qk_ps, 1)

            def project_values(t, u):
                pe.wait_ge(added, t + 1)
                for c in range(2):
                    mm = pe.matmul(ps[:, 4 * u + 3, 0:D], hnt[:, u, c], wv[:, c], start=c == 0, stop=c == 1)
                mm.then_inc(v_ps, 1)

            def scores(t, u):
                pe.wait_ge(q_ready, t + 1)
                pe.wait_ge(kv_ready, 3 * t + 2)
                for g in range(HG):
                    pe.matmul(ps[:, 4 * u + g, 0:HK * P], cstb[:, 0], caus[:], start=True, stop=False)
                for k in range(HK):
                    for g in range(HG):
                        rows, m = slice(32 * g, 32 * g + 32), k // 2
                        mm = pe.matmul(ps[:, 4 * u + g, k * P:(k + 1) * P], qt[rows, u, k % 2, m * P:(m + 1) * P],
                                       kt[rows, u, m * P:(m + 1) * P], start=False, stop=k == HK - 1)
                mm.then_inc(score_ps, 1)

            def turn_probs(t, u):
                pe.wait_ge(exp_ready, t + 1)
                for g in range(HG):
                    for k in range(HK):
                        mm = pe.transpose(ps[:, 4 * u + g, k * P:(k + 1) * P], p[:, u, g, k], ident)
                    mm.then_inc(pt_ps, 1)

            def weigh(t, u, ahead):
                pe.wait_ge(kv_ready, 3 * t + (5 if ahead else 3))
                pe.wait_ge(pt_act, 2 * t + 2)
                pe.wait_ge(pt_dve, t + 1)
                for g in range(HG):
                    for k in range(HK):
                        h = head(g, k)
                        mm = pe.matmul(ps[:, 4 * u + 3, h * (HD + 1):(h + 1) * (HD + 1)],
                                       pt[:, u, g, k * P:(k + 1) * P], v1[:, u, h], start=True, stop=True)
                mm.then_inc(av_ps, 1)

            def turn_values(t, u):
                pe.wait_ge(av_ready, t + 1)
                for c in range(2):
                    mm = pe.transpose(ps[0:DH, 4 * u, c * P:(c + 1) * P], av[:, u, c * DH:(c + 1) * DH], ident)
                mm.then_inc(avt_ps, 1)

            def output(t, u):
                pe.wait_ge(avt_ready, t + 1)
                for c in range(2):
                    k = DH + c
                    mm = pe.matmul(ps[0:T, 4 * u + 3, 0:D], avt[0:k, u, c, 0:T], wo[0:k, c], start=c == 0, stop=c == 1)
                mm.then_inc(out_ps, 1)

            def turn(t, u, ahead=2):
                turn_probs(t, u)
                if ahead > 0:
                    project_values(t + 1, 1 - u)
                    scores(t + 1, 1 - u)
                weigh(t, u, ahead)
                if ahead > 1:
                    turn_over(t + 2, u)
                turn_values(t, u)
                if ahead > 1:
                    project(t + 2, u)
                output(t, u)

            for u in range(U):
                turn_over(u, u)
            for u in range(U):
                project(u, u)
            project_values(0, 0)
            scores(0, 0)
            with pe.Fori(0, NB // U - 1) as it:
                for u in range(U):
                    turn(it * U + u, u)
            for u in range(U):
                turn(NB - U + u, u, 1 - u)

        @block.scalar
        def _(act):
            def turn_over(t, u):
                act.wait_ge(hnt_ps, t + 1)
                act.copy(hnt[:, u], ps[0:DH, 4 * u + 2, 0:2 * P].rearrange("p (c t) -> p c t", c=2)).then_inc(hnt_ready, 1)

            def queries(t, u):
                act.wait_ge(qk_ps, 2 * t + 1)
                act.activation(qt[:, u, 0], ps[0:DH, 4 * u + 1, 0:2 * P], ACT.Identity, scale=cst[0:DH, C_EVEN:C_EVEN + 1])\
                    .then_inc(q_ready, 1)

            def exponentials(t, u):
                for g in range(HG):
                    act.wait_ge(shifted, HG * t + g + 1)
                    ins = act.activation(p[:, u, g], p[:, u, g], ACT.Exp, scale=HD ** -0.5)
                ins.then_inc(exp_ready, 1)

            def probs(t, u):
                for g in (0, 2):
                    act.wait_ge(pt_ps, 3 * t + g + 1)
                    act.copy(pt[:, u, g], ps[:, 4 * u + g]).then_inc(pt_act, 1)

            def values(t, u):
                act.wait_ge(avt_ps, t + 1)
                act.copy(avt[0:DH, u], ps[0:DH, 4 * u, 0:2 * P].rearrange("p (c t) -> p c t", c=2)).then_inc(avt_ready, 1)

            def turn(t, u, ahead=2):
                probs(t, u)
                if ahead > 1:
                    turn_over(t + 2, u)
                values(t, u)
                if ahead > 0:
                    exponentials(t + 1, 1 - u)
                if ahead > 1:
                    queries(t + 2, u)

            for u in range(U):
                turn_over(u, u)
            for u in range(U):
                queries(u, u)
            exponentials(0, 0)
            with act.Fori(0, NB // U - 1) as it:
                for u in range(U):
                    turn(it * U + u, u)
            for u in range(U):
                turn(NB - U + u, u, 1 - u)

        @block.vector
        def _(dve):
            link = Link(dve, chain)
            dve.memset(v1[:], 1.0).then_inc(ones_ready, 1)
            dve.memset(avt[DH:DH + 1], 1.0).then_inc(ones_ready, 1)
            dve.tensor_copy(caus[:].rearrange("p (k n) -> p k n", k=HK),
                            cst[:, C_CAUS:C_CAUS + P].unsqueeze(1).to_broadcast([P, HK, P])).then_inc(ones_ready, 1)
            dve.wait_ge(ones_ready, 3)
            dve.memset(hn[0:1, 0, 0:1], 0.0).then_inc(added, 2)

            def normalise(t, u):
                norm.apply(dve, hn[:, u], t).then_inc(hn_ready, 1)

            def queries_keys(t, u):
                dve.wait_ge(q_ready, t + 1)
                dve.tensor_scalar(qt[:, u, 1], ps[0:DH, 4 * u + 1, 0:2 * P], cst[0:DH, C_ODD:C_ODD + 1], None, ALU.mult)\
                   .then_inc(kv_ready, 1)
                dve.wait_ge(qk_ps, 2 * t + 2)
                dve.tensor_copy(kt[:, u], ps[0:DH, 4 * u + 2, 0:2 * P]).then_inc(kv_ready, 1)

            def new_values(t, u):
                dve.wait_ge(v_ps, t + 1)
                dve.tensor_copy(v1[:, u, :, 0:HD], ps[:, 4 * u + 3, 0:D].rearrange("p (h d) -> p h d", h=NH))\
                   .then_inc(kv_ready, 1)

            def score(u, g):
                return ps[:, 4 * u + g].rearrange("p (k n) -> p k n", k=HK)

            def maxima(t, u):
                dve.wait_ge(score_ps, t + 1)
                for g in range(HG):
                    ins = dve.tensor_reduce(mx[:, u, g], score(u, g), AX.X, ALU.max)
                ins.then_inc(max_ready, 1)

            def shift(t, u):
                dve.wait_ge(max_ready, t + 1)
                for g in range(HG):
                    dve.tensor_tensor(p[:, u, g], score(u, g), mx[:, u, g].unsqueeze(2).to_broadcast([P, HK, P]),
                                      ALU.subtract).then_inc(shifted, 1)

            def probs(t, u):
                dve.wait_ge(pt_ps, 3 * t + 2)
                dve.tensor_copy(pt[:, u, 1], ps[:, 4 * u + 1]).then_inc(pt_dve, 1)

            def values(t, u):
                dve.wait_ge(av_ps, t + 1)
                o = ps[:, 4 * u + 3, 0:NH * (HD + 1)].rearrange("p (h d) -> p h d", h=NH)
                link.done(dve.reciprocal(rec[:, u], o[:, :, HD]))
                dve.tensor_tensor(av[:, u].rearrange("p (h d) -> p h d", h=NH), o[:, :, 0:HD],
                                  rec[:, u].unsqueeze(2).to_broadcast([P, NH, HD]), ALU.mult).then_inc(av_ready, 1)

            def add(t, u):
                dve.wait_ge(out_ps, t + 1)
                h = resid[0:T, bass.ds(t * D, D)]
                dve.tensor_tensor(h, h, ps[0:T, 4 * u + 3, 0:D], ALU.add).then_inc(added, 1)
                dve.wait_ge(added, t + 3)
                norm.add_rows(dve, t).then_inc(six_ready, 1)

            def turn(t, u, ahead=2):
                if ahead > 1:
                    normalise(t + 2, u)
                probs(t, u)
                if ahead > 0:
                    new_values(t + 1, 1 - u)
                    maxima(t + 1, 1 - u)
                values(t, u)
                if ahead > 0:
                    shift(t + 1, 1 - u)
                add(t, u)
                if ahead > 1:
                    queries_keys(t + 2, u)

            dve.wait_ge(added, 2)
            norm.statistics(dve)
            for u in range(U):
                normalise(u, u)
            dve.wait_ge(norm.rstd_ready, 2)
            for u in range(U):
                queries_keys(u, u)
            new_values(0, 0)
            maxima(0, 0)
            shift(0, 0)
            with dve.Fori(0, NB // U - 1) as it:
                link.loop(it, U)
                for u in range(U):
                    turn(it * U + u, u)
            link.end(NB // U - 1)
            for u in range(U):
                turn(NB - U + u, u, 1 - u)
            dve.wait_ge(six_ready, NB)


def expert_ffn(nc, gate_d, w1_d, b2_d, w2_d, bits_d, cst, cstb, resid, norm, out):
    with ExitStack() as ctx:
        def sb(name, shape, dt=F32):
            return ctx.enter_context(nc.sbuf_tensor("mo_" + name, shape, dt))

        take = ctx.enter_context(semaphores(nc))
        rows_x = nc.dram_tensor("rows_x", (NB * T + P, D + NX), F32, kind="Internal").ap()
        rows_y = nc.dram_tensor("rows_y", (NB * T + P, D), F32, kind="Internal").ap()
        w1 = sb("w1", [DH + 1, NX * 2 * HID])
        w2 = sb("w2", [P, NX * HC * D])
        b2 = sb("b2", [P, NX * D])
        score = sb("score", [P, NX, NB])
        row_of = sb("row_of", [P, NBLK1], I32)
        block_expert = sb("block_expert", [1, NBLK1], I32)
        weights_in, bits_in = take("weights_in"), take("bits_in")
        tables = take("tables")
        hn, by_token, zeros = sb("hn", [P, 8, D]), sb("by_token", [P, NB, NX]), sb("zeros", [P, D + NX])
        hn_stored = [take(f"hn_stored{u}") for u in range(8)]
        bits = sb("bits", [P, STEPS, 3], I32)
        gate_scores(nc, hn, by_token, zeros, tables, hn_stored, gate_d, bits, bits_d, bits_in, ((w1, w1_d), (w2, w2_d), (b2, b2_d)), weights_in, cst, resid, norm, score,
                    rows_x, rows_y)
        pick_pairs(nc, bits, bits_in, cst, cstb, score, row_of, block_expert)
        run_experts(nc, tables, hn_stored, cst, w1, w2, b2, weights_in, row_of, block_expert, rows_x, rows_y, out)


def gate_scores(nc, hn, by_token, zeros, tables, hn_stored, gate_d, bits, bits_d, bits_in, weights, weights_in,
                cst, resid, norm, score, rows_x, rows_y):
    U = len(hn_stored)
    with ExitStack() as ctx:
        take = ctx.enter_context(semaphores(nc))

        def sb(name, shape, dt=F32):
            return ctx.enter_context(nc.sbuf_tensor("ga_" + name, shape, dt))

        gate = sb("gate", [DH, 2, NX])
        hnt = sb("hnt", [DH, 4, 2, P])
        logit = sb("logit", [P, NX, NB])
        mx, z, rz = sb("mx", [P, NB]), sb("z", [P, NB]), sb("rz", [P, NB])
        pa = ctx.enter_context(nc.psum_tensor("ga_pa", [P, 4, 512], F32))
        logit_ps = ctx.enter_context(nc.psum_tensor("ga_logit_ps", [P, 512], F32))
        w_in, hn_ready, hnt_ps, hnt_ready = take("ga_w_in"), take("ga_hn_ready"), take("ga_hnt_ps"), take("ga_hnt_ready")
        logit_done, chain, shifted, exp_ready = take("ga_logit_done"), take("ga_chain"), take("ga_shifted"), take("ga_exp")
        score_ready, cleared = take("ga_score_ready"), take("ga_cleared")
        norm.begin(take, "ga")
        block = ctx.enter_context(nc.Block())

        @block.gpsimd
        def _(pool):
            norm.deviations(pool)

        @block.sync
        def _(sp):
            sp.dma_start(gate[:], gate_d).then_inc(w_in, 16)
            sp.dma_start(bits[:], bits_d).then_inc(bits_in, 16)
            sp.dma_start(rows_y[0:NB * T].rearrange("(b t) d -> t b d", t=T),
                         resid[0:T, :].rearrange("t (b d) -> t b d", b=NB)).then_inc(tables, 16)
            sp.wait_ge(cleared, 1)
            sp.dma_start(rows_y[NB * T:NB * T + P], zeros[:, 0:D]).then_inc(tables, 16)
            sp.dma_start(rows_x[NB * T:NB * T + P], zeros[:]).then_inc(tables, 16)
            with sp.Fori(0, NB // U) as it:
                for u in range(U):
                    sp.wait_ge(hn_ready, it * U + u + 1)
                    sp.dma_start(rows_x[bass.ds((it * U + u) * T, T), 0:D], hn[0:T, u]).then_inc(hn_stored[u], 16)
            sp.wait_ge(score_ready, 1)
            sp.dma_start(rows_x[0:NB * T, D:D + NX].rearrange("(b t) e -> t b e", t=T), by_token[0:T])\
              .then_inc(tables, 16)
            for dst, src in weights:
                sp.dma_start(dst[:], src).then_inc(weights_in, 16)

        @block.tensor
        def _(pe):
            ident = cst[:, C_ID:C_ID + P]
            pe.wait_ge(w_in, 16)

            def turn_over(t, u):
                pe.wait_ge(hn_ready, t + 1)
                for c in range(2):
                    mm = pe.transpose(pa[0:DH, u % 4, c * P:(c + 1) * P], hn[:, u, c * DH:(c + 1) * DH], ident)
                mm.then_inc(hnt_ps, 1)

            def gates(t, u):
                pe.wait_ge(hnt_ready, t + 1)
                for c in range(2):
                    mm = pe.matmul(logit_ps[:, bass.ds(t * NX, NX)], hnt[:, u % 4, c], gate[:, c], start=c == 0, stop=c == 1)
                mm.then_inc(logit_done, 1)

            AHEAD = 3
            for u in range(AHEAD):
                turn_over(u, u)
            with pe.Fori(0, NB // U - 1) as it:
                for u in range(U):
                    turn_over(it * U + u + AHEAD, (u + AHEAD) % U)
                    gates(it * U + u, u)
            for u in range(U):
                t = NB - U + u
                if t + AHEAD < NB:
                    turn_over(t + AHEAD, (u + AHEAD) % U)
                gates(t, u)

        @block.scalar
        def _(act):
            with act.Fori(0, NB // U) as it:
                for u in range(U):
                    act.wait_ge(hnt_ps, it * U + u + 1)
                    act.copy(hnt[:, u % 4], pa[0:DH, u % 4, 0:2 * P].rearrange("p (c t) -> p c t", c=2)).then_inc(hnt_ready, 1)
            act.wait_ge(shifted, 1)
            act.activation(logit[:], logit[:], ACT.Exp).then_inc(exp_ready, 1)

        @block.vector
        def _(dve):
            link = Link(dve, chain)
            norm.statistics(dve)
            dve.memset(zeros[:], 0.0).then_inc(cleared, 1)
            for u in range(U):
                dve.memset(hn[:, u], 0.0).then_inc(hn_stored[u], 16)

            def normalise(it, u, first=False):
                dve.wait_ge(hn_stored[u], 16 * it + 16)
                if not first:
                    dve.wait_ge(hnt_ps, (it - 1) * U + u + 1)
                norm.apply(dve, hn[:, u], it * U + u).then_inc(hn_ready, 1)

            for u in range(U):
                if u == 4:
                    dve.wait_ge(norm.rstd_ready, 2)
                normalise(0, u, first=True)
            with dve.Fori(1, NB // U) as it:
                for u in range(U):
                    normalise(it, u)
            dve.wait_ge(logit_done, NB)
            link.done(dve.tensor_copy(logit[:], logit_ps[:, 0:NB * NX].rearrange("p (b e) -> p e b", e=NX)))
            by_e = "p e b -> p b e"
            link.done(dve.tensor_reduce(mx[:], logit[:].rearrange(by_e), AX.X, ALU.max))
            dve.tensor_tensor(logit[:], logit[:], mx[:].unsqueeze(1).to_broadcast([P, NX, NB]), ALU.subtract)\
               .then_inc(shifted, 1)
            dve.wait_ge(exp_ready, 1)
            link.done(dve.tensor_reduce(z[:], logit[:].rearrange(by_e), AX.X, ALU.add))
            link.done(dve.reciprocal(rz[:], z[:]))
            link.done(dve.tensor_tensor(score[:], logit[:], rz[:].unsqueeze(1).to_broadcast([P, NX, NB]), ALU.mult))
            dve.tensor_copy(by_token[:], score[:].rearrange(by_e)).then_inc(score_ready, 1)
            dve.wait_ge(score_ready, 1)
            link.done(dve.tensor_scalar(score[:], score[:], cst[:, C_VALID:C_VALID + 1], cst[:, C_VM1:C_VM1 + 1],
                                        ALU.mult, ALU.add))


def pick_pairs(nc, bits, bits_in, cst, cstb, score, row_of, block_expert):
    NC = NX * NB
    W = 8
    LO = 32
    with ExitStack() as ctx:
        take = ctx.enter_context(semaphores(nc))

        def sb(name, shape, dt=F32):
            return ctx.enter_context(nc.sbuf_tensor("pk_" + name, shape, dt))

        found, cand = sb("found", [P, 1], I32), sb("cand", [P, 3], I32)
        hits, cnt, enough = sb("hits", [P, 3, NC]), sb("cnt", [P, 3]), sb("enough", [P, 3])
        reached = sb("reached", [P, 4])
        above, tie = sb("above", [P, NC]), sb("tie", [P, NC])
        mask_b = sb("mask_b", [P, 2, NC], BF16)
        ones = sb("ones", [P, NC])
        incl, rank, left, kept = sb("incl", [P, NC]), sb("rank", [P, NC]), sb("left", [P, 1]), sb("kept", [P, NC])
        cntx, inclx, startx = sb("cntx", [P, NX]), sb("inclx", [P, NX]), sb("startx", [P, NX])
        ceil_i, blk_i, blk = sb("ceil_i", [P, NX], I32), sb("blk_i", [P, NX], I32), sb("blk", [P, NX])
        iblk, shift = sb("iblk", [P, NX]), sb("shift", [P, NX])
        slot, slot_i, q_i, p_i = sb("slot", [P, NC]), sb("slot_i", [P, NC], I32), sb("q_i", [P, NC], I32), sb("p_i", [P, NC], I32)
        qf, pf = sb("qf", [P, NC], BF16), sb("pf", [P, NC], BF16)
        row1 = sb("row1", [P, NC])
        past, nblk = sb("past", [1, NBLK1, NX]), sb("nblk", [1, NBLK1])
        high_i, high, low = sb("high_i", [P, NC], I32), sb("high", [P, NC], BF16), sb("low", [P, NC], BF16)
        row_i, low_i = sb("row_i", [P, NC], I32), sb("low_i", [P, NC], I32)
        iota_b = sb("iota_b", [P, P], BF16)
        hot_p, hot_q = sb("hot_p", [P, 2, W, P], BF16), sb("hot_q", [P, 2, W, NBLK1], BF16)
        hot_v = sb("hot_v", [P, 2, W, 2, NBLK1], BF16)
        listed, empty = sb("listed", [P, NBLK1]), sb("empty", [P, NBLK1])
        ps = ctx.enter_context(nc.psum_tensor("pk_ps", [P, 4, 512], F32))
        chain, counted, total_ps = take("pk_chain"), take("pk_counted"), take("pk_total_ps")
        mask_ready, prefix_ps, hot_ready, used = take("pk_mask_ready"), take("pk_prefix_ps"), take("pk_hot"), take("pk_used")
        q_ready = take("pk_q_ready")
        block = ctx.enter_context(nc.Block())
        dummy = cst[:, C_DUMMY:C_DUMMY + 1]

        @block.tensor
        def _(pe):
            with pe.Fori(0, STEPS) as i:
                pe.wait_ge(counted, 3 * i + 3)
                pe.matmul(ps[:, 0, 0:3], cst[:, C_ONE:C_ONE + P], cnt[:], start=True, stop=True).then_inc(total_ps, 1)
            pe.wait_ge(counted, 3 * STEPS + 1)
            pe.matmul(ps[:, 0, 0:1], cst[:, C_ONE:C_ONE + P], cnt[:, 0:1], start=True, stop=True).then_inc(total_ps, 1)
            for n in range(2):
                pe.wait_ge(mask_ready, n + 1)
                pe.matmul(ps[:, 1, 0:NC], cstb[:, 1], mask_b[:, n], start=True, stop=True)
                pe.matmul(ps[:, 2, 0:NC], cstb[:, 3], mask_b[:, n], start=True, stop=True).then_inc(prefix_ps, 1)

            def columns(it, h, first=False, last=False):
                pe.wait_ge(hot_ready, 3 * (it * 2 + h) + 3)
                for w in range(W):
                    mm = pe.matmul(ps[:, 3, 0:2 * NBLK1], hot_p[:, h, w], hot_v[:, h, w].rearrange("p v n -> p (v n)"),
                                   start=first and w == 0, stop=last and w == W - 1)
                mm.then_inc(used, 1)

            TURNS = NC // (2 * W)
            columns(0, 0, first=True)
            columns(0, 1)
            with pe.Fori(1, TURNS - 1) as it:
                columns(it, 0)
                columns(it, 1)
            columns(TURNS - 1, 0)
            columns(TURNS - 1, 1, last=True)

        @block.vector
        def _(dve):
            link = Link(dve, chain)
            s = score[:].rearrange("p e b -> p (e b)")
            by_e = "p (e b) -> p e b"
            dve.memset(ones[:], 1.0)
            link.done(dve.memset(found[:], 0))
            link.done(dve.memset(reached[:], 0.0))
            dve.wait_ge(bits_in, 16)
            with dve.Fori(0, STEPS // 5) as turn:
                link.loop(turn, 5 * 5)
                for n in range(5):
                    i = turn * 5 + n
                    link.done(dve.tensor_tensor(cand[:], found[:].to_broadcast([P, 3]),
                                                bits[:, bass.ds(i, 1), :].rearrange("p a n -> p (a n)"), ALU.bitwise_or))
                    for c in range(3):
                        dve.tensor_scalar(hits[:, c], s, cand[:, c:c + 1].bitcast(F32), None, ALU.is_ge, ALU.add,
                                          accum_out=cnt[:, c:c + 1]).then_inc(counted, 1)
                    dve.wait_ge(total_ps, i + 1)
                    link.done(dve.tensor_scalar(enough[:], ps[:, 0, 0:3], float(K1), None, ALU.is_ge))
                    link.done(dve.tensor_tensor(reached[:, 0:3], cand[:].bitcast(F32), enough[:], ALU.mult))
                    link.done(dve.tensor_reduce(found[:].bitcast(F32), reached[:], AX.X, ALU.max))
                    link.done(dve.tensor_copy(reached[:, 3:4], found[:].bitcast(F32)))
            link.end(STEPS // 5)
            kth = found[:].bitcast(F32)
            dve.tensor_scalar(above[:], s, kth, None, ALU.is_gt, ALU.add, accum_out=cnt[:, 0:1]).then_inc(counted, 1)
            link.done(dve.tensor_scalar(tie[:], s, kth, None, ALU.is_equal))
            dve.tensor_copy(mask_b[:, 0], tie[:]).then_inc(mask_ready, 1)
            dve.wait_ge(total_ps, STEPS + 1)
            link.done(dve.tensor_scalar(left[:], ps[:, 0, 0:1], -1.0, float(K1), ALU.mult, ALU.add))

            def prefix(n):
                dve.wait_ge(prefix_ps, n + 1)
                link.done(dve.tensor_tensor_scan(incl[:], ones[:], ps[:, 1, 0:NC], 0.0, ALU.mult, ALU.add))
                link.done(dve.tensor_tensor(rank[:], incl[:], ps[:, 1, 0:NC], ALU.subtract))
                link.done(dve.tensor_tensor(rank[:], rank[:], ps[:, 2, 0:NC], ALU.add))

            prefix(0)
            link.done(dve.scalar_tensor_tensor(kept[:], rank[:], left[:], tie[:], ALU.is_lt, ALU.mult))
            link.done(dve.tensor_tensor(kept[:], kept[:], above[:], ALU.add))
            dve.tensor_copy(mask_b[:, 1], kept[:]).then_inc(mask_ready, 1)
            prefix(1)
            link.done(dve.tensor_reduce(cntx[:], ps[:, 1, 0:NC].rearrange(by_e, e=NX), AX.X, ALU.add))
            link.done(dve.tensor_tensor_scan(inclx[:], ones[:, 0:NX], cntx[:], 0.0, ALU.mult, ALU.add))
            link.done(dve.tensor_tensor(startx[:], inclx[:], cntx[:], ALU.subtract))
            link.done(dve.tensor_scalar(ceil_i[:], cntx[:], P - 1.0, None, ALU.add))
            link.done(dve.tensor_scalar(blk_i[:], ceil_i[:], 7, None, ALU.arith_shift_right))
            link.done(dve.tensor_copy(blk[:], blk_i[:]))
            link.done(dve.tensor_tensor_scan(iblk[:], ones[:, 0:NX], blk[:], 0.0, ALU.mult, ALU.add))
            link.done(dve.tensor_tensor(shift[:], iblk[:], blk[:], ALU.subtract))
            link.done(dve.scalar_tensor_tensor(shift[:], shift[:], float(P), startx[:], ALU.mult, ALU.subtract))
            link.done(dve.tensor_tensor(slot[:].rearrange(by_e, e=NX), rank[:].rearrange(by_e, e=NX),
                                        shift[:].unsqueeze(2).to_broadcast([P, NX, NB]), ALU.add))
            link.done(dve.scalar_tensor_tensor(slot[:], slot[:], 1.0, kept[:], ALU.add, ALU.mult))
            link.done(dve.tensor_scalar(slot_i[:], slot[:], -1.0, None, ALU.add))
            link.done(dve.tensor_scalar(q_i[:], slot_i[:], 7, None, ALU.arith_shift_right))
            link.done(dve.tensor_scalar(p_i[:], slot_i[:], P - 1, None, ALU.bitwise_and))
            link.done(dve.tensor_copy(qf[:], q_i[:]))
            link.done(dve.tensor_copy(pf[:], p_i[:]))
            link.done(dve.tensor_scalar(row1[:].rearrange(by_e, e=NX),
                                        cst[:, C_IOTA:C_IOTA + NB].unsqueeze(1).to_broadcast([P, NX, NB]),
                                        float(T), cst[:, C_ROW1:C_ROW1 + 1], ALU.mult, ALU.add))
            link.done(dve.tensor_copy(row_i[:], row1[:]))
            link.done(dve.tensor_scalar(high_i[:], row_i[:], 5, None, ALU.arith_shift_right))
            link.done(dve.tensor_scalar(low_i[:], row_i[:], LO - 1, None, ALU.bitwise_and))
            link.done(dve.tensor_copy(high[:], high_i[:]))
            link.done(dve.tensor_copy(low[:], low_i[:]))
            link.done(dve.tensor_copy(iota_b[:], cst[:, C_IOTA:C_IOTA + P]))
            link.done(dve.tensor_tensor(past[:], cst[0:1, C_IOTA:C_IOTA + NBLK1].unsqueeze(2).to_broadcast([1, NBLK1, NX]),
                                        iblk[0:1, :].unsqueeze(1).to_broadcast([1, NBLK1, NX]), ALU.is_ge))
            link.done(dve.tensor_reduce(nblk[:], past[:], AX.X, ALU.add))
            link.done(dve.tensor_scalar(block_expert[:], nblk[:], NX - 1.0, None, ALU.min))

            def columns(it, h, first=False):
                turn = it * 2 + h
                at = bass.ds(turn * W, W)
                if not first:
                    dve.wait_ge(used, turn - 1)
                dve.tensor_tensor(hot_q[:, h], iota_b[:, 0:NBLK1].unsqueeze(1).to_broadcast([P, W, NBLK1]),
                                  qf[:, at].unsqueeze(2).to_broadcast([P, W, NBLK1]), ALU.is_equal).then_inc(q_ready, 1)
                dve.tensor_tensor(hot_p[:, h], iota_b[:].unsqueeze(1).to_broadcast([P, W, P]),
                                  pf[:, at].unsqueeze(2).to_broadcast([P, W, P]), ALU.is_equal).then_inc(hot_ready, 1)
                dve.wait_ge(q_ready, turn + 1)
                for v, x in enumerate((high, low)):
                    dve.tensor_tensor(hot_v[:, h, :, v], hot_q[:, h], x[:, at].unsqueeze(2).to_broadcast([P, W, NBLK1]),
                                      ALU.mult).then_inc(hot_ready, 1)

            columns(0, 0, first=True)
            columns(0, 1, first=True)
            columns(1, 0)
            columns(1, 1)
            with dve.Fori(1, NC // (4 * W)) as it:
                for n in range(4):
                    columns(it * 2 + n // 2, n % 2)
            dve.wait_ge(used, NC // W)
            link.done(dve.tensor_copy(listed[:], ps[:, 3, NBLK1:2 * NBLK1]))
            link.done(dve.scalar_tensor_tensor(listed[:], ps[:, 3, 0:NBLK1], float(LO), listed[:], ALU.mult, ALU.add))
            link.done(dve.tensor_scalar(empty[:], listed[:], 0.0, dummy, ALU.is_equal, ALU.mult))
            link.done(dve.scalar_tensor_tensor(row_of[:], listed[:], -1.0, empty[:], ALU.add, ALU.add))


def run_experts(nc, tables, hn_stored, cst, w1, w2, b2, weights_in, row_of, block_expert, rows_x, rows_y, out):
    W = 4
    TURNS = NBLK1 // W
    HH = HID // 2
    with ExitStack() as ctx:
        take = ctx.enter_context(semaphores(nc))

        def sb(name, shape, dt=F32):
            return ctx.enter_context(nc.sbuf_tensor("ex_" + name, shape, dt))

        x = sb("x", [P, W, D + NX])
        xt = sb("xt", [DH + 1, 2, 2, P])
        w1_of = sb("w1_of", [DH + 1, 2, 2 * HID])
        ht = sb("ht", [P, 2, HID])
        yb = sb("yb", [P, W, D])
        y = sb("y", [P, W, D])
        xt_ps = ctx.enter_context(nc.psum_tensor("ex_xt_ps", [P, 2, 512], F32))
        h_ps = ctx.enter_context(nc.psum_tensor("ex_h_ps", [P, 4, 512], F32))
        y_ps = ctx.enter_context(nc.psum_tensor("ex_y_ps", [P, 1, 512], F32))
        x_t, xt_ready, h_done, gelu_ready = take("ex_x_t"), take("ex_xt_ready"), take("ex_h_done"), take("ex_gelu")
        w1_ready, y_done = take("ex_w1_ready"), take("ex_y_done")
        y_read, y_ready, ones_ready, stored = take("ex_y_read"), take("ex_y_ready"), take("ex_ones"), take("ex_stored")
        gathered = [take(f"ex_gathered{u}") for u in range(W)]
        added = [take(f"ex_added{u}") for u in range(W)]
        block = ctx.enter_context(nc.Block())

        @block.gpsimd
        def _(pool):
            last = pool.to_reg(NB * T + P - 1)
            pool.wait_ge(tables, 4 * 16)
            for stored_u in hn_stored:
                pool.wait_ge(stored_u, 16 * (NB // len(hn_stored) + 1))

            def gather(t):
                if t >= W:
                    pool.wait_ge(y_ready, t - W + 1)
                pool.indirect_dma_start(x[:, t % W], None, rows_x, bass.IndirectOffsetOnAxis(row_of[:, t:t + 1], 0),
                                        bounds_check=last, oob_is_err=True).then_inc(gathered[t % W], 16)

            for t in range(W - 1):
                gather(t)
            for t in range(NBLK1):
                if t + W - 1 < NBLK1:
                    gather(t + W - 1)
                pool.wait_ge(y_ready, t + 1)
                if t:
                    pool.wait_ge(added[(t - 1) % W], 16 * ((t - 1) // W + 1))
                pool.indirect_dma_start(rows_y, bass.IndirectOffsetOnAxis(row_of[:, t:t + 1], 0), y[:, t % W], None,
                                        bounds_check=last, oob_is_err=True, compute_op=ALU.add)\
                    .then_inc(added[t % W], 16)
            for u in range(W):
                pool.wait_ge(added[u], 16 * TURNS)
            pool.dma_start(out.rearrange("b t d -> (b t d)").rearrange("(p n) -> p n", p=P),
                           rows_y[0:NB * T].rearrange("r d -> (r d)").rearrange("(p n) -> p n", p=P)).then_inc(stored, 16)
            pool.wait_ge(stored, 16)

        @block.tensor
        def _(pe):
            ident = cst[:, C_ID:C_ID + P]
            pe.wait_ge(weights_in, 3 * 16)
            pe.wait_ge(ones_ready, 1)

            def experts(it, n):
                return load_experts(nc, mybir.EngineType.PE, block_expert[0:1, bass.ds(it * W, n)], NX - 1)

            def turn_over(it, u):
                pe.wait_ge(gathered[u], 16 * it + 16)
                for c in range(2):
                    mm = pe.transpose(xt_ps[0:DH, u % 2, c * P:(c + 1) * P], x[:, u, c * DH:(c + 1) * DH], ident)
                mm.then_inc(x_t, 1)

            def hidden(it, u):
                t = it * W + u
                pe.wait_ge(xt_ready, t + 1)
                pe.wait_ge(w1_ready, t + 1)
                for n in range(2):
                    for m in range(HC // 2):
                        at = n * HH + m * P
                        for c in range(2):
                            k = DH + c
                            mm = pe.matmul(h_ps[:, 2 * (u % 2) + n, m * P:(m + 1) * P],
                                           w1_of[0:k, u % 2, c * HID + at:c * HID + at + P], xt[0:k, u % 2, c],
                                           start=c == 0, stop=c == 1)
                    mm.then_inc(h_done, 1)

            def output(it, u, e):
                t = it * W + u
                pe.wait_ge(y_read, t + 1)
                for k in range(HC):
                    if k % (HC // 2) == 0:
                        pe.wait_ge(gelu_ready, 2 * t + k // (HC // 2) + 1)
                    mm = pe.matmul(y_ps[:, 0, 0:D], ht[:, u % 2, k * P:(k + 1) * P],
                                   w2[:, bass.ds(e * (HC * D) + k * D, D)], start=k == 0, stop=k == HC - 1)
                mm.then_inc(y_done, 1)

            def turn(it, u, e, left=2):
                if left > 1:
                    turn_over(it + (u + 2) // W, (u + 2) % W)
                if left > 0:
                    hidden(it + (u + 1) // W, (u + 1) % W)
                output(it, u, e)

            turn_over(0, 0)
            turn_over(0, 1)
            hidden(0, 0)
            with pe.Fori(0, TURNS - 1) as it:
                es = experts(it, W)
                for u in range(W):
                    turn(it, u, es[u])
            es = experts(TURNS - 1, W)
            for u in range(W):
                turn(TURNS - 1, u, es[u], W - 1 - u)

        @block.scalar
        def _(act):
            def turn_over(it, u):
                act.wait_ge(x_t, it * W + u + 1)
                act.copy(xt[0:DH, u % 2], xt_ps[0:DH, u % 2, 0:2 * P].rearrange("p (c t) -> p c t", c=2)).then_inc(xt_ready, 1)

            def hidden(it, u):
                for n in range(2):
                    act.wait_ge(h_done, 2 * (it * W + u) + n + 1)
                    act.activation(ht[:, u % 2, n * HH:(n + 1) * HH], h_ps[:, 2 * (u % 2) + n, 0:HH],
                                   ACT.Gelu_apprx_tanh).then_inc(gelu_ready, 1)

            def turn(it, u, left=2):
                if left > 1:
                    turn_over(it + (u + 2) // W, (u + 2) % W)
                if left > 0:
                    hidden(it + (u + 1) // W, (u + 1) % W)

            act.wait_ge(ones_ready, 1)
            turn_over(0, 0)
            turn_over(0, 1)
            hidden(0, 0)
            with act.Fori(0, TURNS - 1) as it:
                for u in range(W):
                    turn(it, u)
            for u in range(W):
                turn(TURNS - 1, u, W - 1 - u)

        @block.vector
        def _(dve):
            dve.memset(xt[DH:DH + 1], 1.0).then_inc(ones_ready, 1)
            dve.memset(yb[0:1, 0, 0:1], 0.0).then_inc(y_read, 1)
            dve.wait_ge(weights_in, 3 * 16)

            def experts(it):
                return load_experts(nc, mybir.EngineType.DVE, block_expert[0:1, bass.ds(it * W, W)], NX - 1)

            def copy_w1(t, u, e):
                dve.tensor_copy(w1_of[:, u % 2], w1[:, bass.ds(e * (2 * HID), 2 * HID)]).then_inc(w1_ready, 1)

            def turn(it, first=False, last=False):
                es = list(experts(it)) + ([] if last else list(experts(it + 1)))
                for u in range(W):
                    t, e = it * W + u, es[u]
                    if u + 2 < len(es):
                        dve.wait_ge(h_done, 2 * t + 2)
                        copy_w1(t + 2, u, es[u + 2])
                    dve.wait_ge(y_done, t + 1)
                    dve.tensor_tensor(yb[:, u], y_ps[:, 0, 0:D], b2[:, bass.ds(e * D, D)], ALU.add).then_inc(y_read, 1)
                    dve.wait_ge(y_read, t + 2)
                    if not first:
                        dve.wait_ge(added[u], 16 * it)
                    dve.tensor_scalar(y[:, u], yb[:, u], x[:, u, bass.ds(e + D, 1)], None, ALU.mult)\
                       .then_inc(y_ready, 1)

            es = experts(0)
            for u in range(2):
                copy_w1(u, u, es[u])
            turn(0, first=True)
            with dve.Fori(1, TURNS - 1) as it:
                turn(it)
            turn(TURNS - 1, last=True)


def _consts():
    c = np.zeros((P, C_END), np.float32)
    i = np.arange(P)
    c[:, C_ID:C_ID + P] = np.eye(P)
    c[:, C_ONE:C_ONE + P] = 1
    c[:, C_TRS:C_TRS + P] = i[:, None] < i[None, :]
    c[:, C_TRI:C_TRI + P] = i[:, None] <= i[None, :]
    c[:, C_IOTA:C_IOTA + 256] = np.arange(256)
    c[:, C_CAUS:C_CAUS + P] = np.where(i[None, :] > i[:, None], NEG, 0)
    c[:DH, C_BLKM:C_BLKM + DH] = np.where(i[:DH, None] // 24 == i[None, :DH] // 24, 0, NEG)
    m = np.zeros((2, 16, 2, 16))
    m += 1
    m.reshape(32, 32)[8:24, 8:24] = 2
    for a in range(2):
        for b in range(2):
            for ch in range(NCH):
                y = 8 * (ch % 2)
                c[:, C_MULT + (2 * a + b) * NCH + ch] = m[a, y:y + 8, b].reshape(P)
    c[:, C_EPS] = LN_EPS
    c[:, C_VALID] = i < T
    c[:, C_FAR] = np.where(i < T, 0, FAR)
    c[:, C_SENT:C_SENT + 4] = [-1, -2, -3, -4]
    c[:, C_NHALF] = -0.5
    c[:, C_VM1] = c[:, C_VALID] - 1
    c[:, C_DUMMY] = NB * T + i + 1
    c[:, C_ROW1] = i + 1
    c[:, C_EVEN], c[:, C_ODD] = i // 16 % 2 == 0, i // 16 % 2 == 1
    return c


def _blocks(w):
    w = w.reshape(2, 2, 8, 2, 16, 3, -1)
    return np.ascontiguousarray(w.transpose(2, 4, 0, 3, 5, 1, 6).reshape(P, NK, -1))


def _windows(w):
    w = w.reshape(16, 16, 5, 3, -1)
    shifted = np.zeros((2, 16, 2, 16, 3, w.shape[-1]), w.dtype)
    for part, (a, b) in ((1, (0, 0)), (2, (1, 1)), (3, (0, 1)), (4, (1, 0))):
        shifted[a, :, b] = w[:, :, part]
    base = np.zeros((32, 32, 3, w.shape[-1]), w.dtype)
    base[8:24, 8:24] = w[:, :, 0]
    return _blocks(shifted), _blocks(base)


def kernel(**inputs):
    import concourse.bacc as bacc
    from concourse.bass_utils import run_bass_kernel_spmd as run

    a = {k: np.asarray(v) for k, v in inputs.items()}
    x = np.zeros((NGRP * GRP, 3, 112, 112), np.float32)
    x[:NB, :, 8:104, 8:104] = a["x"]
    x = x.reshape(NGRP, GRP, 3, BLK, 2, 8, BLK, 16).transpose(0, 5, 7, 2, 4, 1, 3, 6)
    feed = {"x_blocks": x.reshape(NGRP, P, NCH * GRP, BLK * BLK), "txt": a["txt"], "consts": _consts()}
    feed["w_shift"], feed["w_base"] = _windows(a["L0_tok_W"].T)
    for name, key in (("g", "L0_tok_ln_gamma"), ("b", "L0_tok_ln_beta")):
        s, b = _windows(a[key][:, None])
        feed[name + "_shift"], feed[name + "_base"] = s[:, :, 0], b[:, :, 0]
    feed["tok_b"] = a["L0_tok_b"][None]
    half = lambda w: w.reshape(2, DH, -1).transpose(1, 0, 2)
    w = a["L0_attn_W_qkv"]
    feed["wqk"] = half(np.concatenate([w[:, 0::3], w[:, 1::3]], 1))
    feed["wv"] = half(w[:, 2::3])
    feed["wp"] = half(a["L0_attn_W_proj"])
    feed["bp"] = np.broadcast_to(a["L0_attn_b_proj"], (4, D))
    feed["temp"] = np.broadcast_to(a["L0_attn_temp"].reshape(2, 4, 1), (2, 4, 24)).reshape(2, DH).T
    feed["emb"] = np.stack([a["L0_ffn_emb_fk"], a["L0_ffn_emb_rk"]], 1)
    feed["wcat"] = half(np.concatenate([a["L0_ffn_W_fk"], a["L0_ffn_W_rk"]], 1))
    feed["bcat"] = np.concatenate([a["L0_ffn_b_fk"], a["L0_ffn_b_rk"]])[:, None]
    feed["f_know"], feed["r_know"] = a["L0_ffn_f_know"], a["L0_ffn_r_know"]
    feed["wq1"], feed["wk1"], feed["wv1"] = (half(a["L1_attn_w_" + x]) for x in ("query", "key", "value"))
    with_bias = lambda w, b: np.concatenate([half(w), np.stack([np.zeros_like(b), b])[None]])
    feed["wo1"] = with_bias(a["L1_attn_w_out"], a["L1_attn_b_out"])
    feed["gate_w"] = half(a["L1_ffn_gate_weight"].T)
    w1 = np.zeros((DH + 1, NX, 2, HID), np.float32)
    w1[:DH] = a["L1_ffn_w1"].reshape(NX, 2, DH, HID).transpose(2, 0, 1, 3)
    w1[DH, :, 1] = a["L1_ffn_b1"]
    feed["w1"] = w1.reshape(DH + 1, -1)
    feed["w2"] = a["L1_ffn_w2"].reshape(NX, HC, P, D).transpose(2, 0, 1, 3).reshape(P, -1)
    feed["b2"] = np.broadcast_to(a["L1_ffn_b2"].reshape(1, -1), (P, NX * D))
    feed["bits"] = np.broadcast_to((np.int32([1, 2, 3]) << np.int32(2 * np.arange(14, -1, -1))[:, None]), (P, 15, 3))
    nc = bacc.Bacc("TRN2", target_bir_lowering=False, num_devices=1)
    feed = {k: np.ascontiguousarray(v) for k, v in feed.items()}
    aps = {k: nc.dram_tensor("in_" + k, v.shape, mybir.dt.from_np(v.dtype), kind="ExternalInput").ap()
           for k, v in feed.items()}
    out = nc.dram_tensor("out", (NB, T, D), F32, kind="ExternalOutput").ap()
    program(nc, **aps, out=out)
    r = run(nc, [{"in_" + k: v for k, v in feed.items()}], core_ids=[0])
    return r.results[0]["out"]
```
